# Optimizing a Trainium2 kernel written in Bass

```python
import numpy as np
import jax
import jax.numpy as jnp

def _softmax(x, axis=-1):
    return jax.nn.softmax(x, axis=axis)

def _gelu(x):
    return jax.nn.gelu(x, approximate=True)

def _silu(x):
    return jax.nn.silu(x)

def _sigmoid(x):
    return jax.nn.sigmoid(x)

def _layernorm(x, axis=-1, eps=1e-05):
    m = jnp.mean(x, axis=axis, keepdims=True)
    v = jnp.var(x, axis=axis, keepdims=True)
    return (x - m) / jnp.sqrt(v + eps)

def _scatter_add(tgt, idx, src, axis=0):
    return tgt.at[idx].add(src)

def _segment_sum(src, seg, n):
    return jax.ops.segment_sum(src, seg, n)
kernel_name = 'mk_gnn_preln_d2_gnn_r32_413f5f'

def setup_inputs(seed: int=0):
    np.random.seed(seed)
    _w = jnp.asarray

    def _rec_inputs():
        import jax
        import jax.numpy as jnp
        _gk = jax.random.key(seed)
        x = -0.0005121 + 1.001 * jax.random.normal(jax.random.fold_in(_gk, 1), (3125, 64), jnp.float32)
        _s = jax.random.randint(jax.random.fold_in(_gk, 2), (50000,), 0, 3125, jnp.int32)
        _d = jax.random.randint(jax.random.fold_in(_gk, 3), (50000,), 0, 3125, jnp.int32)
        _loop = jnp.arange(3125, dtype=jnp.int32)
        src = jnp.concatenate([_s, _d, _loop])
        dst = jnp.concatenate([_d, _s, _loop])
        _o = jnp.argsort(dst, stable=True)
        src = src[_o]
        dst = dst[_o]
        edge_attr_8 = -4.12889e-05 + 1 * jax.random.normal(jax.random.fold_in(_gk, 12), (103125, 8), jnp.float32)
        edge_type_65 = jax.random.randint(jax.random.fold_in(_gk, 14), (103125,), 0, 65, jnp.int32)
        return (x, src, dst, edge_attr_8, edge_type_65)
    x, src, dst, edge_attr_8, edge_type_65 = _rec_inputs()

    def _L0_gnn_setup():
        import jax, jax.numpy as jnp
        import numpy as np
        N_NODES = 50000
        N_EDGES = 25000
        D = 64
        N_BASIS = 8
        key = jax.random.key(seed)
        ks = jax.random.split(key, 16)
        inp = {'p': jax.random.normal(ks[0], (N_NODES, D), dtype=jnp.float32), 'idx_i': jax.random.randint(ks[1], (N_EDGES,), 0, N_NODES), 'idx_j': jax.random.randint(ks[2], (N_EDGES,), 0, N_NODES), 'basis': jax.random.normal(ks[3], (N_EDGES, N_BASIS), dtype=jnp.float32), 'pp_W1': jax.random.normal(ks[4], (D, D), dtype=jnp.float32) / np.sqrt(D), 'pp_b1': jnp.zeros((D,), dtype=jnp.float32), 'pp_W2': jax.random.normal(ks[5], (D, D), dtype=jnp.float32) / np.sqrt(D), 'pp_b2': jnp.zeros((D,), dtype=jnp.float32), 'pi_W1': jax.random.normal(ks[6], (2 * D, D), dtype=jnp.float32) / np.sqrt(2 * D), 'pi_b1': jnp.zeros((D,), dtype=jnp.float32), 'pi_W2': jax.random.normal(ks[7], (D, D), dtype=jnp.float32) / np.sqrt(D), 'pi_b2': jnp.zeros((D,), dtype=jnp.float32), 'pi_W3': jax.random.normal(ks[8], (D, D * N_BASIS), dtype=jnp.float32) / np.sqrt(D), 'ii_W1': jax.random.normal(ks[9], (D, D), dtype=jnp.float32) / np.sqrt(D), 'ii_b1': jnp.zeros((D,), dtype=jnp.float32), 'ii_W2': jax.random.normal(ks[10], (D, D), dtype=jnp.float32) / np.sqrt(D), 'ii_b2': jnp.zeros((D,), dtype=jnp.float32)}
        return inp
    _L0_gnn_all = _L0_gnn_setup()
    _L0_gnn_in = {k: v for k, v in _L0_gnn_all.items() if k in ('pp_W1', 'pp_b1', 'pp_W2', 'pp_b2', 'pi_W1', 'pi_b1', 'pi_W2', 'pi_b2', 'pi_W3', 'ii_W1', 'ii_b1', 'ii_W2', 'ii_b2')}
    del _L0_gnn_all

    def _L1_gnn_setup():
        import jax, jax.numpy as jnp
        import numpy as np
        N, E, D, R, L = (50000, 18750, 64, 65, 2)

        def _rgcn_conv(x, src, dst, edge_type, W_r, W_root, b):
            n, d = x.shape
            r = W_r.shape[0]
            seg = dst * r + edge_type
            msg = x[src]
            agg = jax.ops.segment_sum(msg, seg, num_segments=n * r).reshape(n, r, d)
            cnt = jax.ops.segment_sum(jnp.ones((msg.shape[0],), x.dtype), seg, num_segments=n * r).reshape(n, r, 1)
            mean = agg / jnp.maximum(cnt, 1.0)
            out = jnp.einsum('nrd,rdk->nk', mean, W_r)
            return out + x @ W_root + b
        key = jax.random.key(seed)
        ks = jax.random.split(key, 10)
        x = jax.random.normal(ks[0], (N, D), dtype=jnp.float32)
        edge_index = jax.random.randint(ks[1], (2, E), 0, N, dtype=jnp.int64)
        edge_type = jax.random.randint(ks[2], (E,), 0, R, dtype=jnp.int64)
        s = 1.0 / np.sqrt(D)
        W = jax.random.normal(ks[3], (L, R, D, D), dtype=jnp.float32) * s
        root = jax.random.normal(ks[4], (L, D, D), dtype=jnp.float32) * s
        bias = jax.random.normal(ks[5], (L, D), dtype=jnp.float32) * 0.01
        res_W = jax.random.normal(ks[6], (L, D, D), dtype=jnp.float32) * s
        res_b = jax.random.normal(ks[7], (L, D), dtype=jnp.float32) * 0.01
        return {'x': x, 'edge_index': edge_index, 'edge_type': edge_type, 'W': W, 'root': root, 'bias': bias, 'res_W': res_W, 'res_b': res_b}
    _L1_gnn_all = _L1_gnn_setup()
    _L1_gnn_in = {k: v for k, v in _L1_gnn_all.items() if k in ('W', 'root', 'bias', 'res_W', 'res_b')}
    del _L1_gnn_all
    return {'x': x, 'src': src, 'dst': dst, 'edge_attr_8': edge_attr_8, 'edge_type_65': edge_type_65, 'L0_gnn_pp_W1': _L0_gnn_in['pp_W1'], 'L0_gnn_pp_b1': _L0_gnn_in['pp_b1'], 'L0_gnn_pp_W2': _L0_gnn_in['pp_W2'], 'L0_gnn_pp_b2': _L0_gnn_in['pp_b2'], 'L0_gnn_pi_W1': _L0_gnn_in['pi_W1'], 'L0_gnn_pi_b1': _L0_gnn_in['pi_b1'], 'L0_gnn_pi_W2': _L0_gnn_in['pi_W2'], 'L0_gnn_pi_b2': _L0_gnn_in['pi_b2'], 'L0_gnn_pi_W3': _L0_gnn_in['pi_W3'], 'L0_gnn_ii_W1': _L0_gnn_in['ii_W1'], 'L0_gnn_ii_b1': _L0_gnn_in['ii_b1'], 'L0_gnn_ii_W2': _L0_gnn_in['ii_W2'], 'L0_gnn_ii_b2': _L0_gnn_in['ii_b2'], 'L1_gnn_W': _L1_gnn_in['W'], 'L1_gnn_root': _L1_gnn_in['root'], 'L1_gnn_bias': _L1_gnn_in['bias'], 'L1_gnn_res_W': _L1_gnn_in['res_W'], 'L1_gnn_res_b': _L1_gnn_in['res_b']}

def reference(x, src, dst, edge_attr_8, edge_type_65, L0_gnn_pp_W1, L0_gnn_pp_b1, L0_gnn_pp_W2, L0_gnn_pp_b2, L0_gnn_pi_W1, L0_gnn_pi_b1, L0_gnn_pi_W2, L0_gnn_pi_b2, L0_gnn_pi_W3, L0_gnn_ii_W1, L0_gnn_ii_b1, L0_gnn_ii_W2, L0_gnn_ii_b2, L1_gnn_W, L1_gnn_root, L1_gnn_bias, L1_gnn_res_W, L1_gnn_res_b):
    import jax
    import jax.numpy as jnp

    def _L0_gnn_ref(p, idx_i, idx_j, basis, pp_W1, pp_b1, pp_W2, pp_b2, pi_W1, pi_b1, pi_W2, pi_b2, pi_W3, ii_W1, ii_b1, ii_W2, ii_b2):
        import jax, jax.numpy as jnp
        import numpy as np
        N_NODES = 50000
        N_EDGES = 25000
        D = 64
        N_BASIS = 8
        p1 = jnp.tanh(p @ pp_W1 + pp_b1) @ pp_W2 + pp_b2
        inter = jnp.concatenate([p1[idx_i], p1[idx_j]], axis=-1)
        inter = inter @ pi_W1 + pi_b1
        inter = inter @ pi_W2 + pi_b2
        inter = inter @ pi_W3
        inter = inter.reshape(inter.shape[0], D, N_BASIS)
        i1 = jnp.einsum('ecb,eb->ec', inter, basis)
        i1 = jnp.tanh(i1 @ ii_W1 + ii_b1) @ ii_W2 + ii_b2
        out = jax.ops.segment_sum(i1, idx_j, num_segments=p1.shape[0])
        return out

    def _L1_gnn_ref(x, edge_index, edge_type, W, root, bias, res_W, res_b):
        import jax, jax.numpy as jnp
        import numpy as np
        N, E, D, R, L = (50000, 18750, 64, 65, 2)

        def _rgcn_conv(x, src, dst, edge_type, W_r, W_root, b):
            n, d = x.shape
            r = W_r.shape[0]
            seg = dst * r + edge_type
            msg = x[src]
            agg = jax.ops.segment_sum(msg, seg, num_segments=n * r).reshape(n, r, d)
            cnt = jax.ops.segment_sum(jnp.ones((msg.shape[0],), x.dtype), seg, num_segments=n * r).reshape(n, r, 1)
            mean = agg / jnp.maximum(cnt, 1.0)
            out = jnp.einsum('nrd,rdk->nk', mean, W_r)
            return out + x @ W_root + b
        src, dst = (edge_index[0], edge_index[1])
        h = x
        for l in range(W.shape[0]):
            conv = _rgcn_conv(h, src, dst, edge_type, W[l], root[l], bias[l])
            conv = jax.nn.relu(conv)
            res = jax.nn.relu(h @ res_W[l] + res_b[l])
            h = conv + res
        return h
    edge_index = jnp.stack([src, dst])
    h = jnp.maximum(_layernorm(x, axis=-1), 0.0)
    x = x + _L0_gnn_ref(h, src, dst, edge_attr_8, L0_gnn_pp_W1, L0_gnn_pp_b1, L0_gnn_pp_W2, L0_gnn_pp_b2, L0_gnn_pi_W1, L0_gnn_pi_b1, L0_gnn_pi_W2, L0_gnn_pi_b2, L0_gnn_pi_W3, L0_gnn_ii_W1, L0_gnn_ii_b1, L0_gnn_ii_W2, L0_gnn_ii_b2)
    h = jnp.maximum(_layernorm(x, axis=-1), 0.0)
    x = x + _L1_gnn_ref(h, edge_index, edge_type_65, L1_gnn_W, L1_gnn_root, L1_gnn_bias, L1_gnn_res_W, L1_gnn_res_b)
    return x

_drawn_inputs = setup_inputs


def setup_inputs(seed=0):
    import zlib

    import numpy as np

    out = dict(_drawn_inputs(seed))
    spreads = {'L0_gnn_pp_b1': (0.0, 0.1),
     'L0_gnn_pp_b2': (0.0, 0.1),
     'L0_gnn_pi_b1': (0.0, 0.1),
     'L0_gnn_pi_b2': (0.0, 0.1),
     'L0_gnn_ii_b1': (0.0, 0.1),
     'L0_gnn_ii_b2': (0.0, 0.1)}
    factors = {'L1_gnn_bias': 24.219, 'L1_gnn_res_b': 27.662}
    for name, (base, spread) in spreads.items():
        noise = np.random.default_rng([zlib.crc32(name.encode()), seed]).standard_normal(out[name].shape)
        drawn = base * np.exp(spread * noise) if base else spread * noise
        out[name] = jnp.asarray(drawn.astype(out[name].dtype))
    for name, factor in factors.items():
        out[name] = (out[name] * factor).astype(out[name].dtype)
    return out
```

```python
from contextlib import ExitStack

import concourse.bass as bass
from concourse import mybir

P = 128
D = 64
RELS = 65
BASIS = 8
NODES = 3125
EDGES_ALL = 103125

BINS = (NODES + P - 1) // P
LAST = NODES - (BINS - 1) * P
K = 2
GE = K * P
U = 6
GROUPS = (EDGES_ALL // GE + BINS + U - 1) // U * U
TURNS = GROUPS // U
COLS = (EDGES_ALL + P - 1) // P
FULL = EDGES_ALL // COLS
REST = EDGES_ALL - FULL * COLS
ROWS = P * COLS + 2 * GE
W = 16
SPLIT = 3 * BASIS
PAD_DST = BINS * P
SUP = 4
SUPS = (BINS + SUP - 1) // SUP
NT = SUP * SUPS
SC = 13
SCT = COLS // SC
ND = D + RELS
YW = RELS * D
YU = 1024
NYU = YW // YU
FIVE = 5

ALU = mybir.AluOpType
ACT = mybir.ActivationFunctionType
AX = mybir.AxisListType
F32 = mybir.dt.float32
BF16 = mybir.dt.bfloat16
I32 = mybir.dt.int32
U32 = mybir.dt.uint32


def steps(eng, lead, step):
    for i in range(U):
        step(i, i, 0)
    with eng.Fori(1, TURNS) as t:
        for u in range(U):
            step(t * U + u, u, t)
    for i in range(GROUPS, GROUPS + lead):
        step(i, i % U, i // U)


def live(i, lag):
    return not isinstance(i, int) or 0 <= i - lag < GROUPS


def wait(eng, sem, value):
    if not isinstance(value, int) or value > 0:
        eng.wait_ge(sem, value)


def held_wait(eng, sem, value, tick):
    if not isinstance(value, int) or value > 0:
        eng.wait_ge(sem, value)
        eng.sem_inc(tick, 1)


def uses(l, t, u, lag=0):
    return t + (l * TURNS + (1 if u >= lag else 0))


def build(nc, x, src, dst, basis, etype, pp_W1, pp_b1, pp_W2, pp_b2, pi_W1, pi_b1, pi_W2, pi_b2,
          pi_W3, ii_W1, ii_b1, ii_W2, ii_b2, r_W, r_root, r_bias, r_res_W, r_res_b, out, stop=9):
    rec_d = nc.dram_tensor("rec_d", (ROWS, W), F32, kind="Internal").ap()
    p_d = nc.dram_tensor("p_d", (NT * P, D), F32, kind="Internal").ap()
    y_d = nc.dram_tensor("y_d", (BINS * P * RELS, D), F32, kind="Internal").ap()
    y_rows = y_d.rearrange("(n r) d -> n (r d)", r=RELS)

    with ExitStack() as ctx:
        def sb(name, shape, dt):
            return ctx.enter_context(nc.sbuf_tensor(name, shape, dt))

        def sem(name):
            return ctx.enter_context(nc.semaphore(name))

        region_a = sb("region_a", [P, max(COLS * W, GROUPS * K * W)], F32)
        rec_a = region_a[:, 0:COLS * W].rearrange("p (n w) -> p n w", w=W)
        rec_p = region_a[:, 0:GROUPS * K * W]
        rec_v = rec_p.rearrange("p (t w) -> p t w", w=W)
        region_c = sb("region_c", [P, 9800], F32)
        basis_in = region_c[:, 0:COLS * BASIS].rearrange("p (n b) -> p n b", b=BASIS)
        dst_in = region_c[:, COLS * BASIS:COLS * (BASIS + 1)].bitcast(I32)
        src_in = region_c[:, COLS * (BASIS + 1):COLS * (BASIS + 2)].bitcast(I32)
        typ_in = region_c[:, COLS * (BASIS + 2):COLS * (BASIS + 3)].bitcast(I32)
        y_stage = region_c[:, 0:NYU * YU + D]
        w_rel = region_c[0:D, NYU * YU + D:NYU * YU + D + YW + 2 * D]
        region_r = sb("region_r", [P, 4 * COLS], F32)
        spot = [0]

        def part_of_c(width):
            spot[0] += width
            return region_c[:, spot[0] - width:spot[0]]
        vT = part_of_c(8 * K * P).rearrange("p (s c n) -> p s c n", s=2, c=4)
        uT = part_of_c(2 * K * P).rearrange("p (s n) -> p s n", s=2)
        u_sb = part_of_c(4 * K * D).rearrange("p (s k o d) -> p s k o d", s=2, k=K, o=2)
        ohT_b = part_of_c(K * P).bitcast(BF16).rearrange("p (s n) -> p s n", s=2)
        bT = part_of_c(K * P).bitcast(BF16)[0:SPLIT, :].rearrange("p (s n) -> p s n", s=2)
        spot[0] = NYU * YU + D
        hT, tT, p1T, aT, qT = [part_of_c(SUP * P)[0:D, :] for _ in range(5)]
        p_st = part_of_c(SUP * D).rearrange("p (t d) -> p t d", t=SUP)
        q_st = part_of_c(2 * SUP * D).rearrange("p (s t d) -> p s t d", s=2, t=SUP)
        spot[0] = NYU * YU + D + YW + 2 * D
        s_st = part_of_c(FIVE * (D + 1)).rearrange("p (t d) -> p t d", t=FIVE)
        sT = part_of_c(FIVE * P)[0:D + 1, :]
        bin_of = region_r[:, 0:COLS]
        bin_int = region_r[:, COLS:2 * COLS].bitcast(I32)
        junk = region_r[:, 2 * COLS:3 * COLS]
        place = region_r[:, 3 * COLS:4 * COLS]
        place_i = bin_int
        rr = region_r[:, 0:BINS * 2 * D].rearrange("p (a n) -> p a n", a=BINS)
        next_int = sb("next_int", [P, 1], I32)
        next_bin = sb("next_bin", [P, 1], F32)
        count_pa = sb("count_pa", [P, BINS + 1], F32)
        pad_rec = sb("pad_rec", [P, (ROWS - P * COLS) // P * W], F32)

        ident = sb("ident", [P, P], F32)
        ident_b = sb("ident_b", [P, P], BF16)
        ones = sb("ones", [P, P], F32)
        before = sb("before", [P, P], F32)
        upto = sb("upto", [P, P], F32)
        iota_p = sb("iota_p", [P, P], F32)
        iota_g = sb("iota_g", [P, GROUPS], F32)
        zero_c = sb("zero_c", [P, BINS + 1], F32)
        small = sb("small", [P, 16], F32)
        small_i = sb("small_i", [P, 4], I32)
        mask_ag = sb("mask_ag", [BINS, GROUPS], F32)
        gap_b = sb("gap_b", [BINS, P], F32)
        bin_g = sb("bin_g", [P, GROUPS], F32)
        bin_gi = sb("bin_gi", [P, GROUPS], I32)
        start_g = sb("start_g", [P, GROUPS], F32)
        start_gi = sb("start_gi", [P, GROUPS], I32)
        offset_pa = sb("offset_pa", [P, BINS + 1], F32)
        total_pa = sb("total_pa", [P, BINS + 1], F32)
        flag_i = sb("flag_i", [P, 1], I32)
        place_s = sb("place_s", [P, SC], U32)
        rec_s = sb("rec_s", [P, SC * W], F32)

        x_sb = sb("x_sb", [P, NT, D], F32)
        h_sb = sb("h_sb", [P, NT, D], F32)
        ln_s = sb("ln_s", [P, 3, NT], F32)
        sq = sb("sq", [P, NT, D], F32)
        q_parts = sb("q_parts", [P, NT, 3, D], BF16)
        acc = sb("acc", [P, BINS + 1, ND], F32)
        loc = sb("loc", [P, GROUPS * K], F32)
        typ = sb("typ", [P, GROUPS * K], F32)
        w_edge = sb("w_edge", [P, GROUPS * K], F32)

        w1 = sb("w1", [D, D], F32)
        w2 = sb("w2", [D, D], F32)
        wa = sb("wa", [D, 2, D], F32)
        wi2 = sb("wi2", [D, D], F32)
        w3 = sb("w3", [D, D, BASIS], F32)
        w3t = sb("w3t", [D, BASIS * D], F32)
        wii1 = sb("wii1", [D, D], F32)
        wz = sb("wz", [P, BASIS // 2, D], F32)
        wii2 = sb("wii2", [D + 1, D], F32)
        b1c = sb("b1c", [D, 1], F32)
        b2c = sb("b2c", [D, 1], F32)
        pib1c = sb("pib1c", [D, 1], F32)
        pib2r = sb("pib2r", [P, D], F32)
        iib1 = sb("iib1", [1, D], F32)
        iib1_p = sb("iib1_p", [1, 3, K * D], BF16)
        iib1_s = sb("iib1_s", [3, K * D], BF16)
        ones3 = sb("ones3", [3, P], BF16)
        brr = sb("brr", [P, 2, 2 * D], F32)
        sel_f = sb("sel_f", [SPLIT, 4 * P], F32)
        sel_t = h_sb[0:SPLIT, 0:NT - 4, :].rearrange("k t d -> k (t d)").rearrange("k (t m) -> k t m", t=3)
        sel = sb("sel", [SPLIT, 4, P], BF16)

        h_st = sb("h_st", [P, SUP * D], F32)

        rec_u = sb("rec_u", [P, U, K * W], F32)
        gat = sb("gat", [P, U, K, D], F32)
        oh = sb("oh", [P, U, K, P], F32)
        ohT_f = sb("ohT_f", [P, 2, K * P], F32)
        tr = sb("tr", [P, 2, K, ND], F32)
        hh_st = sb("hh_st", [P, 2, D], F32)
        hhT = sb("hhT", [D, 2, P], F32)
        pick = sb("pick", [P, 2, RELS], F32)

        ps = ctx.enter_context(nc.psum_tensor("ps", [P, 8, 512], F32))
        ps_flat = ps[:, :, :].rearrange("p b n -> p (b n)")
        bb = ps_flat[:, 0:4 * 512].rearrange("p (s c n) -> p s c n", s=2, c=4)
        ps_t, ps_b = ps[:, 4, 0:K * P], ps[:, 4, K * P:K * P + K * D].bitcast(BF16)
        ps_u = ps[:, 5, 0:K * P]
        ps_z = ps[:, 6, 0:K * D]
        ps_s, ps_q = ps[:, 7, 0:ND], ps[:, 7, 256:256 + K * D]
        ps_t2 = [ps[:, 4 + q, 0:K * P] for q in range(2)]
        ps_s2 = [ps[:, 6 + q, 0:D] for q in range(2)]
        ps_w = [ps[:, q, 0:K * RELS].rearrange("p (k r) -> p k r", k=K) for q in range(2)]

        edges_in = sem("edges_in")
        basis_in_s = sem("basis_in_s")
        x_in = sem("x_in")
        w_in = sem("w_in")
        const = sem("const")
        dve_c = sem("dve_c")
        pe_c = sem("pe_c")
        act_c = sem("act_c")
        pool_c = sem("pool_c")
        split_in = sem("split_in")
        counted = sem("counted")
        totals = sem("totals")
        in_groups = sem("in_groups")
        cumulated = sem("cumulated")
        masks = sem("masks")
        spread = sem("spread")
        tables = sem("tables")
        flag = sem("flag")
        placed = sem("placed")
        rec_made = sem("rec_made")
        pad_out = sem("pad_out")
        rec_out = sem("rec_out")
        rec_ready = sem("rec_ready")
        scat = sem("scat")
        scat_in = sem("scat_in")
        rec_in = sem("rec_in")
        w3_t = sem("w3_t")
        w3_c = sem("w3_c")
        wz_p = sem("wz_p")
        wz_c = sem("wz_c")
        var_ready = sem("var_ready")
        std_ready = sem("std_ready")
        h_ready = sem("h_ready")
        n_hs = sem("n_hs")
        n_hp = sem("n_hp")
        n_hT = sem("n_hT")
        n_tp = sem("n_tp")
        n_tT = sem("n_tT")
        n_pp = sem("n_pp")
        n_pT = sem("n_pT")
        n_ap = sem("n_ap")
        n_aT = sem("n_aT")
        n_qT = sem("n_qT")
        n_PQ = sem("n_PQ")
        n_Ps = sem("n_Ps")
        n_Q = sem("n_Q")
        n_Pout = sem("n_Pout")
        loc_ready = sem("loc_ready")
        tick = sem("tick")
        placed_c = sem("placed_c")

        ctx.enter_context(nc.allow_non_contiguous_dma(reason='a few columns of single words'))
        block = ctx.enter_context(nc.Block())

        def gsems(tag, slots):
            return [sem(f"{tag}{u}") for u in range(slots)]

        rec_slot = gsems("rec_slot", U)
        gathered = gsems("gathered", U)
        names = (("oh", "ohT", "ohTc", "bTc", "q", "bb", "u", "uT", "uTc", "v", "z", "t", "rel", "s", "acc"),
                 ("oh", "ohT", "ohTc", "wt", "w", "scaled", "s", "acc"),
                 ("oh", "s", "acc"))
        L = [{n: sem(f"l{l}_{n}") for n in names[l]} for l in range(3)]
        nd = {n: sem(f"nd_{n}") for n in ("st", "tp", "tT", "o", "x", "h")}
        Y = [{n: sem(f"y{l}_{n}") for n in ("w", "st", "tp", "hT", "mm0", "mm1", "mm2", "mm3", "mm4",
                                           "ev0", "ev1", "ev2", "ev3", "ev4", "o0", "o1", "o2", "o3", "h")}
             for l in range(2)]
        final = sem("final")
        out_s = sem("out_s")

        STT = nc.vector.scalar_tensor_tensor
        TT = nc.vector.tensor_tensor
        TS = nc.vector.tensor_scalar

        def cols(ap, row_first, n):
            return ap[row_first * COLS:row_first * COLS + n]

        @block.sync
        def _(sp):
            def edge_array(ap_sb, ap_d, s):
                sp.dma_start(ap_sb[0:FULL, :], ap_d[0:FULL * COLS].rearrange("(p n) -> p n", n=COLS)).then_inc(s, 16)
                sp.dma_start(ap_sb[FULL:FULL + 1, 0:REST],
                             ap_d[FULL * COLS:EDGES_ALL].rearrange("(p n) -> p n", p=1)).then_inc(s, 16)

            sp.wait_ge(const, 1)
            edge_array(dst_in, dst, edges_in)
            sp.dma_start(next_int[0:FULL, :],
                         dst[COLS:EDGES_ALL].rearrange("(n o) -> n o", o=1)[0:(FULL - 1) * COLS + 1:COLS, :]
                         ).then_inc(edges_in, 16)
            edge_array(src_in, src, edges_in)
            edge_array(typ_in, etype, edges_in)
            sp.dma_start(basis_in[0:FULL, :, :],
                         basis[0:FULL * COLS, :].rearrange("(p n) b -> p n b", n=COLS)).then_inc(basis_in_s, 16)
            sp.dma_start(basis_in[FULL:FULL + 1, 0:REST, :],
                         basis[FULL * COLS:EDGES_ALL, :].rearrange("(p n) b -> p n b", p=1)).then_inc(basis_in_s, 16)
            sp.dma_start(x_sb[:, 0:BINS - 1, :],
                         x[0:(BINS - 1) * P, :].rearrange("(a p) d -> p a d", p=P)).then_inc(x_in, 16)
            sp.dma_start(x_sb[0:LAST, BINS - 1, :], x[(BINS - 1) * P:NODES, :]).then_inc(x_in, 16)
            loads = [
                (w1[:, :], pp_W1), (w2[:, :], pp_W2), (wi2[:, :], pi_W2), (wii1[:, :], ii_W1),
                (wa[:, 0, :], pi_W1[0:D, :]), (wa[:, 1, :], pi_W1[D:2 * D, :]),
                (w3[:, :, :], pi_W3.rearrange("d (c b) -> d c b", b=BASIS)),
                (wii2[0:D, :], ii_W2), (wii2[D:D + 1, :], ii_b2.rearrange("(o d) -> o d", o=1)),
                (b1c[:, :], pp_b1.rearrange("(d o) -> d o", o=1)), (b2c[:, :], pp_b2.rearrange("(d o) -> d o", o=1)),
                (pib1c[:, :], pi_b1.rearrange("(d o) -> d o", o=1)),
                (pib2r[:, :], pi_b2.rearrange("(o d) -> o d", o=1).broadcast_to([P, D])),
                (iib1[:, :], ii_b1.rearrange("(o d) -> o d", o=1)),
            ]
            for l in range(2):
                loads.append((brr[:, l, 0:D], r_bias[l:l + 1, :].broadcast_to([P, D])))
                loads.append((brr[:, l, D:2 * D], r_res_b[l:l + 1, :].broadcast_to([P, D])))
            for a, b in loads:
                sp.dma_start(a, b).then_inc(w_in, 16)
            sp.wait_ge(dve_c, SPLIT_DONE)
            sp.dma_start(iib1_s[:, :], iib1_p[0:1, :, :].rearrange("o t d -> (o t) d")
                         if False else iib1_p[0:1, :, :]).then_inc(split_in, 16)
            with sp.Fori(0, SUPS) as j:
                held_wait(sp, n_Ps, j + 1, tick)
                sp.dma_start(p_d[bass.ds(j * (SUP * P), SUP * P), :].rearrange("(t p) d -> p t d", p=P),
                             p_st[:, :, :]).then_inc(n_Pout, 16)
            sp.wait_ge(tables, 1)
            sp.wait_ge(rec_ready, 1)
            with sp.Fori(0, GROUPS) as g:
                first = sp.value_load(start_gi[0:1, bass.ds(g, 1)], min_val=0, max_val=EDGES_ALL)
                sp.dma_start(rec_p[:, bass.ds(g * (K * W), K * W)],
                             rec_d[bass.ds(first, GE), :].rearrange("(p k) w -> p (k w)", k=K)).then_inc(rec_in, 16)

            def slots(l):
                s = L[l]
                sp.wait_ge(rec_in, 16 * GROUPS)

                def step(j, u, t):
                    held_wait(sp, gathered[u], (uses(l, t, u) - 1) * (16 * K), tick)
                    if l == 0:
                        held_wait(sp, s["ohT"], j - U + 1, tick)
                    sp.dma_start(rec_u[:, u, :], rec_p[:, bass.ds(j * (K * W), K * W)]).then_inc(rec_slot[u], 16)
                steps(sp, 0, step)

            slots(0)
            if stop >= 2:
                for l in range(2):
                    y = Y[l]
                    sp.wait_ge(L[l]["acc"], GROUPS)
                    if l == 1:
                        sp.wait_ge(Y[0]["mm4"], BINS)
                    sp.dma_start(w_rel[:, 0:YW].rearrange("d (r k) -> d r k", k=D),
                                 r_W[l].rearrange("r d k -> d r k")).then_inc(y["w"], 16)
                    sp.dma_start(w_rel[:, YW:YW + D], r_root[l]).then_inc(y["w"], 16)
                    sp.dma_start(w_rel[:, YW + D:YW + 2 * D], r_res_W[l]).then_inc(y["w"], 16)

                    def store(a):
                        for c in range(NYU):
                            n = YU + (D if c == NYU - 1 else 0)
                            held_wait(sp, y[f"ev{c}"], a + 1, tick)
                            if c == NYU - 1:
                                held_wait(sp, y["ev4"], a + 1, tick)
                            sp.dma_start(y_rows[bass.ds(a * P, P), c * YU:c * YU + n],
                                         y_stage[:, c * YU:c * YU + n]).then_inc(y[f"o{c}"], 16)
                    with sp.Fori(0, BINS) as a:
                        store(a)
                    slots(l + 1)
            sp.wait_ge(final, 1)
            sp.dma_start(out[0:(BINS - 1) * P, :].rearrange("(a p) d -> p a d", p=P),
                         h_sb[:, 0:BINS - 1, :]).then_inc(out_s, 16)
            sp.dma_start(out[(BINS - 1) * P:NODES, :], h_sb[0:LAST, BINS - 1, :]).then_inc(out_s, 16)
            sp.wait_ge(out_s, 32)
            sp.wait_ge(n_Pout, 16 * SUPS)

        @block.gpsimd
        def _(pool):
            nc.gpsimd.memset(ones[:, :], 1.0).then_inc(pool_c, 1)
            nc.gpsimd.iota(iota_p[:, :], [[1, P]], base=0, channel_multiplier=0,
                           allow_small_or_imprecise_dtypes=True).then_inc(pool_c, 1)
            nc.gpsimd.iota(iota_g[:, :], [[1, GROUPS]], base=0, channel_multiplier=0,
                           allow_small_or_imprecise_dtypes=True).then_inc(pool_c, 1)
            nc.gpsimd.iota(sel_f[:, :], [[-1, BASIS], [0, D]], base=0, channel_multiplier=1,
                           allow_small_or_imprecise_dtypes=True).then_inc(pool_c, 1)
            pool.wait_ge(pool_c, 1)
            nc.gpsimd.affine_select(out=ident[:, :], in_=ones[:, :], compare_op=ALU.is_equal, fill=0.0, base=0,
                                    pattern=[[-1, P]], channel_multiplier=1).then_inc(pool_c, 1)
            nc.gpsimd.affine_select(out=before[:, :], in_=ones[:, :], compare_op=ALU.is_gt, fill=0.0, base=0,
                                    pattern=[[1, P]], channel_multiplier=-1).then_inc(pool_c, 1)
            nc.gpsimd.affine_select(out=upto[:, :], in_=ones[:, :], compare_op=ALU.is_ge, fill=0.0, base=0,
                                    pattern=[[1, P]], channel_multiplier=-1).then_inc(pool_c, 1)

            pool.wait_ge(rec_made, 1)
            pool.dma_start(rec_d[P * COLS:ROWS, :].rearrange("(p n) w -> p (n w)", p=P),
                           pad_rec[:, :]).then_inc(pad_out, 16)
            pool.wait_ge(flag, 1)
            unsorted = pool.value_load(flag_i[0:1, 0:1], min_val=0, max_val=EDGES_ALL)
            with pool.If(unsorted < 1):
                pool.dma_start(rec_d[0:P * COLS, :].rearrange("(p n) w -> p (n w)", p=P),
                               region_a[:, 0:COLS * W]).then_inc(rec_out, 16)
                pool.wait_ge(rec_out, 16)
            with pool.Else():
                pool.wait_ge(placed, 1)
                with pool.Fori(0, SCT) as n:
                    pool.dma_start(rec_s[:, :], region_a[:, bass.ds(n * (SC * W), SC * W)]).then_inc(scat_in, 16)
                    pool.dma_start(place_s[:, :], place_i[:, bass.ds(n * SC, SC)].bitcast(U32)).then_inc(scat_in, 16)
                    pool.wait_ge(scat_in, 32 * (n + 1))
                    pool.sem_inc(tick, 1)
                    for c in range(SC):
                        nc.gpsimd.indirect_dma_start(
                            rec_d[0:P * COLS, :], bass.IndirectOffsetOnAxis(ap=place_s[:, c:c + 1], axis=0),
                            rec_s[:, c * W:(c + 1) * W], None).then_inc(scat, 16)
                    pool.wait_ge(scat, 16 * SC * (n + 1))
                    pool.sem_inc(tick, 1)
            pool.end_ifs()
            pool.wait_ge(pad_out, 16)
            pool.sem_inc(rec_ready, 1)

            def gathers(l):
                s = L[l]
                used = s[("u", "scaled", "s")[l]]

                def step(j, u, t):
                    wait(pool, rec_slot[u], uses(l, t, u) * 16)
                    wait(pool, used, j - U + 1)
                    pool.sem_inc(tick, 1)
                    for k in range(K):
                        word = k * W + (0 if l == 0 else 1)
                        nc.gpsimd.indirect_dma_start(
                            gat[:, u, k, :], None, p_d[0:NODES, :] if l == 0 else y_d[:, :],
                            bass.IndirectOffsetOnAxis(ap=rec_u[:, u, word:word + 1].bitcast(U32), axis=0)
                        ).then_inc(gathered[u], 16)
                steps(pool, 0, step)

            pool.wait_ge(n_Pout, 16 * SUPS)
            gathers(0)
            if stop >= 2:
                for l in range(2):
                    for c in range(NYU):
                        pool.wait_ge(Y[l][f"o{c}"], 16 * BINS)
                    gathers(l + 1)

        @block.scalar
        def _(act):
            A = nc.scalar.activation
            act.wait_ge(w3_t, 1)
            A(w3t[:, :], ps[0:D, 3, :], ACT.Copy).then_inc(w3_c, 1)
            act.wait_ge(wz_p, 1)
            A(wz[:, :, :], ps[:, 2, 0:4 * D].rearrange("p (c d) -> p c d", c=4), ACT.Copy).then_inc(wz_c, 1)
            act.wait_ge(var_ready, 1)
            A(ln_s[:, 2, :], ln_s[:, 1, :], ACT.Sqrt).then_inc(std_ready, 1)
            with act.Fori(0, SUPS) as j:
                act.wait_ge(n_tp, j + 1)
                A(tT[:, :], ps[0:D, 1, :], ACT.Tanh, bias=b1c[:, 0:1]).then_inc(n_tT, 1)
                act.wait_ge(n_pp, j + 1)
                A(p1T[:, :], ps[0:D, 2, :], ACT.Identity, bias=b2c[:, 0:1]).then_inc(n_pT, 1)
                act.wait_ge(n_ap, j + 1)
                A(aT[:, :], ps[0:D, 3, :], ACT.Copy).then_inc(n_aT, 1)
                act.wait_ge(n_PQ, j + 1)
                act.wait_ge(n_Pout, 16 * j)
                A(p_st[:, :, :], ps[:, 5, 0:SUP * D].rearrange("p (t d) -> p t d", t=SUP), ACT.Copy).then_inc(n_Ps, 1)

            s = L[0]

            def step(i, u, t):
                if live(i, 0):
                    a = i % 2 if isinstance(i, int) else u % 2
                    wait(act, s["q"], i - 1)
                    wait(act, s["ohT"], i + 1)
                    A(ohT_b[:, a, :], ps_t, ACT.Copy).then_inc(s["ohTc"], 1)
                    wait(act, s["bb"], i - 1)
                    A(bT[:, a, :], ps_b[0:SPLIT, :], ACT.Copy).then_inc(s["bTc"], 1)
                if live(i, 2):
                    a = u % 2
                    wait(act, s["v"], i - 3)
                    wait(act, s["uT"], i - 1)
                    A(uT[:, a, :], ps_u, ACT.Copy).then_inc(s["uTc"], 1)
                if live(i, 3):
                    a = (u + 1) % 2
                    wait(act, s["s"], i - 4)
                    wait(act, s["z"], i - 2)
                    A(tr[:, a, :, 0:D], ps_z.rearrange("p (k d) -> p k d", k=K),
                      ACT.Tanh).then_inc(s["t"], 1)
            steps(act, 3, step)

            if stop >= 1:
                act.wait_ge(var_ready, 2)
                A(ln_s[:, 2, :], ln_s[:, 1, :], ACT.Sqrt).then_inc(std_ready, 1)
            if stop >= 2:
                for l in range(2):
                    y = Y[l]

                    def turn_y(a, q, ahead):
                        if ahead:
                            act.wait_ge(y["tp"], a + 2)
                            A(hhT[:, 1 - q, :], ps[0:D, 7, (1 - q) * P:(2 - q) * P], ACT.Copy).then_inc(y["hT"], 1)
                        for c in (0, 2):
                            act.wait_ge(y[f"mm{c}"], a + 1)
                            wait(act, y[f"o{c}"], 16 * a)
                            A(y_stage[:, c * YU:(c + 1) * YU], ps_flat[:, c * YU:(c + 1) * YU],
                              ACT.Copy).then_inc(y[f"ev{c}"], 1)
                    act.wait_ge(y["tp"], 1)
                    A(hhT[:, 0, :], ps[0:D, 7, 0:P], ACT.Copy).then_inc(y["hT"], 1)
                    with act.Fori(0, BINS // 2) as pair:
                        turn_y(pair * 2, 0, True)
                        turn_y(pair * 2 + 1, 1, True)
                    turn_y(BINS - 1, 0, False)

                    if l == 0:
                        s = L[1]

                        def step1(i, u, t):
                            if live(i, 0):
                                wait(act, s["wt"], i - 1)
                                wait(act, s["ohT"], i + 1)
                                A(ohT_f[:, u % 2, :], ps_t2[u % 2], ACT.Copy).then_inc(s["ohTc"], 1)
                        steps(act, 0, step1)

        @block.vector
        def _(dve):
            n = [0]

            def link(ins):
                n[0] += 1
                ins.then_inc(dve_c, 1)
                dve.wait_ge(dve_c, n[0])

            lo = FULL // 32 * 32
            nc.vector.memset(basis_in[lo:P, REST:COLS, :], 0.0)
            nc.vector.memset(dst_in[lo:P, REST:COLS], PAD_DST)
            nc.vector.memset(src_in[lo:P, REST:COLS], 0)
            nc.vector.memset(typ_in[lo:P, REST:COLS], 0)
            nc.vector.memset(next_int[:, :], PAD_DST)
            link(nc.vector.memset(x_sb[:, :, :], 0.0))
            link(nc.vector.memset(pad_rec[:, :], 0.0))
            dve.sem_inc(const, 1)
            link(nc.vector.memset(pad_rec[:, :].rearrange("p (n w) -> p n w", w=W)[:, :, 2], float(PAD_DST)))
            nc.vector.memset(acc[:, :, :], 0.0)
            nc.vector.memset(zero_c[:, :], 0.0)
            link(nc.vector.memset(ones3[:, :], 1.0))

            dve.wait_ge(w_in, 16 * 18)
            bsplit = iib1[0:1, :].rearrange("o (k d) -> o k d", k=1).broadcast_to([1, K, D])
            parts = [iib1_p[0:1, t, :].rearrange("o (k d) -> o k d", k=K) for t in range(3)]
            jk = junk[0:1, 0:K * D].rearrange("o (k d) -> o k d", k=K)
            link(nc.vector.tensor_copy(parts[0], bsplit))
            link(TT(jk, bsplit, parts[0], ALU.subtract))
            link(nc.vector.tensor_copy(parts[1], jk))
            link(TT(jk, jk, parts[1], ALU.subtract))
            link(nc.vector.tensor_copy(parts[2], jk))
            assert n[0] == SPLIT_DONE
            dve.wait_ge(pool_c, 7)
            for t in range(3):
                nc.vector.tensor_scalar(sel_t[:, t, :], sel_f[:, :], float(BASIS * t), None, ALU.is_equal
                                        ).then_inc(dve_c, 1)
                n[0] += 1
            nc.vector.tensor_copy(ident_b[:, :], ident[:, :]).then_inc(dve_c, 1)
            n[0] += 1
            dve.wait_ge(dve_c, n[0])
            link(TT(sel_t[:, 0, :], sel_t[:, 0, :], sel_t[:, 1, :], ALU.add))
            link(TT(sel[:, :, :].rearrange("k c m -> k (c m)"), sel_t[:, 0, :], sel_t[:, 2, :], ALU.add))

            dve.wait_ge(edges_in, 16 * 7)
            nc.vector.tensor_single_scalar(next_int[:, :], next_int[:, :], 7, ALU.arith_shift_right).then_inc(dve_c, 1)
            n[0] += 1
            link(nc.vector.tensor_single_scalar(bin_int[:, :], dst_in, 7, ALU.arith_shift_right))
            nc.vector.tensor_copy(next_bin[:, :], next_int[:, :]).then_inc(dve_c, 1)
            n[0] += 1
            link(nc.vector.tensor_copy(bin_of[:, :], bin_int[:, :]))
            for a in range(BINS + 1):
                link(TS(junk[:, :], bin_of[:, :], float(a), 0.0, ALU.is_equal, ALU.add,
                        accum_out=count_pa[:, a:a + 1]))
            link(TT(junk[:, 0:COLS - 1], bin_of[:, 0:COLS - 1], bin_of[:, 1:COLS], ALU.is_gt))
            link(TT(junk[:, COLS - 1:COLS], bin_of[:, COLS - 1:COLS], next_bin[:, :], ALU.is_gt))
            link(nc.vector.tensor_reduce(small[:, 0:1], junk[:, :], AX.X, ALU.add))
            dve.sem_inc(counted, 1)
            dve.wait_ge(totals, 1)
            link(nc.vector.tensor_copy(small[:, 1:2], ps[:, 6, 0:1]))
            link(TS(small[0:BINS + 1, 2:3], small[0:BINS + 1, 1:2], float(GE - 1), None, ALU.add)
                 if False else nc.vector.tensor_copy(small[0:BINS + 1, 2:3], ps[0:BINS + 1, 6, 1:2]))
            link(TS(small[0:BINS, 3:4], small[0:BINS, 2:3], float(GE - 1), None, ALU.add))
            link(nc.vector.tensor_copy(small_i[0:BINS, 0:1], small[0:BINS, 3:4]))
            link(nc.vector.tensor_single_scalar(small_i[0:BINS, 1:2], small_i[0:BINS, 0:1], GE.bit_length() - 1,
                                                ALU.arith_shift_right))
            nc.vector.tensor_copy(flag_i[:, :], small[:, 1:2]).then_inc(dve_c, 1)
            n[0] += 1
            link(nc.vector.tensor_copy(small[0:BINS, 4:5], small_i[0:BINS, 1:2]))
            dve.sem_inc(flag, 1)
            dve.sem_inc(in_groups, 1)
            link(STT(out=small[0:BINS, 5:6], in0=small[0:BINS, 4:5], scalar=-float(GE),
                     in1=small[0:BINS, 2:3], op0=ALU.mult, op1=ALU.add))
            link(nc.vector.tensor_copy(gap_b[:, :], small[0:BINS, 5:6].broadcast_to([BINS, P])))
            dve.wait_ge(cumulated, 1)
            link(nc.vector.tensor_copy(small[0:BINS, 6:7], ps[0:BINS, 6, 2:3]))
            link(TS(mask_ag[:, :], iota_g[0:BINS, :], small[0:BINS, 6:7], None, ALU.is_ge))
            dve.sem_inc(masks, 1)
            dve.wait_ge(spread, 1)
            link(nc.vector.tensor_copy(bin_g[:, :], ps[:, 4, 0:GROUPS]))
            link(STT(out=start_g[:, :], in0=iota_g[:, :], scalar=float(GE), in1=ps[:, 5, 0:GROUPS],
                     op0=ALU.mult, op1=ALU.add))
            link(TS(start_g[:, :], start_g[:, :], float(EDGES_ALL), None, ALU.min))
            link(nc.vector.tensor_copy(start_gi[:, :], start_g[:, :]))
            link(nc.vector.tensor_copy(bin_gi[:, :], bin_g[:, :]))
            dve.sem_inc(tables, 1)

            link(nc.vector.tensor_copy(rec_a[:, :, 0].bitcast(I32), src_in))
            link(STT(out=rec_a[:, :, 1].bitcast(I32), in0=src_in, scalar=float(RELS), in1=typ_in,
                     op0=ALU.mult, op1=ALU.add))
            link(nc.vector.tensor_copy(rec_a[:, :, 2], dst_in))
            link(nc.vector.tensor_copy(rec_a[:, :, 3], typ_in))
            dve.wait_ge(basis_in_s, 32)
            part = [region_a[:, 0:COLS * W].bitcast(BF16).rearrange("p (n w) -> p n w", w=2 * W)
                    [:, :, 8 + BASIS * t:8 + BASIS * (t + 1)] for t in range(3)]
            link(nc.vector.tensor_copy(part[0], basis_in))
            link(TT(basis_in, basis_in, part[0], ALU.subtract))
            link(nc.vector.tensor_copy(part[1], basis_in))
            link(TT(part[2], basis_in, part[1], ALU.subtract))
            dve.sem_inc(rec_made, 1)

            out_of_order = dve.value_load(flag_i[0:1, 0:1], min_val=0, max_val=EDGES_ALL)
            with dve.If(out_of_order > 0):
                m = [0]

                def slow(ins):
                    m[0] += 1
                    ins.then_inc(placed_c, 1)
                    dve.wait_ge(placed_c, m[0])
                slow(nc.vector.tensor_copy(total_pa[:, :], ps[:, 6, 64:64 + BINS + 1]))
                slow(nc.vector.tensor_tensor_scan(offset_pa[:, :], total_pa[:, :], zero_c[:, :], 0.0, ALU.add, ALU.add))
                slow(TT(offset_pa[:, :], offset_pa[:, :], total_pa[:, :], ALU.subtract))
                slow(TT(offset_pa[:, :], offset_pa[:, :], ps[:, 6, 128:128 + BINS + 1], ALU.add))
                slow(nc.vector.memset(place[:, :], -1.0))
                same, ranks = basis_in.rearrange("p n b -> p (n b)")[:, 0:COLS], \
                    basis_in.rearrange("p n b -> p (n b)")[:, COLS:2 * COLS]
                slow(nc.vector.memset(junk[:, :], 0.0))
                for a in range(BINS + 1):
                    slow(TS(same, bin_of[:, :], float(a), None, ALU.is_equal))
                    slow(nc.vector.tensor_tensor_scan(ranks, same, junk[:, :], 0.0, ALU.add, ALU.add))
                    slow(STT(out=ranks, in0=ranks, scalar=offset_pa[:, a:a + 1], in1=same, op0=ALU.add, op1=ALU.mult))
                    slow(TT(place[:, :], place[:, :], ranks, ALU.add))
                slow(nc.vector.tensor_copy(place_i[:, :], place[:, :]))
                dve.sem_inc(placed, 1)
            dve.end_ifs()

            def layernorm(tiles, k):
                xs, hs, qs = x_sb[:, 0:tiles, :], h_sb[:, 0:tiles, :], sq[:, 0:tiles, :]

                def bc(i):
                    return ln_s[:, i, 0:tiles].rearrange("p (t o) -> p t o", o=1).broadcast_to([P, tiles, D])
                link(nc.vector.tensor_reduce(ln_s[:, 0, 0:tiles], xs, AX.X, ALU.add))
                link(TS(ln_s[:, 0, 0:tiles], ln_s[:, 0, 0:tiles], 1.0 / D, None, ALU.mult))
                link(TT(hs, xs, bc(0), ALU.subtract))
                link(TT(qs, hs, hs, ALU.mult))
                link(nc.vector.tensor_reduce(ln_s[:, 1, 0:tiles], qs, AX.X, ALU.add))
                link(TS(ln_s[:, 1, 0:tiles], ln_s[:, 1, 0:tiles], 1.0 / D, 1e-5, ALU.mult, ALU.add))
                dve.sem_inc(var_ready, 1)
                dve.wait_ge(std_ready, k)
                link(nc.vector.reciprocal(ln_s[:, 0, 0:tiles], ln_s[:, 2, 0:tiles]))
                link(STT(out=hs, in0=hs, scalar=0.0, in1=bc(0), op0=ALU.max, op1=ALU.mult))

            dve.wait_ge(x_in, 32)
            layernorm(NT, 1)
            hf = h_sb[:, :, :].rearrange("p t d -> p (t d)")
            with dve.Fori(0, SUPS) as j:
                wait(dve, n_hp, j)
                nc.vector.tensor_copy(h_st[:, :], hf[:, bass.ds(j * (SUP * D), SUP * D)]).then_inc(n_hs, 1)
                dve.wait_ge(n_hp, j + 1)
                nc.vector.tensor_copy(hT[:, :], ps[0:D, 0, :]).then_inc(n_hT, 1)
                dve.wait_ge(n_ap, j + 1)
                TS(qT[:, :], ps[0:D, 4, :], pib1c[:, 0:1], None, ALU.add).then_inc(n_qT, 1)
                dve.wait_ge(n_PQ, j + 1)
                q0, q1 = q_st[:, 0, :, :], q_st[:, 1, :, :]
                qd = q_parts[:, :, :, :].rearrange("p t s d -> p t (s d)")
                qp = [qd[:, bass.ds(j * SUP, SUP), t * D:(t + 1) * D] for t in range(3)]
                TT(q0, ps[:, 6, 0:SUP * D].rearrange("p (t d) -> p t d", t=SUP),
                   pib2r[:, :].rearrange("p (o d) -> p o d", o=1).broadcast_to([P, SUP, D]), ALU.add).then_inc(n_Q, 1)
                dve.wait_ge(n_Q, j * 5 + 1)
                nc.vector.tensor_copy(qp[0], q0).then_inc(n_Q, 1)
                dve.wait_ge(n_Q, j * 5 + 2)
                TT(q1, q0, qp[0], ALU.subtract).then_inc(n_Q, 1)
                dve.wait_ge(n_Q, j * 5 + 3)
                nc.vector.tensor_copy(qp[1], q1).then_inc(n_Q, 1)
                dve.wait_ge(n_Q, j * 5 + 4)
                TT(qp[2], q1, qp[1], ALU.subtract).then_inc(n_Q, 1)

            dve.wait_ge(rec_in, 16 * GROUPS)
            base = bin_g[:, :].rearrange("p (g o) -> p g o", o=1).broadcast_to([P, GROUPS, K])
            nc.vector.tensor_copy(typ[:, :], rec_v[:, :, 3]).then_inc(dve_c, 1)
            n[0] += 1
            link(STT(out=loc[:, :].rearrange("p (g k) -> p g k", k=K), in0=base, scalar=-float(P),
                     in1=rec_v[:, :, 2].rearrange("p (g k) -> p g k", k=K), op0=ALU.mult, op1=ALU.add))

            iota3 = iota_p[:, :].rearrange("p (o m) -> p o m", o=1).broadcast_to([P, K, P])
            iota_r = iota_p[:, 0:RELS].rearrange("p (o m) -> p o m", o=1).broadcast_to([P, K, RELS])

            def per_edge(ap, j, width):
                return ap[:, bass.ds(j * K, K)].rearrange("p (k o) -> p k o", o=1).broadcast_to([P, K, width])

            def add_to_bin(j, width, s, sums_ps):
                b = dve.value_load(bin_gi[0:1, bass.ds(j, 1)], min_val=0, max_val=BINS)
                dst_acc = acc[:, :, :].rearrange("p a n -> p (a n)")[:, bass.ds(b * ND, width)]
                wait(dve, s["acc"], j)
                wait(dve, s["s"], j + 1)
                TT(dst_acc, dst_acc, sums_ps, ALU.add).then_inc(s["acc"], 1)

            s = L[0]

            def step(i, u, t):
                if live(i, 0):
                    wait(dve, s["s"], i - U + 1)
                    TT(oh[:, u, :, :], iota3, per_edge(loc, i, P), ALU.is_equal).then_inc(s["oh"], 1)
                if live(i, 3):
                    a = (u + 1) % 2
                    wait(dve, s["z"], i - 4)
                    wait(dve, s["bb"], i - 2)
                    wait(dve, s["uTc"], i - 2)
                    TT(vT[:, a, :, :], bb[:, a, :, :],
                       uT[:, a, :].rearrange("p (o n) -> p o n", o=1).broadcast_to([P, 4, K * P]),
                       ALU.mult).then_inc(s["v"], 1)
                    wait(dve, s["s"], i - 4)
                    TT(tr[:, a, :, D:ND], iota_r, per_edge(typ, i - 3, RELS), ALU.is_equal).then_inc(s["rel"], 1)
                if live(i, 5):
                    if live(i, 2):
                        wait(dve, s["q"], i - 1)
                    add_to_bin(i - 5, ND, s, ps_s)
                if live(i, 2):
                    a = u % 2
                    v = (u - 2) % U
                    wait(dve, gathered[v], uses(0, t, u, 2) * (16 * K))
                    wait(dve, s["uT"], i - 3)
                    wait(dve, s["q"], i - 1)
                    TT(u_sb[:, a, :, :, :],
                       gat[:, v, :, :].rearrange("p k (o d) -> p k o d", o=1).broadcast_to([P, K, 2, D]),
                       ps_q.rearrange("p (k o d) -> p k o d", k=K, o=1).broadcast_to([P, K, 2, D]),
                       ALU.add).then_inc(s["u"], 1)
            steps(dve, 5, step)

            if stop < 1:
                dve.wait_ge(s["acc"], GROUPS)
                nc.vector.tensor_copy(h_sb[:, 0:BINS, :], acc[:, 0:BINS, 0:D]).then_inc(final, 1)
                return

            sums, counts = acc[:, 0:BINS, 0:D], acc[:, 0:BINS, D:ND]
            dve.wait_ge(s["acc"], GROUPS)
            link(nc.vector.tensor_reduce(ln_s[:, 0, 0:BINS], counts, AX.X, ALU.add))
            xf = x_sb[:, :, :].rearrange("p t d -> p (t d)")
            with dve.Fori(0, BINS // FIVE) as j:
                wait(dve, nd["tp"], j)
                nc.vector.tensor_copy(s_st[:, :, 0:D], acc[:, bass.ds(j * FIVE, FIVE), 0:D]).then_inc(nd["st"], 1)
                nc.vector.tensor_copy(s_st[:, :, D:D + 1].rearrange("p t o -> p (t o)"),
                                      ln_s[:, 0, bass.ds(j * FIVE, FIVE)]).then_inc(nd["st"], 1)
                dve.wait_ge(nd["tp"], j + 1)
                nc.vector.tensor_copy(sT[:, :], ps_flat[0:D + 1, 0:FIVE * P]).then_inc(nd["tT"], 1)
                dve.wait_ge(nd["o"], j + 1)
                xj = xf[:, bass.ds(j * (FIVE * D), FIVE * D)]
                TT(xj, xj, ps[:, 2, 0:FIVE * D], ALU.add).then_inc(nd["x"], 1)
            dve.wait_ge(nd["x"], BINS // FIVE)
            link(TS(counts, counts, 1.0, None, ALU.max))
            link(nc.vector.reciprocal(counts, counts))
            link(nc.vector.memset(sums, 0.0))
            layernorm(BINS, 2)
            dve.sem_inc(h_ready, 1)
            if stop < 2:
                nc.vector.tensor_copy(h_sb[:, 0:BINS, :], x_sb[:, 0:BINS, :]).then_inc(final, 1)
                return

            for l in range(2):
                y = Y[l]

                def stage(a, q):
                    nc.vector.tensor_copy(hh_st[:, q, :], hf[:, bass.ds(a * D, D)]).then_inc(y["st"], 1)

                def turn_y(a, q, ahead):
                    if ahead:
                        wait(dve, y["tp"], a)
                        stage(a + 1, 1 - q)
                    for c in (1, 3):
                        dve.wait_ge(y[f"mm{c}"], a + 1)
                        wait(dve, y[f"o{c}"], 16 * a)
                        r = 0 if c == 3 else c
                        nc.vector.tensor_copy(y_stage[:, c * YU:(c + 1) * YU],
                                              ps_flat[:, r * YU:(r + 1) * YU]).then_inc(y[f"ev{c}"], 1)
                    dve.wait_ge(y["mm4"], a + 1)
                    nc.vector.tensor_copy(y_stage[:, NYU * YU:NYU * YU + D], ps[:, 6, 0:D]).then_inc(y["ev4"], 1)
                    TT(rr[:, :, :].rearrange("p a n -> p (a n)")[:, bass.ds(a * (2 * D), 2 * D)],
                       ps[:, 6, D:3 * D], brr[:, l, :], ALU.add).then_inc(y["h"], 1)
                stage(0, 0)
                with dve.Fori(0, BINS // 2) as pair:
                    turn_y(pair * 2, 0, True)
                    turn_y(pair * 2 + 1, 1, True)
                turn_y(BINS - 1, 0, False)

                s = L[l + 1]
                if l == 0:
                    def step1(i, u, t):
                        if live(i, 0):
                            wait(dve, s["s"], i - U + 1)
                            TT(oh[:, u, :, :], iota3, per_edge(loc, i, P), ALU.is_equal).then_inc(s["oh"], 1)
                        if live(i, 3):
                            a, v = (u + 1) % 2, (u - 3) % U
                            wait(dve, s["wt"], i - 2)
                            for k in range(K):
                                e = (i - 3) * K + k
                                STT(out=pick[:, k, :], in0=iota_p[:, 0:RELS], scalar=typ[:, bass.ds(e, 1)],
                                    in1=ps_w[a][:, k, :], op0=ALU.is_equal, op1=ALU.mult,
                                    accum_out=w_edge[:, bass.ds(e, 1)]).then_inc(s["w"], 1)
                            wait(dve, s["w"], K * (i - 2))
                            wait(dve, gathered[v], uses(1, t, u, 3) * (16 * K))
                            wait(dve, s["s"], i - 4)
                            TT(tr[:, a, :, 0:D], gat[:, v, :, :], per_edge(w_edge, i - 3, D), ALU.mult
                               ).then_inc(s["scaled"], 1)
                        if live(i, 5):
                            add_to_bin(i - 5, D, s, ps_s2[(u + 1) % 2])
                    steps(dve, 5, step1)
                else:
                    def step2(i, u, t):
                        if live(i, 0):
                            wait(dve, s["s"], i - U + 1)
                            for k in range(K):
                                e = i * K + k
                                TS(oh[:, u, k, :], iota_p[:, :], loc[:, bass.ds(e, 1)], w_edge[:, bass.ds(e, 1)],
                                   ALU.is_equal, ALU.mult).then_inc(s["oh"], 1)
                        if live(i, 3):
                            add_to_bin(i - 3, D, s, ps_s2[(u + 1) % 2])
                    steps(dve, 3, step2)
                dve.wait_ge(s["acc"], GROUPS)
                link(TT(sq[:, 0:BINS, :], sums, rr[:, :, 0:D], ALU.add))
                link(TS(rr[:, :, D:2 * D], rr[:, :, D:2 * D], 0.0, None, ALU.max))
                link(STT(out=h_sb[:, 0:BINS, :], in0=sq[:, 0:BINS, :], scalar=0.0, in1=rr[:, :, D:2 * D],
                         op0=ALU.max, op1=ALU.add))
                if l == 0:
                    link(nc.vector.memset(sums, 0.0))
            TT(h_sb[:, 0:BINS, :], h_sb[:, 0:BINS, :], x_sb[:, 0:BINS, :], ALU.add).then_inc(final, 1)

        @block.tensor
        def _(pe):
            MM = nc.tensor.matmul
            pe.wait_ge(w_in, 16 * 18)
            pe.wait_ge(pool_c, 7)
            for b in range(BASIS):
                mm = MM(ps[0:D, 3, b * D:(b + 1) * D], w3[:, :, b], ident[0:D, 0:D], start=True, stop=True)
            mm.then_inc(w3_t, 1)
            pe.wait_ge(w3_c, 1)
            for c in range(4):
                mm = MM(ps[:, 2, c * D:(c + 1) * D], w3t[:, c * P:(c + 1) * P], wii1[:, :], start=True, stop=True)
            mm.then_inc(wz_p, 1)
            pe.wait_ge(counted, 1)
            MM(ps[:, 6, 0:1], ones[:, :], small[:, 0:1], start=True, stop=True)
            MM(ps[0:BINS + 1, 6, 1:2], count_pa[:, :], ones[:, 0:1], start=True, stop=True)
            MM(ps[:, 6, 64:64 + BINS + 1], ones[:, :], count_pa[:, :], start=True, stop=True)
            MM(ps[:, 6, 128:128 + BINS + 1], before[:, :], count_pa[:, :], start=True, stop=True).then_inc(totals, 1)
            pe.wait_ge(in_groups, 1)
            MM(ps[0:BINS, 6, 2:3], upto[0:BINS, 0:BINS], small[0:BINS, 4:5], start=True, stop=True
               ).then_inc(cumulated, 1)
            pe.wait_ge(masks, 1)
            MM(ps[:, 4, 0:GROUPS], ones[0:BINS, :], mask_ag[:, :], start=True, stop=True)
            MM(ps[:, 5, 0:GROUPS], gap_b[:, :], mask_ag[:, :], start=True, stop=True).then_inc(spread, 1)

            pe.wait_ge(wz_c, 1)
            with pe.Fori(0, SUPS) as j:
                held_wait(pe, n_hs, j + 1, tick)
                for t in range(SUP):
                    mm = MM(ps[0:D, 0, t * P:(t + 1) * P], h_st[:, t * D:(t + 1) * D], ident[:, :],
                            start=True, stop=True)
                mm.then_inc(n_hp, 1)
                held_wait(pe, n_hT, j + 1, tick)
                MM(ps[0:D, 1, :], w1[:, :], hT[:, :], start=True, stop=True).then_inc(n_tp, 1)
                held_wait(pe, n_tT, j + 1, tick)
                MM(ps[0:D, 2, :], w2[:, :], tT[:, :], start=True, stop=True).then_inc(n_pp, 1)
                held_wait(pe, n_pT, j + 1, tick)
                MM(ps[0:D, 3, :], wa[:, 0, :], p1T[:, :], start=True, stop=True)
                MM(ps[0:D, 4, :], wa[:, 1, :], p1T[:, :], start=True, stop=True).then_inc(n_ap, 1)
                held_wait(pe, n_aT, j + 1, tick)
                held_wait(pe, n_qT, j + 1, tick)
                wait(pe, n_Q, j * 5)
                for t in range(SUP):
                    MM(ps[:, 5, t * D:(t + 1) * D], aT[:, t * P:(t + 1) * P], wi2[:, :], start=True, stop=True)
                    mm = MM(ps[:, 6, t * D:(t + 1) * D], qT[:, t * P:(t + 1) * P], wi2[:, :], start=True, stop=True)
                mm.then_inc(n_PQ, 1)

            pe.wait_ge(n_Q, SUPS * 5)
            pe.wait_ge(n_Ps, SUPS)
            pe.wait_ge(split_in, 16)
            s = L[0]
            qf = q_parts[:, :, :, :].rearrange("p t s d -> p (t s d)")
            Z3 = (3 * D)

            def step(i, u, t):
                if live(i, 0):
                    a = u % 2
                    wait(pe, s["oh"], i + 1)
                    wait(pe, s["bTc"], i)
                    for k in range(K):
                        pe.transpose(ps_t[:, k * P:(k + 1) * P], oh[:, u, k, :], ident[:, :])
                    wait(pe, rec_slot[u], uses(0, t, u) * 16)
                    for k in range(K):
                        mm = pe.transpose(ps_b[0:SPLIT, k * P:(k + 1) * P],
                                          rec_u[:, u, k * W + 4:(k + 1) * W].bitcast(BF16), ident_b[:, :])
                    mm.then_inc(s["ohT"], 1)
                if live(i, 2):
                    a = u % 2
                    wait(pe, s["u"], i - 1)
                    wait(pe, s["uTc"], i - 2)
                    for k in range(K):
                        mm = pe.transpose(ps_u[:, k * P:(k + 1) * P],
                                          u_sb[:, a, k, :, :].rearrange("p o d -> p (o d)"), ident[:, :])
                    mm.then_inc(s["uT"], 1)
                if live(i, 4):
                    a, v = u % 2, (u - 4) % U
                    wait(pe, s["acc"], i - 4)
                    wait(pe, s["t"], i - 3)
                    wait(pe, s["rel"], i - 3)
                    if live(i, 2):
                        wait(pe, s["u"], i - 1)
                    for k in range(K):
                        mm = MM(ps_s, oh[:, v, k, :], tr[:, a, k, :], start=(k == 0), stop=(k == K - 1))
                    mm.then_inc(s["s"], 1)
                if live(i, 1):
                    a = (u + 1) % 2
                    b = pe.value_load(bin_gi[0:1, bass.ds(i - 1, 1)], min_val=0, max_val=BINS)
                    wait(pe, s["ohTc"], i)
                    wait(pe, s["u"], i - 1)
                    for k in range(K):
                        for part in range(3):
                            mm = MM(ps_q[:, k * D:(k + 1) * D], ohT_b[:, a, k * P:(k + 1) * P],
                                    qf[:, bass.ds(b * Z3 + part * D, D)], start=(part == 0), stop=(part == 2))
                    mm.then_inc(s["q"], 1)
                if live(i, 3):
                    a = (u + 1) % 2
                    wait(pe, s["v"], i - 2)
                    wait(pe, s["t"], i - 3)
                    for k in range(K):
                        MM(ps_z[:, k * D:(k + 1) * D], ones3[:, :], iib1_s[:, 0:D], start=True, stop=False)
                        for c in range(4):
                            mm = MM(ps_z[:, k * D:(k + 1) * D], vT[:, a, c, k * P:(k + 1) * P], wz[:, c, :],
                                    start=False, stop=(c == 3))
                    mm.then_inc(s["z"], 1)
                if live(i, 1):
                    a = (u + 1) % 2
                    wait(pe, s["bTc"], i)
                    for c in range(4):
                        mm = MM(bb[:, a, c, :], sel[:, c, :], bT[:, a, :], start=True, stop=True)
                    mm.then_inc(s["bb"], 1)
            steps(pe, 4, step)

            if stop < 1:
                return
            pe.wait_ge(s["acc"], GROUPS)
            with pe.Fori(0, BINS // FIVE) as j:
                pe.wait_ge(nd["st"], 2 * (j + 1))
                for t in range(FIVE):
                    mm = MM(ps_flat[0:D + 1, t * P:(t + 1) * P], s_st[:, t, :], ident[:, :], start=True, stop=True)
                mm.then_inc(nd["tp"], 1)
                pe.wait_ge(nd["tT"], j + 1)
                wait(pe, nd["x"], j)
                for t in range(FIVE):
                    mm = MM(ps[:, 2, t * D:(t + 1) * D], sT[:, t * P:(t + 1) * P], wii2[:, :], start=True, stop=True)
                mm.then_inc(nd["o"], 1)
            if stop < 2:
                return

            for l in range(2):
                y = Y[l]

                def transpose_h(a, q):
                    pe.wait_ge(y["st"], a + 1)
                    MM(ps[0:D, 7, q * P:(q + 1) * P], hh_st[:, q, :], ident[:, :], start=True, stop=True
                       ).then_inc(y["tp"], 1)

                def turn_y(a, q, ahead):
                    pe.wait_ge(y["hT"], a + 1)
                    if ahead:
                        transpose_h(a + 1, 1 - q)
                    for c in range(NYU):
                        r = 0 if c == 3 else c
                        if c == 3:
                            pe.wait_ge(y["ev0"], a + 1)
                        else:
                            wait(pe, y["ev3" if c == 0 else f"ev{c}"], a)
                        for half in range(2):
                            o = c * YU + half * 512
                            mm = MM(ps_flat[:, r * YU + half * 512:r * YU + (half + 1) * 512], hhT[:, q, :],
                                    w_rel[:, o:o + 512], start=True, stop=True)
                        mm.then_inc(y[f"mm{c}"], 1)
                    wait(pe, y["ev4"], a)
                    wait(pe, y["h"], a)
                    MM(ps[:, 6, 0:3 * D], hhT[:, q, :], w_rel[:, NYU * YU:NYU * YU + 3 * D],
                       start=True, stop=True).then_inc(y["mm4"], 1)
                pe.wait_ge(y["w"], 48)
                transpose_h(0, 0)
                with pe.Fori(0, BINS // 2) as pair:
                    turn_y(pair * 2, 0, True)
                    turn_y(pair * 2 + 1, 1, True)
                turn_y(BINS - 1, 0, False)
                for c in range(4):
                    pe.wait_ge(y[f"ev{c}"], BINS)
                pe.wait_ge(y["h"], BINS)
                pe.wait_ge(y["ev4"], BINS)

                s = L[l + 1]
                af = acc[:, :, :].rearrange("p a n -> p (a n)")
                if l == 0:
                    def step1(i, u, t):
                        if live(i, 0):
                            a = u % 2
                            wait(pe, s["oh"], i + 1)
                            wait(pe, s["ohTc"], i - 1)
                            for k in range(K):
                                mm = pe.transpose(ps_t2[a][:, k * P:(k + 1) * P], oh[:, u, k, :], ident[:, :])
                            mm.then_inc(s["ohT"], 1)
                        if live(i, 4):
                            a, v = u % 2, (u - 4) % U
                            wait(pe, s["acc"], i - 5)
                            wait(pe, s["scaled"], i - 3)
                            for k in range(K):
                                mm = MM(ps_s2[a], oh[:, v, k, :], tr[:, a, k, 0:D],
                                        start=(k == 0), stop=(k == K - 1))
                            mm.then_inc(s["s"], 1)
                        if live(i, 1):
                            a = (u + 1) % 2
                            b = pe.value_load(bin_gi[0:1, bass.ds(i - 1, 1)], min_val=0, max_val=BINS)
                            wait(pe, s["ohTc"], i)
                            wait(pe, s["w"], K * (i - 2))
                            for k in range(K):
                                mm = MM(ps_w[a][:, k, :], ohT_f[:, a, k * P:(k + 1) * P],
                                        af[:, bass.ds(b * ND + D, RELS)], start=True, stop=True)
                            mm.then_inc(s["wt"], 1)
                    steps(pe, 4, step1)
                else:
                    def step2(i, u, t):
                        if live(i, 2):
                            a, v = u % 2, (u - 2) % U
                            wait(pe, s["oh"], K * (i - 1))
                            wait(pe, gathered[v], uses(2, t, u, 2) * (16 * K))
                            wait(pe, s["acc"], i - 3)
                            for k in range(K):
                                mm = MM(ps_s2[a], oh[:, v, k, :], gat[:, v, k, :],
                                        start=(k == 0), stop=(k == K - 1))
                            mm.then_inc(s["s"], 1)
                    steps(pe, 2, step2)


SPLIT_DONE = 9

_INS = ["x", "src", "dst", "edge_attr_8", "edge_type_65",
        "L0_gnn_pp_W1", "L0_gnn_pp_b1", "L0_gnn_pp_W2", "L0_gnn_pp_b2", "L0_gnn_pi_W1", "L0_gnn_pi_b1",
        "L0_gnn_pi_W2", "L0_gnn_pi_b2", "L0_gnn_pi_W3", "L0_gnn_ii_W1", "L0_gnn_ii_b1", "L0_gnn_ii_W2",
        "L0_gnn_ii_b2", "L1_gnn_W", "L1_gnn_root", "L1_gnn_bias", "L1_gnn_res_W", "L1_gnn_res_b"]


def kernel(**inputs):
    import numpy as np
    import concourse.bacc as bacc
    from concourse.bass_utils import run_bass_kernel_spmd

    nc = bacc.Bacc("TRN2", target_bir_lowering=False, num_devices=1)
    arrays, args = {}, []
    for name in _INS:
        a = np.ascontiguousarray(inputs[name])
        arrays[f"in_{name}"] = a
        args.append(nc.dram_tensor(f"in_{name}", a.shape, mybir.dt.from_np(a.dtype), kind="ExternalInput").ap())
    args.append(nc.dram_tensor("out_0", (NODES, D), F32, kind="ExternalOutput").ap())
    build(nc, *args)
    r = run_bass_kernel_spmd(nc, [arrays], core_ids=[0])
    return r.results[0]["out_0"]
```

```python
from contextlib import ExitStack

import concourse.bass as bass
from concourse import mybir

P = 128
D = 64
RELS = 65
BASIS = 8
NODES = 3125
EDGES_ALL = 103125

BINS = (NODES + P - 1) // P
LAST = NODES - (BINS - 1) * P
K = 2
GE = K * P
U = 6
GROUPS = (EDGES_ALL // GE + BINS + U - 1) // U * U
TURNS = GROUPS // U
COLS = (EDGES_ALL + P - 1) // P
FULL = EDGES_ALL // COLS
REST = EDGES_ALL - FULL * COLS
ROWS = P * COLS + 2 * GE
W = 16
SPLIT = 3 * BASIS
PAD_DST = BINS * P
SUP = 4
SUPS = (BINS + SUP - 1) // SUP
NT = SUP * SUPS
SC = 13
SCT = COLS // SC
ND = D + RELS
YW = RELS * D
YN = YW + 2 * D
YU = 1024
NYU = YW // YU
FIVE = 5

ALU = mybir.AluOpType
ACT = mybir.ActivationFunctionType
AX = mybir.AxisListType
F32 = mybir.dt.float32
BF16 = mybir.dt.bfloat16
I32 = mybir.dt.int32
U32 = mybir.dt.uint32


def steps(eng, lead, step, peel=1):
    for i in range(peel * U):
        step(i, i % U, i // U)
    with eng.Fori(peel, TURNS) as t:
        for u in range(U):
            step(t * U + u, u, t)
    for i in range(GROUPS, GROUPS + lead):
        step(i, i % U, i // U)


def turns(eng, n, turn):
    turn(0)
    with eng.Fori(1, n) as j:
        turn(j)


def live(i, lag):
    return not isinstance(i, int) or 0 <= i - lag < GROUPS


def wait(eng, sem, value):
    if not isinstance(value, int) or value > 0:
        eng.wait_ge(sem, value)


def held_wait(eng, sem, value, tick):
    if not isinstance(value, int) or value > 0:
        eng.wait_ge(sem, value)
        eng.sem_inc(tick, 1)


def uses(l, t, u, lag=0):
    return t + (l * TURNS + (1 if u >= lag else 0))


def build(nc, x, src, dst, basis, etype, pp_W1, pp_b1, pp_W2, pp_b2, pi_W1, pi_b1, pi_W2, pi_b2,
          pi_W3, ii_W1, ii_b1, ii_W2, ii_b2, r_W, r_root, r_bias, r_res_W, r_res_b, out, stop=9):
    rec_d = nc.dram_tensor("rec_d", (ROWS, W), F32, kind="Internal").ap()
    p_d = nc.dram_tensor("p_d", (NT * P, D), F32, kind="Internal").ap()
    y_d = nc.dram_tensor("y_d", (BINS * P * RELS, D), F32, kind="Internal").ap()
    y_rows = y_d.rearrange("(n r) d -> n (r d)", r=RELS)

    with ExitStack() as ctx:
        def sb(name, shape, dt):
            return ctx.enter_context(nc.sbuf_tensor(name, shape, dt))

        def sem(name):
            return ctx.enter_context(nc.semaphore(name))

        region_a = sb("region_a", [P, COLS * W], F32)
        rec_a = region_a[:, 0:COLS * W].rearrange("p (n w) -> p n w", w=W)
        w_all = region_a[:, 0:YN]
        w_parts = region_a[:, YN:YN + 3 * YN // 2].bitcast(BF16).rearrange("p (s n) -> p s n", s=3)
        region_c = sb("region_c", [P, 9800], F32)
        basis_in = region_c[:, 0:COLS * BASIS].rearrange("p (n b) -> p n b", b=BASIS)
        dst_in = region_c[:, COLS * BASIS:COLS * (BASIS + 1)].bitcast(I32)
        src_in = region_c[:, COLS * (BASIS + 1):COLS * (BASIS + 2)].bitcast(I32)
        typ_in = region_c[:, COLS * (BASIS + 2):COLS * (BASIS + 3)].bitcast(I32)
        y_stage = region_c[:, 0:NYU * YU + D]
        region_r = sb("region_r", [P, 4 * COLS], F32)
        spot = [0]

        def part_of_c(width):
            spot[0] += width
            return region_c[:, spot[0] - width:spot[0]]
        vT = part_of_c(8 * K * P).rearrange("p (s c n) -> p s c n", s=2, c=4)
        uT = part_of_c(2 * K * P).rearrange("p (s n) -> p s n", s=2)
        u_sb = part_of_c(4 * K * D).rearrange("p (s k o d) -> p s k o d", s=2, k=K, o=2)
        ohT_b = part_of_c(K * P).bitcast(BF16).rearrange("p (s n) -> p s n", s=2)
        bT = part_of_c(K * P).bitcast(BF16).rearrange("p (s n) -> p s n", s=2)
        spot[0] = NYU * YU + D
        hT, tT, p1T, aT, qT = [part_of_c(SUP * P)[0:D, :] for _ in range(5)]
        p_st = part_of_c(SUP * D).rearrange("p (t d) -> p t d", t=SUP)
        q_st = part_of_c(2 * SUP * D).rearrange("p (s t d) -> p s t d", s=2, t=SUP)
        spot[0] = NYU * YU + D
        h_parts = part_of_c(BINS * 3 * D // 2).bitcast(BF16).rearrange("p (a n) -> p a n", a=BINS)
        hh_st = part_of_c(3 * D).bitcast(BF16).rearrange("p (q n) -> p q n", q=2)
        hhT = part_of_c(2 * P).bitcast(BF16).rearrange("p (q s n) -> p q s n", q=2, s=2)
        s_st = part_of_c(FIVE * (D + 1)).rearrange("p (t d) -> p t d", t=FIVE)
        sT = part_of_c(FIVE * P)[0:D + 1, :]
        bin_of = region_r[:, 0:COLS]
        bin_int = region_r[:, COLS:2 * COLS].bitcast(I32)
        junk = region_r[:, 2 * COLS:3 * COLS]
        place = region_r[:, 3 * COLS:4 * COLS]
        place_i = bin_int
        rr = region_r[:, 0:BINS * 2 * D].rearrange("p (a n) -> p a n", a=BINS)
        next_int = sb("next_int", [P, 1], I32)
        next_bin = sb("next_bin", [P, 1], F32)
        count_pa = sb("count_pa", [P, BINS + 1], F32)
        pad_rec = sb("pad_rec", [P, (ROWS - P * COLS) // P * W], F32)

        ident = sb("ident", [P, P], F32)
        ident_b = sb("ident_b", [P, P], BF16)
        ones = sb("ones", [P, P], F32)
        before = sb("before", [P, P], F32)
        upto = sb("upto", [P, P], F32)
        iota_p = sb("iota_p", [P, P], F32)
        iota_g = sb("iota_g", [P, GROUPS], F32)
        zero_c = sb("zero_c", [P, BINS + 1], F32)
        small = sb("small", [P, 16], F32)
        small_i = sb("small_i", [P, 4], I32)
        mask_ag = sb("mask_ag", [BINS, GROUPS], F32)
        gap_b = sb("gap_b", [BINS, P], F32)
        bin_g = sb("bin_g", [P, GROUPS], F32)
        base_neg = sb("base_neg", [P, GROUPS], F32)
        bin_gi = sb("bin_gi", [P, GROUPS], I32)
        start_g = sb("start_g", [P, GROUPS], F32)
        start_gi = sb("start_gi", [P, GROUPS], I32)
        offset_pa = sb("offset_pa", [P, BINS + 1], F32)
        total_pa = sb("total_pa", [P, BINS + 1], F32)
        flag_i = sb("flag_i", [P, 1], I32)
        place_s = sb("place_s", [P, SC], U32)
        rec_s = sb("rec_s", [P, SC * W], F32)

        x_sb = sb("x_sb", [P, NT, D], F32)
        h_sb = sb("h_sb", [P, NT, D], F32)
        ln_s = sb("ln_s", [P, 3, NT], F32)
        sq = sb("sq", [P, NT, D], F32)
        q_parts = sb("q_parts", [P, NT, 3, D], BF16)
        acc = sb("acc", [P, BINS + 1, ND], F32)
        loc = sb("loc", [P, GROUPS * K], F32)
        typ = sb("typ", [P, GROUPS * K], F32)
        w_edge = sb("w_edge", [P, GROUPS * K], F32)

        w1 = sb("w1", [D, D], F32)
        w2 = sb("w2", [D, D], F32)
        wa = sb("wa", [D, 2, D], F32)
        wi2 = sb("wi2", [D, D], F32)
        w3 = sb("w3", [D, D, BASIS], F32)
        w3t = sb("w3t", [D, BASIS * D], F32)
        wii1 = sb("wii1", [D, D], F32)
        wz = sb("wz", [P, BASIS // 2, D], F32)
        wii2 = sb("wii2", [D + 1, D], F32)
        b1c = sb("b1c", [D, 1], F32)
        b2c = sb("b2c", [D, 1], F32)
        pib1c = sb("pib1c", [D, 1], F32)
        pib2r = sb("pib2r", [P, D], F32)
        iib1c = sb("iib1c", [P, 1], F32)
        ident2 = sb("ident2", [P, D], F32)
        zT = sb("zT", [P, K * P], F32)
        brr = sb("brr", [P, 2, 2 * D], F32)
        sel_f = sb("sel_f", [P, 4 * P], F32)
        sel_t = h_sb[:, 0:NT - 4, :].rearrange("k t d -> k (t d)").rearrange("k (t m) -> k t m", t=3)
        sel = sb("sel", [P, 4, P], BF16)

        h_st = sb("h_st", [P, SUP * D], F32)

        rec_u = sb("rec_u", [P, U, K * W], F32)
        gat = sb("gat", [P, U, K, D], F32)
        oh = sb("oh", [P, U, K, P], F32)
        oh_b = sb("oh_b", [P, U, K, P], BF16)
        rel_b = sb("rel_b", [P, 2, K, RELS], BF16)
        ohT_f = sb("ohT_f", [P, 2, K * P], F32)
        tr = sb("tr", [P, 2, K, D], F32)
        pick = sb("pick", [P, 2, RELS], F32)

        ps = ctx.enter_context(nc.psum_tensor("ps", [P, 8, 512], F32))
        ps_flat = ps[:, :, :].rearrange("p b n -> p (b n)")
        bb = ps_flat[:, 0:4 * 512].rearrange("p (s c n) -> p s c n", s=2, c=4)
        ps_t, ps_b = ps[:, 4, 0:K * D].bitcast(BF16), ps[:, 4, K * P:K * P + K * D].bitcast(BF16)
        ps_u = ps[:, 5, 0:K * P]
        ps_zT, ps_z = ps[:, 6, 0:K * P], ps[:, 6, K * P:K * P + K * D]
        ps_s, ps_q = ps[:, 7, 0:ND], ps[:, 7, 256:256 + K * D]
        ps_t2 = [ps[:, 4 + q, 0:K * P] for q in range(2)]
        ps_s2 = [ps[:, 6 + q, 0:D] for q in range(2)]
        ps_hT = [ps[:, 7, q * P:(q + 1) * P].bitcast(BF16).rearrange("p (s n) -> p s n", s=2) for q in range(2)]
        ps_w = [ps[:, q, 0:K * RELS].rearrange("p (k r) -> p k r", k=K) for q in range(2)]

        edges_in = sem("edges_in")
        basis_in_s = sem("basis_in_s")
        x_in = sem("x_in")
        w_in = sem("w_in")
        const = sem("const")
        dve_c = sem("dve_c")
        pe_c = sem("pe_c")
        act_c = sem("act_c")
        pool_c = sem("pool_c")
        counted = sem("counted")
        totals = sem("totals")
        in_groups = sem("in_groups")
        cumulated = sem("cumulated")
        masks = sem("masks")
        spread = sem("spread")
        tables = sem("tables")
        flag = sem("flag")
        placed = sem("placed")
        rec_made = sem("rec_made")
        pad_out = sem("pad_out")
        rec_out = sem("rec_out")
        rec_ready = sem("rec_ready")
        scat = sem("scat")
        scat_in = sem("scat_in")
        w_split = [sem(f"w_split{l}") for l in range(2)]
        w3_t = sem("w3_t")
        w3_c = sem("w3_c")
        wz_p = sem("wz_p")
        wz_c = sem("wz_c")
        var_ready = sem("var_ready")
        std_ready = sem("std_ready")
        h_ready = sem("h_ready")
        n_hs = sem("n_hs")
        n_hp = sem("n_hp")
        n_hT = sem("n_hT")
        n_tp = sem("n_tp")
        n_tT = sem("n_tT")
        n_pp = sem("n_pp")
        n_pT = sem("n_pT")
        n_ap = sem("n_ap")
        n_aT = sem("n_aT")
        n_qT = sem("n_qT")
        n_PQ = sem("n_PQ")
        n_Ps = sem("n_Ps")
        n_Q = sem("n_Q")
        n_Pout = sem("n_Pout")
        loc_ready = sem("loc_ready")
        tick = sem("tick")
        placed_c = sem("placed_c")

        ctx.enter_context(nc.allow_non_contiguous_dma(reason='a few columns of single words'))
        block = ctx.enter_context(nc.Block())

        def gsems(tag, slots):
            return [sem(f"{tag}{u}") for u in range(slots)]

        rec_slot = gsems("rec_slot", U)
        gathered = gsems("gathered", U)
        names = (("oh", "ohT", "ohTc", "bTc", "q", "bb", "u", "uT", "uTc", "v", "zT", "zTc", "z", "t", "rel", "s", "acc",
                  "ohb", "loc"),
                 ("oh", "ohT", "ohTc", "wt", "w", "scaled", "s", "acc"),
                 ("oh", "s", "acc"))
        L = [{n: sem(f"l{l}_{n}") for n in names[l]} for l in range(3)]
        nd = {n: sem(f"nd_{n}") for n in ("st", "tp", "tT", "o", "x", "h")}
        Y = [{n: sem(f"y{l}_{n}") for n in ("w", "hp", "st", "tp", "hT", "mm0", "mm1", "mm2", "mm3", "mm4",
                                           "ev0", "ev1", "ev2", "ev3", "ev4", "o0", "o1", "o2", "o3", "h")}
             for l in range(2)]
        final = sem("final")
        out_s = sem("out_s")

        STT = nc.vector.scalar_tensor_tensor
        TT = nc.vector.tensor_tensor
        TS = nc.vector.tensor_scalar

        def cols(ap, row_first, n):
            return ap[row_first * COLS:row_first * COLS + n]

        @block.sync
        def _(sp):
            def edge_array(ap_sb, ap_d, s):
                sp.dma_start(ap_sb[0:FULL, :], ap_d[0:FULL * COLS].rearrange("(p n) -> p n", n=COLS)).then_inc(s, 16)
                sp.dma_start(ap_sb[FULL:FULL + 1, 0:REST],
                             ap_d[FULL * COLS:EDGES_ALL].rearrange("(p n) -> p n", p=1)).then_inc(s, 16)

            sp.wait_ge(const, 1)
            edge_array(dst_in, dst, edges_in)
            sp.dma_start(next_int[0:FULL, :],
                         dst[COLS:EDGES_ALL].rearrange("(n o) -> n o", o=1)[0:(FULL - 1) * COLS + 1:COLS, :]
                         ).then_inc(edges_in, 16)
            edge_array(src_in, src, edges_in)
            edge_array(typ_in, etype, edges_in)
            sp.dma_start(basis_in[0:FULL, :, :],
                         basis[0:FULL * COLS, :].rearrange("(p n) b -> p n b", n=COLS)).then_inc(basis_in_s, 16)
            sp.dma_start(basis_in[FULL:FULL + 1, 0:REST, :],
                         basis[FULL * COLS:EDGES_ALL, :].rearrange("(p n) b -> p n b", p=1)).then_inc(basis_in_s, 16)
            sp.dma_start(x_sb[:, 0:BINS - 1, :],
                         x[0:(BINS - 1) * P, :].rearrange("(a p) d -> p a d", p=P)).then_inc(x_in, 16)
            sp.dma_start(x_sb[0:LAST, BINS - 1, :], x[(BINS - 1) * P:NODES, :]).then_inc(x_in, 16)
            loads = [
                (w1[:, :], pp_W1), (w2[:, :], pp_W2), (wi2[:, :], pi_W2), (wii1[:, :], ii_W1),
                (wa[:, 0, :], pi_W1[0:D, :]), (wa[:, 1, :], pi_W1[D:2 * D, :]),
                (w3[:, :, :], pi_W3.rearrange("d (c b) -> d c b", b=BASIS)),
                (wii2[0:D, :], ii_W2), (wii2[D:D + 1, :], ii_b2.rearrange("(o d) -> o d", o=1)),
                (b1c[:, :], pp_b1.rearrange("(d o) -> d o", o=1)), (b2c[:, :], pp_b2.rearrange("(d o) -> d o", o=1)),
                (pib1c[:, :], pi_b1.rearrange("(d o) -> d o", o=1)),
                (pib2r[:, :], pi_b2.rearrange("(o d) -> o d", o=1).broadcast_to([P, D])),
                (iib1c[0:D, :], ii_b1.rearrange("(d o) -> d o", o=1)),
            ]
            for l in range(2):
                loads.append((brr[:, l, 0:D], r_bias[l:l + 1, :].broadcast_to([P, D])))
                loads.append((brr[:, l, D:2 * D], r_res_b[l:l + 1, :].broadcast_to([P, D])))
            for a, b in loads:
                sp.dma_start(a, b).then_inc(w_in, 16)
            def turn(j):
                held_wait(sp, n_Ps, j + 1, tick)
                sp.dma_start(p_d[bass.ds(j * (SUP * P), SUP * P), :].rearrange("(t p) d -> p t d", p=P),
                             p_st[:, :, :]).then_inc(n_Pout, 16)
            turns(sp, SUPS, turn)
            sp.wait_ge(tables, 1)
            sp.wait_ge(rec_ready, 1)

            def load_w(l):
                for half in range(2):
                    w = w_all[half * D:(half + 1) * D, :]
                    sp.dma_start(w[:, 0:YW].rearrange("d (r k) -> d r k", k=D),
                                 r_W[l].rearrange("r d k -> d r k")).then_inc(Y[l]["w"], 16)
                    sp.dma_start(w[:, YW:YW + D], r_root[l]).then_inc(Y[l]["w"], 16)
                    sp.dma_start(w[:, YW + D:YN], r_res_W[l]).then_inc(Y[l]["w"], 16)

            def slots(l):
                def step(j, u, t):
                    first = sp.value_load(start_gi[0:1, bass.ds(j, 1)], min_val=0, max_val=EDGES_ALL)
                    held_wait(sp, gathered[u], (uses(l, t, u) - 1) * (16 * K), tick)
                    if l == 0:
                        held_wait(sp, L[0]["ohT"], j - U + 1, tick)
                        held_wait(sp, L[0]["loc"], 2 * (j - U + 1), tick)
                    sp.dma_start(rec_u[:, u, :],
                                 rec_d[bass.ds(first, GE), :].rearrange("(p k) w -> p (k w)", k=K)
                                 ).then_inc(rec_slot[u], 16)
                steps(sp, 0, step)

            load_w(0)
            slots(0)
            if stop >= 2:
                for l in range(2):
                    y = Y[l]
                    if l == 1:
                        sp.wait_ge(L[1]["acc"], GROUPS)

                    def store(a):
                        for c in range(NYU):
                            n = YU + (D if c == NYU - 1 else 0)
                            held_wait(sp, y[f"ev{c}"], a + 1, tick)
                            if c == NYU - 1:
                                held_wait(sp, y["ev4"], a + 1, tick)
                            sp.dma_start(y_rows[bass.ds(a * P, P), c * YU:c * YU + n],
                                         y_stage[:, c * YU:c * YU + n]).then_inc(y[f"o{c}"], 16)
                    def turn(a):
                        store(a)
                    turns(sp, BINS, turn)
                    if l == 0:
                        sp.wait_ge(Y[0]["mm4"], BINS)
                        load_w(1)
                    slots(l + 1)
            sp.wait_ge(final, 1)
            sp.dma_start(out[0:(BINS - 1) * P, :].rearrange("(a p) d -> p a d", p=P),
                         h_sb[:, 0:BINS - 1, :]).then_inc(out_s, 16)
            sp.dma_start(out[(BINS - 1) * P:NODES, :], h_sb[0:LAST, BINS - 1, :]).then_inc(out_s, 16)
            sp.wait_ge(out_s, 32)
            sp.wait_ge(n_Pout, 16 * SUPS)

        @block.gpsimd
        def _(pool):
            nc.gpsimd.memset(ones[:, :], 1.0).then_inc(pool_c, 1)
            nc.gpsimd.iota(iota_p[:, :], [[1, P]], base=0, channel_multiplier=0,
                           allow_small_or_imprecise_dtypes=True).then_inc(pool_c, 1)
            nc.gpsimd.iota(iota_g[:, :], [[1, GROUPS]], base=0, channel_multiplier=0,
                           allow_small_or_imprecise_dtypes=True).then_inc(pool_c, 1)
            nc.gpsimd.iota(sel_f[:, :], [[-1, BASIS], [0, D]], base=0, channel_multiplier=1,
                           allow_small_or_imprecise_dtypes=True).then_inc(pool_c, 1)
            pool.wait_ge(pool_c, 1)
            nc.gpsimd.affine_select(out=ident[:, :], in_=ones[:, :], compare_op=ALU.is_equal, fill=0.0, base=0,
                                    pattern=[[-1, P]], channel_multiplier=1).then_inc(pool_c, 1)
            nc.gpsimd.affine_select(out=before[:, :], in_=ones[:, :], compare_op=ALU.is_gt, fill=0.0, base=0,
                                    pattern=[[1, P]], channel_multiplier=-1).then_inc(pool_c, 1)
            nc.gpsimd.affine_select(out=upto[:, :], in_=ones[:, :], compare_op=ALU.is_ge, fill=0.0, base=0,
                                    pattern=[[1, P]], channel_multiplier=-1).then_inc(pool_c, 1)

            pool.wait_ge(rec_made, 1)
            pool.dma_start(rec_d[P * COLS:ROWS, :].rearrange("(p n) w -> p (n w)", p=P),
                           pad_rec[:, :]).then_inc(pad_out, 16)
            pool.wait_ge(flag, 1)
            unsorted = pool.value_load(flag_i[0:1, 0:1], min_val=0, max_val=EDGES_ALL)
            with pool.If(unsorted < 1):
                pool.dma_start(rec_d[0:P * COLS, :].rearrange("(p n) w -> p (n w)", p=P),
                               region_a[:, 0:COLS * W]).then_inc(rec_out, 16)
                pool.wait_ge(rec_out, 16)
            with pool.Else():
                pool.wait_ge(placed, 1)
                def turn(n):
                    pool.dma_start(rec_s[:, :], region_a[:, bass.ds(n * (SC * W), SC * W)]).then_inc(scat_in, 16)
                    pool.dma_start(place_s[:, :], place_i[:, bass.ds(n * SC, SC)].bitcast(U32)).then_inc(scat_in, 16)
                    pool.wait_ge(scat_in, 32 * (n + 1))
                    pool.sem_inc(tick, 1)
                    for c in range(SC):
                        nc.gpsimd.indirect_dma_start(
                            rec_d[0:P * COLS, :], bass.IndirectOffsetOnAxis(ap=place_s[:, c:c + 1], axis=0),
                            rec_s[:, c * W:(c + 1) * W], None).then_inc(scat, 16)
                    pool.wait_ge(scat, 16 * SC * (n + 1))
                    pool.sem_inc(tick, 1)
                turns(pool, SCT, turn)
            pool.end_ifs()
            pool.wait_ge(pad_out, 16)
            pool.sem_inc(rec_ready, 1)

            def gathers(l):
                s = L[l]
                used = s[("u", "scaled", "s")[l]]

                def step(j, u, t):
                    wait(pool, rec_slot[u], uses(l, t, u) * 16)
                    wait(pool, used, j - U + 1)
                    pool.sem_inc(tick, 1)
                    for k in range(K):
                        word = k * W + (0 if l == 0 else 1)
                        nc.gpsimd.indirect_dma_start(
                            gat[:, u, k, :], None, p_d[0:NODES, :] if l == 0 else y_d[:, :],
                            bass.IndirectOffsetOnAxis(ap=rec_u[:, u, word:word + 1].bitcast(U32), axis=0)
                        ).then_inc(gathered[u], 16)
                steps(pool, 0, step)

            pool.wait_ge(n_Pout, 16 * SUPS)
            gathers(0)
            if stop >= 2:
                for l in range(2):
                    for c in range(NYU):
                        pool.wait_ge(Y[l][f"o{c}"], 16 * BINS)
                    gathers(l + 1)

        @block.scalar
        def _(act):
            A = nc.scalar.activation
            act.wait_ge(w3_t, 1)
            A(w3t[:, :], ps[0:D, 3, :], ACT.Copy).then_inc(w3_c, 1)
            act.wait_ge(wz_p, 1)
            A(wz[:, :, :], ps[:, 2, 0:4 * D].rearrange("p (c d) -> p c d", c=4), ACT.Copy).then_inc(wz_c, 1)
            act.wait_ge(var_ready, 1)
            A(ln_s[:, 2, :], ln_s[:, 1, :], ACT.Sqrt).then_inc(std_ready, 1)
            def turn(j):
                act.wait_ge(n_tp, j + 1)
                A(tT[:, :], ps[0:D, 1, :], ACT.Tanh, bias=b1c[:, 0:1]).then_inc(n_tT, 1)
                act.wait_ge(n_pp, j + 1)
                A(p1T[:, :], ps[0:D, 2, :], ACT.Identity, bias=b2c[:, 0:1]).then_inc(n_pT, 1)
                act.wait_ge(n_ap, j + 1)
                A(aT[:, :], ps[0:D, 3, :], ACT.Copy).then_inc(n_aT, 1)
                act.wait_ge(n_PQ, j + 1)
                wait(act, n_Pout, 16 * j)
                A(p_st[:, :, :], ps[:, 5, 0:SUP * D].rearrange("p (t d) -> p t d", t=SUP), ACT.Copy).then_inc(n_Ps, 1)
            turns(act, SUPS, turn)
            def split_w(l):
                act.wait_ge(Y[l]["w"], 96)
                A(w_parts[:, 0, :], w_all, ACT.Copy).then_inc(w_split[l], 1)
                act.wait_ge(w_split[l], 2)
                A(w_parts[:, 1, :], w_all, ACT.Copy).then_inc(w_split[l], 1)
                act.wait_ge(w_split[l], 4)
                A(w_parts[0:D, 2, :], w_all[0:D, :], ACT.Copy).then_inc(w_split[l], 1)
                A(w_parts[D:P, 2, :], w_parts[D:P, 0, :], ACT.Copy).then_inc(w_split[l], 1)
            split_w(0)
            s = L[0]

            def step(i, u, t):
                if live(i, 3):
                    a = (u + 1) % 2
                    wait(act, s["v"], i - 4)
                    wait(act, s["uT"], i - 2)
                    A(uT[:, a, :], ps_u, ACT.Copy).then_inc(s["uTc"], 1)
                if live(i, 0):
                    wait(act, rec_slot[u], uses(0, t, u) * 16)
                    words = rec_u[:, u, :].rearrange("p (k w) -> p k w", w=W)
                    A(loc[:, bass.ds(i * K, K)], words[:, :, 2], ACT.Identity,
                      bias=base_neg[:, bass.ds(i, 1)]).then_inc(s["loc"], 1)
                    A(typ[:, bass.ds(i * K, K)], words[:, :, 3], ACT.Copy).then_inc(s["loc"], 1)
                if live(i, 1):
                    v = (u - 1) % U
                    wait(act, s["s"], i - U)
                    wait(act, s["oh"], i)
                    A(oh_b[:, v, :, :], oh[:, v, :, :], ACT.Copy).then_inc(s["ohb"], 1)
                if live(i, 4):
                    wait(act, s["z"], i - 4)
                    wait(act, s["zT"], i - 3)
                    A(zT[:, :], ps_zT, ACT.Identity, bias=iib1c[:, 0:1]).then_inc(s["zTc"], 1)
                if live(i, 1):
                    a = (u + 1) % 2
                    wait(act, s["q"], i - 2)
                    wait(act, s["ohT"], i)
                    A(ohT_b[:, a, :], ps_t, ACT.Copy).then_inc(s["ohTc"], 1)
                    wait(act, s["bb"], i - 2)
                    A(bT[0:SPLIT, a, :], ps_b[0:SPLIT, :], ACT.Copy).then_inc(s["bTc"], 1)
                if live(i, 4):
                    wait(act, s["s"], i - 5)
                    wait(act, s["z"], i - 3)
                    A(tr[:, u % 2, :, :], ps_z.rearrange("p (k d) -> p k d", k=K),
                      ACT.Tanh).then_inc(s["t"], 1)
            steps(act, 4, step, peel=2)

            if stop >= 1:
                act.wait_ge(var_ready, 2)
                A(ln_s[:, 2, :], ln_s[:, 1, :], ACT.Sqrt).then_inc(std_ready, 1)
            if stop >= 2:
                for l in range(2):
                    y = Y[l]

                    def turn_y(a, q, ahead):
                        if ahead:
                            act.wait_ge(y["tp"], a + 2)
                            A(hhT[:, 1 - q, :, :], ps_hT[1 - q], ACT.Copy).then_inc(y["hT"], 1)
                        for c in (0, 2):
                            act.wait_ge(y[f"mm{c}"], a + 1)
                            wait(act, y[f"o{c}"], 16 * a)
                            A(y_stage[:, c * YU:(c + 1) * YU], ps_flat[:, c * YU:(c + 1) * YU],
                              ACT.Copy).then_inc(y[f"ev{c}"], 1)
                    act.wait_ge(y["tp"], 1)
                    A(hhT[:, 0, :, :], ps_hT[0], ACT.Copy).then_inc(y["hT"], 1)
                    def turn(pair):
                        turn_y(pair * 2, 0, True)
                        turn_y(pair * 2 + 1, 1, True)
                    turns(act, BINS // 2, turn)
                    turn_y(BINS - 1, 0, False)

                    if l == 0:
                        split_w(1)
                        s = L[1]

                        def step1(i, u, t):
                            if live(i, 0):
                                wait(act, s["wt"], i - 1)
                                wait(act, s["ohT"], i + 1)
                                A(ohT_f[:, u % 2, :], ps_t2[u % 2], ACT.Copy).then_inc(s["ohTc"], 1)
                        steps(act, 0, step1)

        @block.vector
        def _(dve):
            n = [0]

            def link(ins):
                n[0] += 1
                ins.then_inc(dve_c, 1)
                dve.wait_ge(dve_c, n[0])

            lo = FULL // 32 * 32
            nc.vector.memset(basis_in[lo:P, REST:COLS, :], 0.0)
            nc.vector.memset(dst_in[lo:P, REST:COLS], PAD_DST)
            nc.vector.memset(src_in[lo:P, REST:COLS], 0)
            nc.vector.memset(typ_in[lo:P, REST:COLS], 0)
            nc.vector.memset(next_int[:, :], PAD_DST)
            link(nc.vector.memset(x_sb[:, :, :], 0.0))
            link(nc.vector.memset(pad_rec[:, :], 0.0))
            dve.sem_inc(const, 1)
            link(nc.vector.memset(pad_rec[:, :].rearrange("p (n w) -> p n w", w=W)[:, :, 2], float(PAD_DST)))
            nc.vector.memset(acc[:, :, :], 0.0)
            nc.vector.memset(zero_c[:, :], 0.0)
            nc.vector.memset(iib1c[D:P, :], 0.0)
            dve.wait_ge(pool_c, 7)
            for t in range(3):
                nc.vector.tensor_scalar(sel_t[:, t, :], sel_f[:, :], float(BASIS * t), None, ALU.is_equal
                                        ).then_inc(dve_c, 1)
                n[0] += 1
            nc.vector.tensor_copy(ident_b[:, :], ident[:, :]).then_inc(dve_c, 1)
            n[0] += 1
            dve.wait_ge(dve_c, n[0])
            link(TT(sel_t[:, 0, :], sel_t[:, 0, :], sel_t[:, 1, :], ALU.add))
            link(TT(ident2[:, :], ident[:, 0:D], ident[:, D:P], ALU.add))
            link(TT(sel[:, :, :].rearrange("k c m -> k (c m)"), sel_t[:, 0, :], sel_t[:, 2, :], ALU.add))

            dve.wait_ge(edges_in, 16 * 7)
            nc.vector.tensor_single_scalar(next_int[:, :], next_int[:, :], 7, ALU.arith_shift_right).then_inc(dve_c, 1)
            n[0] += 1
            link(nc.vector.tensor_single_scalar(bin_int[:, :], dst_in, 7, ALU.arith_shift_right))
            nc.vector.tensor_copy(next_bin[:, :], next_int[:, :]).then_inc(dve_c, 1)
            n[0] += 1
            link(nc.vector.tensor_copy(bin_of[:, :], bin_int[:, :]))
            for a in range(BINS + 1):
                link(TS(junk[:, :], bin_of[:, :], float(a), 0.0, ALU.is_equal, ALU.add,
                        accum_out=count_pa[:, a:a + 1]))
            link(TT(junk[:, 0:COLS - 1], bin_of[:, 0:COLS - 1], bin_of[:, 1:COLS], ALU.is_gt))
            link(TT(junk[:, COLS - 1:COLS], bin_of[:, COLS - 1:COLS], next_bin[:, :], ALU.is_gt))
            link(nc.vector.tensor_reduce(small[:, 0:1], junk[:, :], AX.X, ALU.add))
            dve.sem_inc(counted, 1)
            dve.wait_ge(totals, 1)
            link(nc.vector.tensor_copy(small[:, 1:2], ps[:, 6, 0:1]))
            link(nc.vector.tensor_copy(small[0:BINS + 1, 2:3], ps[0:BINS + 1, 6, 1:2]))
            link(TS(small[0:BINS, 3:4], small[0:BINS, 2:3], float(GE - 1), None, ALU.add))
            link(nc.vector.tensor_copy(small_i[0:BINS, 0:1], small[0:BINS, 3:4]))
            link(nc.vector.tensor_single_scalar(small_i[0:BINS, 1:2], small_i[0:BINS, 0:1], GE.bit_length() - 1,
                                                ALU.arith_shift_right))
            nc.vector.tensor_copy(flag_i[:, :], small[:, 1:2]).then_inc(dve_c, 1)
            n[0] += 1
            link(nc.vector.tensor_copy(small[0:BINS, 4:5], small_i[0:BINS, 1:2]))
            dve.sem_inc(flag, 1)
            dve.sem_inc(in_groups, 1)
            link(STT(out=small[0:BINS, 5:6], in0=small[0:BINS, 4:5], scalar=-float(GE),
                     in1=small[0:BINS, 2:3], op0=ALU.mult, op1=ALU.add))
            link(nc.vector.tensor_copy(gap_b[:, :], small[0:BINS, 5:6].broadcast_to([BINS, P])))
            dve.wait_ge(cumulated, 1)
            link(nc.vector.tensor_copy(small[0:BINS, 6:7], ps[0:BINS, 6, 2:3]))
            link(TS(mask_ag[:, :], iota_g[0:BINS, :], small[0:BINS, 6:7], None, ALU.is_ge))
            dve.sem_inc(masks, 1)
            dve.wait_ge(spread, 1)
            link(nc.vector.tensor_copy(bin_g[:, :], ps[:, 4, 0:GROUPS]))
            link(STT(out=start_g[:, :], in0=iota_g[:, :], scalar=float(GE), in1=ps[:, 5, 0:GROUPS],
                     op0=ALU.mult, op1=ALU.add))
            link(TS(start_g[:, :], start_g[:, :], float(EDGES_ALL), None, ALU.min))
            link(nc.vector.tensor_copy(start_gi[:, :], start_g[:, :]))
            link(nc.vector.tensor_copy(bin_gi[:, :], bin_g[:, :]))
            link(TS(base_neg[:, :], bin_g[:, :], -float(P), None, ALU.mult))
            dve.sem_inc(tables, 1)

            link(nc.vector.tensor_copy(rec_a[:, :, 0].bitcast(I32), src_in))
            link(STT(out=rec_a[:, :, 1].bitcast(I32), in0=src_in, scalar=float(RELS), in1=typ_in,
                     op0=ALU.mult, op1=ALU.add))
            link(nc.vector.tensor_copy(rec_a[:, :, 2], dst_in))
            link(nc.vector.tensor_copy(rec_a[:, :, 3], typ_in))
            dve.wait_ge(basis_in_s, 32)
            part = [region_a[:, 0:COLS * W].bitcast(BF16).rearrange("p (n w) -> p n w", w=2 * W)
                    [:, :, 8 + BASIS * t:8 + BASIS * (t + 1)] for t in range(3)]
            link(nc.vector.tensor_copy(part[0], basis_in))
            link(TT(basis_in, basis_in, part[0], ALU.subtract))
            link(nc.vector.tensor_copy(part[1], basis_in))
            link(TT(part[2], basis_in, part[1], ALU.subtract))
            dve.sem_inc(rec_made, 1)

            out_of_order = dve.value_load(flag_i[0:1, 0:1], min_val=0, max_val=EDGES_ALL)
            with dve.If(out_of_order > 0):
                m = [0]

                def slow(ins):
                    m[0] += 1
                    ins.then_inc(placed_c, 1)
                    dve.wait_ge(placed_c, m[0])
                slow(nc.vector.tensor_copy(total_pa[:, :], ps[:, 6, 64:64 + BINS + 1]))
                slow(nc.vector.tensor_tensor_scan(offset_pa[:, :], total_pa[:, :], zero_c[:, :], 0.0, ALU.add, ALU.add))
                slow(TT(offset_pa[:, :], offset_pa[:, :], total_pa[:, :], ALU.subtract))
                slow(TT(offset_pa[:, :], offset_pa[:, :], ps[:, 6, 128:128 + BINS + 1], ALU.add))
                slow(nc.vector.memset(place[:, :], -1.0))
                same, ranks = basis_in.rearrange("p n b -> p (n b)")[:, 0:COLS], \
                    basis_in.rearrange("p n b -> p (n b)")[:, COLS:2 * COLS]
                slow(nc.vector.memset(junk[:, :], 0.0))
                for a in range(BINS + 1):
                    slow(TS(same, bin_of[:, :], float(a), None, ALU.is_equal))
                    slow(nc.vector.tensor_tensor_scan(ranks, same, junk[:, :], 0.0, ALU.add, ALU.add))
                    slow(STT(out=ranks, in0=ranks, scalar=offset_pa[:, a:a + 1], in1=same, op0=ALU.add, op1=ALU.mult))
                    slow(TT(place[:, :], place[:, :], ranks, ALU.add))
                slow(nc.vector.tensor_copy(place_i[:, :], place[:, :]))
                dve.sem_inc(placed, 1)
            dve.end_ifs()
            link(nc.vector.memset(bT[:, :, :], 0.0))

            def layernorm(tiles, k):
                xs, hs, qs = x_sb[:, 0:tiles, :], h_sb[:, 0:tiles, :], sq[:, 0:tiles, :]

                def bc(i):
                    return ln_s[:, i, 0:tiles].rearrange("p (t o) -> p t o", o=1).broadcast_to([P, tiles, D])
                link(nc.vector.tensor_reduce(ln_s[:, 0, 0:tiles], xs, AX.X, ALU.add))
                link(TS(ln_s[:, 0, 0:tiles], ln_s[:, 0, 0:tiles], 1.0 / D, None, ALU.mult))
                link(TT(hs, xs, bc(0), ALU.subtract))
                link(TT(qs, hs, hs, ALU.mult))
                link(nc.vector.tensor_reduce(ln_s[:, 1, 0:tiles], qs, AX.X, ALU.add))
                link(TS(ln_s[:, 1, 0:tiles], ln_s[:, 1, 0:tiles], 1.0 / D, 1e-5, ALU.mult, ALU.add))
                dve.sem_inc(var_ready, 1)
                dve.wait_ge(std_ready, k)
                link(nc.vector.reciprocal(ln_s[:, 0, 0:tiles], ln_s[:, 2, 0:tiles]))
                link(STT(out=hs, in0=hs, scalar=0.0, in1=bc(0), op0=ALU.max, op1=ALU.mult))

            dve.wait_ge(x_in, 32)
            layernorm(NT, 1)
            hf = h_sb[:, :, :].rearrange("p t d -> p (t d)")
            def turn(j):
                wait(dve, n_hp, j)
                nc.vector.tensor_copy(h_st[:, :], hf[:, bass.ds(j * (SUP * D), SUP * D)]).then_inc(n_hs, 1)
                dve.wait_ge(n_hp, j + 1)
                nc.vector.tensor_copy(hT[:, :], ps[0:D, 0, :]).then_inc(n_hT, 1)
                dve.wait_ge(n_ap, j + 1)
                TS(qT[:, :], ps[0:D, 4, :], pib1c[:, 0:1], None, ALU.add).then_inc(n_qT, 1)
                dve.wait_ge(n_PQ, j + 1)
                q0, q1 = q_st[:, 0, :, :], q_st[:, 1, :, :]
                qd = q_parts[:, :, :, :].rearrange("p t s d -> p t (s d)")
                qp = [qd[:, bass.ds(j * SUP, SUP), t * D:(t + 1) * D] for t in range(3)]
                TT(q0, ps[:, 6, 0:SUP * D].rearrange("p (t d) -> p t d", t=SUP),
                   pib2r[:, :].rearrange("p (o d) -> p o d", o=1).broadcast_to([P, SUP, D]), ALU.add).then_inc(n_Q, 1)
                dve.wait_ge(n_Q, j * 5 + 1)
                nc.vector.tensor_copy(qp[0], q0).then_inc(n_Q, 1)
                dve.wait_ge(n_Q, j * 5 + 2)
                TT(q1, q0, qp[0], ALU.subtract).then_inc(n_Q, 1)
                dve.wait_ge(n_Q, j * 5 + 3)
                nc.vector.tensor_copy(qp[1], q1).then_inc(n_Q, 1)
                dve.wait_ge(n_Q, j * 5 + 4)
                TT(qp[2], q1, qp[1], ALU.subtract).then_inc(n_Q, 1)
            turns(dve, SUPS, turn)
            iota3 = iota_p[:, :].rearrange("p (o m) -> p o m", o=1).broadcast_to([P, K, P])
            iota_r = iota_p[:, 0:RELS].rearrange("p (o m) -> p o m", o=1).broadcast_to([P, K, RELS])

            def split_w(l):
                for m in range(2):
                    dve.wait_ge(w_split[l], 2 * m + 1)
                    TT(w_all, w_all, w_parts[:, m, :], ALU.subtract).then_inc(w_split[l], 1)
            split_w(0)

            def per_edge(ap, j, width):
                return ap[:, bass.ds(j * K, K)].rearrange("p (k o) -> p k o", o=1).broadcast_to([P, K, width])

            def bin_sums(j, width):
                b = dve.value_load(bin_gi[0:1, bass.ds(j, 1)], min_val=0, max_val=BINS)
                return acc[:, :, :].rearrange("p a n -> p (a n)")[:, bass.ds(dve.snap(b * ND), width)]

            def add_to_bin(dst_acc, j, s, sums_ps):
                wait(dve, s["acc"], j)
                wait(dve, s["s"], j + 1)
                TT(dst_acc, dst_acc, sums_ps, ALU.add).then_inc(s["acc"], 1)

            s = L[0]

            def step(i, u, t):
                if live(i, 5):
                    dst_acc = bin_sums(i - 5, ND)
                if live(i, 2):
                    a, v = u % 2, (u - 2) % U
                    wait(dve, gathered[v], uses(0, t, u, 2) * (16 * K))
                    wait(dve, s["uT"], i - 3)
                    wait(dve, s["q"], i - 1)
                    TT(u_sb[:, a, :, :, :],
                       gat[:, v, :, :].rearrange("p k (o d) -> p k o d", o=1).broadcast_to([P, K, 2, D]),
                       ps_q.rearrange("p (k o d) -> p k o d", k=K, o=1).broadcast_to([P, K, 2, D]),
                       ALU.add).then_inc(s["u"], 1)
                if live(i, 5):
                    add_to_bin(dst_acc, i - 5, s, ps_s)
                if live(i, 3):
                    a = (u + 1) % 2
                    wait(dve, s["zT"], i - 4)
                    wait(dve, s["bb"], i - 2)
                    wait(dve, s["uTc"], i - 2)
                    TT(vT[:, a, :, :], bb[:, a, :, :],
                       uT[:, a, :].rearrange("p (o n) -> p o n", o=1).broadcast_to([P, 4, K * P]),
                       ALU.mult).then_inc(s["v"], 1)
                    wait(dve, s["s"], i - 4)
                    TT(rel_b[:, a, :, :], iota_r, per_edge(typ, i - 3, RELS), ALU.is_equal).then_inc(s["rel"], 1)
                if live(i, 0):
                    wait(dve, s["ohb"], i - U + 1)
                    wait(dve, s["s"], i - U + 1)
                    wait(dve, s["loc"], 2 * (i + 1))
                    TT(oh[:, u, :, :], iota3, per_edge(loc, i, P), ALU.is_equal).then_inc(s["oh"], 1)
            steps(dve, 5, step)

            if stop < 1:
                dve.wait_ge(s["acc"], GROUPS)
                nc.vector.tensor_copy(h_sb[:, 0:BINS, :], acc[:, 0:BINS, 0:D]).then_inc(final, 1)
                return

            sums, counts = acc[:, 0:BINS, 0:D], acc[:, 0:BINS, D:ND]
            dve.wait_ge(s["acc"], GROUPS)
            link(nc.vector.tensor_reduce(ln_s[:, 0, 0:BINS], counts, AX.X, ALU.add))
            xf = x_sb[:, :, :].rearrange("p t d -> p (t d)")
            def turn(j):
                wait(dve, nd["tp"], j)
                nc.vector.tensor_copy(s_st[:, :, 0:D], acc[:, bass.ds(j * FIVE, FIVE), 0:D]).then_inc(nd["st"], 1)
                nc.vector.tensor_copy(s_st[:, :, D:D + 1].rearrange("p t o -> p (t o)"),
                                      ln_s[:, 0, bass.ds(j * FIVE, FIVE)]).then_inc(nd["st"], 1)
                dve.wait_ge(nd["tp"], j + 1)
                nc.vector.tensor_copy(sT[:, :], ps_flat[0:D + 1, 0:FIVE * P]).then_inc(nd["tT"], 1)
                dve.wait_ge(nd["o"], j + 1)
                xj = xf[:, bass.ds(j * (FIVE * D), FIVE * D)]
                TT(xj, xj, ps[:, 2, 0:FIVE * D], ALU.add).then_inc(nd["x"], 1)
            turns(dve, BINS // FIVE, turn)
            dve.wait_ge(nd["x"], BINS // FIVE)
            link(TS(counts, counts, 1.0, None, ALU.max))
            link(nc.vector.reciprocal(counts, counts))
            link(nc.vector.memset(sums, 0.0))
            layernorm(BINS, 2)
            dve.sem_inc(h_ready, 1)
            if stop < 2:
                nc.vector.tensor_copy(h_sb[:, 0:BINS, :], x_sb[:, 0:BINS, :]).then_inc(final, 1)
                return

            for l in range(2):
                y = Y[l]

                hi, mid, lo = h_parts[:, :, D:2 * D], h_parts[:, :, 0:D], h_parts[:, :, 2 * D:3 * D]
                hs, rest = h_sb[:, 0:BINS, :], sq[:, 0:BINS, :]
                link(nc.vector.tensor_copy(hi, hs))
                link(TT(rest, hs, hi, ALU.subtract))
                link(nc.vector.tensor_copy(mid, rest))
                link(TT(lo, rest, mid, ALU.subtract))

                def stage(a, q):
                    nc.vector.tensor_copy(hh_st[:, q, :],
                                          h_parts[:, :, :].rearrange("p a n -> p (a n)")[:, bass.ds(a * (3 * D), 3 * D)]
                                          ).then_inc(y["st"], 1)

                def turn_y(a, q, ahead):
                    if ahead:
                        wait(dve, y["tp"], a)
                        stage(a + 1, 1 - q)
                    for c in (1, 3):
                        dve.wait_ge(y[f"mm{c}"], a + 1)
                        wait(dve, y[f"o{c}"], 16 * a)
                        r = 0 if c == 3 else c
                        nc.vector.tensor_copy(y_stage[:, c * YU:(c + 1) * YU],
                                              ps_flat[:, r * YU:(r + 1) * YU]).then_inc(y[f"ev{c}"], 1)
                    dve.wait_ge(y["mm4"], a + 1)
                    nc.vector.tensor_copy(y_stage[:, NYU * YU:NYU * YU + D], ps[:, 6, 0:D]).then_inc(y["ev4"], 1)
                    TT(rr[:, :, :].rearrange("p a n -> p (a n)")[:, bass.ds(a * (2 * D), 2 * D)],
                       ps[:, 6, D:3 * D], brr[:, l, :], ALU.add).then_inc(y["h"], 1)
                stage(0, 0)
                def turn(pair):
                    turn_y(pair * 2, 0, True)
                    turn_y(pair * 2 + 1, 1, True)
                turns(dve, BINS // 2, turn)
                turn_y(BINS - 1, 0, False)

                if l == 0:
                    split_w(1)
                s = L[l + 1]
                if l == 0:
                    def step1(i, u, t):
                        if live(i, 5):
                            dst_acc = bin_sums(i - 5, D)
                        if live(i, 0):
                            wait(dve, s["s"], i - U + 1)
                            TT(oh[:, u, :, :], iota3, per_edge(loc, i, P), ALU.is_equal).then_inc(s["oh"], 1)
                        if live(i, 3):
                            a, v = (u + 1) % 2, (u - 3) % U
                            wait(dve, s["wt"], i - 2)
                            for k in range(K):
                                e = (i - 3) * K + k
                                STT(out=pick[:, k, :], in0=iota_p[:, 0:RELS], scalar=typ[:, bass.ds(e, 1)],
                                    in1=ps_w[a][:, k, :], op0=ALU.is_equal, op1=ALU.mult,
                                    accum_out=w_edge[:, bass.ds(e, 1)]).then_inc(s["w"], 1)
                            wait(dve, s["w"], K * (i - 2))
                            wait(dve, gathered[v], uses(1, t, u, 3) * (16 * K))
                            wait(dve, s["s"], i - 4)
                            TT(tr[:, a, :, :], gat[:, v, :, :], per_edge(w_edge, i - 3, D), ALU.mult
                               ).then_inc(s["scaled"], 1)
                        if live(i, 5):
                            add_to_bin(dst_acc, i - 5, s, ps_s2[(u + 1) % 2])
                    steps(dve, 5, step1)
                else:
                    def step2(i, u, t):
                        if live(i, 3):
                            dst_acc = bin_sums(i - 3, D)
                        if live(i, 0):
                            wait(dve, s["s"], i - U + 1)
                            for k in range(K):
                                e = i * K + k
                                TS(oh[:, u, k, :], iota_p[:, :], loc[:, bass.ds(e, 1)], w_edge[:, bass.ds(e, 1)],
                                   ALU.is_equal, ALU.mult).then_inc(s["oh"], 1)
                        if live(i, 3):
                            add_to_bin(dst_acc, i - 3, s, ps_s2[(u + 1) % 2])
                    steps(dve, 3, step2)
                dve.wait_ge(s["acc"], GROUPS)
                link(TT(sq[:, 0:BINS, :], sums, rr[:, :, 0:D], ALU.add))
                link(TS(rr[:, :, D:2 * D], rr[:, :, D:2 * D], 0.0, None, ALU.max))
                link(STT(out=h_sb[:, 0:BINS, :], in0=sq[:, 0:BINS, :], scalar=0.0, in1=rr[:, :, D:2 * D],
                         op0=ALU.max, op1=ALU.add))
                if l == 0:
                    link(nc.vector.memset(sums, 0.0))
            TT(h_sb[:, 0:BINS, :], h_sb[:, 0:BINS, :], x_sb[:, 0:BINS, :], ALU.add).then_inc(final, 1)

        @block.tensor
        def _(pe):
            MM = nc.tensor.matmul
            pe.wait_ge(w_in, 16 * 18)
            pe.wait_ge(pool_c, 7)
            for b in range(BASIS):
                mm = MM(ps[0:D, 3, b * D:(b + 1) * D], w3[:, :, b], ident[0:D, 0:D], start=True, stop=True)
            mm.then_inc(w3_t, 1)
            pe.wait_ge(w3_c, 1)
            for c in range(4):
                mm = MM(ps[:, 2, c * D:(c + 1) * D], w3t[:, c * P:(c + 1) * P], wii1[:, :], start=True, stop=True)
            mm.then_inc(wz_p, 1)
            pe.wait_ge(counted, 1)
            MM(ps[:, 6, 0:1], ones[:, :], small[:, 0:1], start=True, stop=True)
            MM(ps[0:BINS + 1, 6, 1:2], count_pa[:, :], ones[:, 0:1], start=True, stop=True)
            MM(ps[:, 6, 64:64 + BINS + 1], ones[:, :], count_pa[:, :], start=True, stop=True)
            MM(ps[:, 6, 128:128 + BINS + 1], before[:, :], count_pa[:, :], start=True, stop=True).then_inc(totals, 1)
            pe.wait_ge(in_groups, 1)
            MM(ps[0:BINS, 6, 2:3], upto[0:BINS, 0:BINS], small[0:BINS, 4:5], start=True, stop=True
               ).then_inc(cumulated, 1)
            pe.wait_ge(masks, 1)
            MM(ps[:, 4, 0:GROUPS], ones[0:BINS, :], mask_ag[:, :], start=True, stop=True)
            MM(ps[:, 5, 0:GROUPS], gap_b[:, :], mask_ag[:, :], start=True, stop=True).then_inc(spread, 1)

            pe.wait_ge(wz_c, 1)
            def turn(j):
                held_wait(pe, n_hs, j + 1, tick)
                for t in range(SUP):
                    mm = MM(ps[0:D, 0, t * P:(t + 1) * P], h_st[:, t * D:(t + 1) * D], ident[:, :],
                            start=True, stop=True)
                mm.then_inc(n_hp, 1)
                held_wait(pe, n_hT, j + 1, tick)
                MM(ps[0:D, 1, :], w1[:, :], hT[:, :], start=True, stop=True).then_inc(n_tp, 1)
                held_wait(pe, n_tT, j + 1, tick)
                MM(ps[0:D, 2, :], w2[:, :], tT[:, :], start=True, stop=True).then_inc(n_pp, 1)
                held_wait(pe, n_pT, j + 1, tick)
                MM(ps[0:D, 3, :], wa[:, 0, :], p1T[:, :], start=True, stop=True)
                MM(ps[0:D, 4, :], wa[:, 1, :], p1T[:, :], start=True, stop=True).then_inc(n_ap, 1)
                held_wait(pe, n_aT, j + 1, tick)
                held_wait(pe, n_qT, j + 1, tick)
                wait(pe, n_Q, j * 5)
                for t in range(SUP):
                    MM(ps[:, 5, t * D:(t + 1) * D], aT[:, t * P:(t + 1) * P], wi2[:, :], start=True, stop=True)
                    mm = MM(ps[:, 6, t * D:(t + 1) * D], qT[:, t * P:(t + 1) * P], wi2[:, :], start=True, stop=True)
                mm.then_inc(n_PQ, 1)
            turns(pe, SUPS, turn)
            pe.wait_ge(n_Q, SUPS * 5)
            pe.wait_ge(n_Ps, SUPS)
            s = L[0]
            qf = q_parts[:, :, :, :].rearrange("p t s d -> p (t s d)")
            Z3 = (3 * D)

            def step(i, u, t):
                if live(i, 3):
                    a = (u + 1) % 2
                    wait(pe, s["u"], i - 2)
                    wait(pe, s["uTc"], i - 3)
                    for k in range(K):
                        mm = pe.transpose(ps_u[:, k * P:(k + 1) * P],
                                          u_sb[:, a, k, :, :].rearrange("p o d -> p (o d)"), ident[:, :])
                    mm.then_inc(s["uT"], 1)
                if live(i, 5):
                    a, v = (u + 1) % 2, (u - 5) % U
                    wait(pe, s["acc"], i - 5)
                    wait(pe, s["t"], i - 4)
                    if live(i, 3):
                        wait(pe, s["u"], i - 2)
                    for k in range(K):
                        MM(ps_s[:, 0:D], oh[:, v, k, :], tr[:, a, k, :], start=(k == 0), stop=(k == K - 1))
                    wait(pe, s["rel"], i - 4)
                    for k in range(K):
                        mm = MM(ps_s[:, D:ND], oh_b[:, v, k, :], rel_b[:, a, k, :],
                                start=(k == 0), stop=(k == K - 1))
                    mm.then_inc(s["s"], 1)
                if live(i, 4):
                    a = u % 2
                    wait(pe, s["v"], i - 3)
                    wait(pe, s["t"], i - 4)
                    for c in range(2):
                        for q in range(2):
                            mm = MM(ps_zT[q * D:(q + 1) * D, :], wz[:, 2 * q + c, :], vT[:, a, 2 * q + c, :],
                                    start=(c == 0), stop=(c == 1))
                    mm.then_inc(s["zT"], 1)
                if live(i, 2):
                    a = u % 2
                    b = pe.snap(pe.value_load(bin_gi[0:1, bass.ds(i - 2, 1)], min_val=0, max_val=BINS) * Z3)
                    wait(pe, s["ohTc"], i - 1)
                    wait(pe, s["u"], i - 2)
                    for k in range(K):
                        for part in range(3):
                            mm = MM(ps_q[:, k * D:(k + 1) * D], ohT_b[:, a, k * P:(k + 1) * P],
                                    qf[:, bass.ds(b + part * D, D)], start=(part == 0), stop=(part == 2))
                    mm.then_inc(s["q"], 1)
                if live(i, 1):
                    v = (u - 1) % U
                    wait(pe, s["ohb"], i)
                    wait(pe, s["bTc"], i - 1)
                    for k in range(K):
                        pe.transpose(ps_t[:, k * P:(k + 1) * P], oh_b[:, v, k, :], ident_b[:, :])
                    wait(pe, rec_slot[v], uses(0, t, u, 1) * 16)
                    for k in range(K):
                        mm = pe.transpose(ps_b[0:SPLIT, k * P:(k + 1) * P],
                                          rec_u[:, v, k * W + 4:(k + 1) * W].bitcast(BF16), ident_b[:, :])
                    mm.then_inc(s["ohT"], 1)
                if live(i, 2):
                    a = u % 2
                    wait(pe, s["bTc"], i - 1)
                    for c in range(2):
                        MM(bb[:, a, c, :], sel[:, c, :], bT[:, a, :], start=True, stop=True)
                if live(i, 4):
                    wait(pe, s["zTc"], i - 3)
                    for k in range(K):
                        mm = MM(ps_z[:, k * D:(k + 1) * D], zT[:, k * P:(k + 1) * P], ident2[:, :],
                                start=True, stop=True)
                    mm.then_inc(s["z"], 1)
                if live(i, 2):
                    for c in range(2, 4):
                        mm = MM(bb[:, a, c, :], sel[:, c, :], bT[:, a, :], start=True, stop=True)
                    mm.then_inc(s["bb"], 1)
            steps(pe, 5, step)

            if stop < 1:
                return
            pe.wait_ge(s["acc"], GROUPS)
            def turn(j):
                pe.wait_ge(nd["st"], 2 * (j + 1))
                for t in range(FIVE):
                    mm = MM(ps_flat[0:D + 1, t * P:(t + 1) * P], s_st[:, t, :], ident[:, :], start=True, stop=True)
                mm.then_inc(nd["tp"], 1)
                pe.wait_ge(nd["tT"], j + 1)
                wait(pe, nd["x"], j)
                for t in range(FIVE):
                    mm = MM(ps[:, 2, t * D:(t + 1) * D], sT[:, t * P:(t + 1) * P], wii2[:, :], start=True, stop=True)
                mm.then_inc(nd["o"], 1)
            turns(pe, BINS // FIVE, turn)
            if stop < 2:
                return

            for l in range(2):
                y = Y[l]

                def transpose_h(a, q):
                    pe.wait_ge(y["st"], a + 1)
                    for m in range(2):
                        mm = pe.transpose(ps_hT[q][:, m, :], hh_st[:, q, m * D:m * D + P], ident_b[:, :])
                    mm.then_inc(y["tp"], 1)

                def product(o, q, first, n):
                    for m, (half, part) in enumerate(((0, 0), (0, 1), (1, 2))):
                        mm = MM(o, hhT[:, q, half, :], w_parts[:, part, first:first + n], start=(m == 0), stop=(m == 2))
                    return mm

                def turn_y(a, q, ahead):
                    pe.wait_ge(y["hT"], a + 1)
                    if ahead:
                        transpose_h(a + 1, 1 - q)
                    for c in range(NYU):
                        r = 0 if c == 3 else c
                        if c == 3:
                            pe.wait_ge(y["ev0"], a + 1)
                        else:
                            wait(pe, y["ev3" if c == 0 else f"ev{c}"], a)
                        for half in range(2):
                            o = c * YU + half * 512
                            mm = product(ps_flat[:, r * YU + half * 512:r * YU + (half + 1) * 512], q, o, 512)
                        mm.then_inc(y[f"mm{c}"], 1)
                    wait(pe, y["ev4"], a)
                    wait(pe, y["h"], a)
                    product(ps[:, 6, 0:3 * D], q, NYU * YU, 3 * D).then_inc(y["mm4"], 1)
                pe.wait_ge(w_split[l], 6)
                transpose_h(0, 0)
                def turn(pair):
                    turn_y(pair * 2, 0, True)
                    turn_y(pair * 2 + 1, 1, True)
                turns(pe, BINS // 2, turn)
                turn_y(BINS - 1, 0, False)
                for c in range(4):
                    pe.wait_ge(y[f"ev{c}"], BINS)
                pe.wait_ge(y["h"], BINS)
                pe.wait_ge(y["ev4"], BINS)

                s = L[l + 1]
                af = acc[:, :, :].rearrange("p a n -> p (a n)")
                if l == 0:
                    def step1(i, u, t):
                        if live(i, 0):
                            a = u % 2
                            wait(pe, s["oh"], i + 1)
                            wait(pe, s["ohTc"], i - 1)
                            for k in range(K):
                                mm = pe.transpose(ps_t2[a][:, k * P:(k + 1) * P], oh[:, u, k, :], ident[:, :])
                            mm.then_inc(s["ohT"], 1)
                        if live(i, 4):
                            a, v = u % 2, (u - 4) % U
                            wait(pe, s["acc"], i - 5)
                            wait(pe, s["scaled"], i - 3)
                            for k in range(K):
                                mm = MM(ps_s2[a], oh[:, v, k, :], tr[:, a, k, :],
                                        start=(k == 0), stop=(k == K - 1))
                            mm.then_inc(s["s"], 1)
                        if live(i, 1):
                            a = (u + 1) % 2
                            b = pe.value_load(bin_gi[0:1, bass.ds(i - 1, 1)], min_val=0, max_val=BINS)
                            wait(pe, s["ohTc"], i)
                            wait(pe, s["w"], K * (i - 2))
                            for k in range(K):
                                mm = MM(ps_w[a][:, k, :], ohT_f[:, a, k * P:(k + 1) * P],
                                        af[:, bass.ds(b * ND + D, RELS)], start=True, stop=True)
                            mm.then_inc(s["wt"], 1)
                    steps(pe, 4, step1)
                else:
                    def step2(i, u, t):
                        if live(i, 2):
                            a, v = u % 2, (u - 2) % U
                            wait(pe, s["oh"], K * (i - 1))
                            wait(pe, gathered[v], uses(2, t, u, 2) * (16 * K))
                            wait(pe, s["acc"], i - 3)
                            for k in range(K):
                                mm = MM(ps_s2[a], oh[:, v, k, :], gat[:, v, k, :],
                                        start=(k == 0), stop=(k == K - 1))
                            mm.then_inc(s["s"], 1)
                    steps(pe, 2, step2)


_INS = ["x", "src", "dst", "edge_attr_8", "edge_type_65",
        "L0_gnn_pp_W1", "L0_gnn_pp_b1", "L0_gnn_pp_W2", "L0_gnn_pp_b2", "L0_gnn_pi_W1", "L0_gnn_pi_b1",
        "L0_gnn_pi_W2", "L0_gnn_pi_b2", "L0_gnn_pi_W3", "L0_gnn_ii_W1", "L0_gnn_ii_b1", "L0_gnn_ii_W2",
        "L0_gnn_ii_b2", "L1_gnn_W", "L1_gnn_root", "L1_gnn_bias", "L1_gnn_res_W", "L1_gnn_res_b"]


def kernel(**inputs):
    import numpy as np
    import concourse.bacc as bacc
    from concourse.bass_utils import run_bass_kernel_spmd

    nc = bacc.Bacc("TRN2", target_bir_lowering=False, num_devices=1)
    arrays, args = {}, []
    for name in _INS:
        a = np.ascontiguousarray(inputs[name])
        arrays[f"in_{name}"] = a
        args.append(nc.dram_tensor(f"in_{name}", a.shape, mybir.dt.from_np(a.dtype), kind="ExternalInput").ap())
    args.append(nc.dram_tensor("out_0", (NODES, D), F32, kind="ExternalOutput").ap())
    build(nc, *args)
    r = run_bass_kernel_spmd(nc, [arrays], core_ids=[0])
    return r.results[0]["out_0"]
```

```python
from contextlib import ExitStack

import concourse.bass as bass
from concourse import mybir

P = 128
D = 64
RELS = 65
BASIS = 8
NODES = 3125
EDGES_ALL = 103125

BINS = (NODES + P - 1) // P
LAST = NODES - (BINS - 1) * P
K = 2
GE = K * P
U = 6
GROUPS = (EDGES_ALL // GE + BINS + U - 1) // U * U
TURNS = GROUPS // U
PARTS = 5
COLS = (EDGES_ALL + P - 1) // P
FULL = EDGES_ALL // COLS
REST = EDGES_ALL - FULL * COLS
ROWS = P * COLS + 2 * GE
W = 16
SPLIT = 3 * BASIS
PAD_DST = BINS * P
SUP = 4
SUPS = (BINS + SUP - 1) // SUP
NT = SUP * SUPS
SC = 13
SCT = COLS // SC
ND = D + RELS
YW = RELS * D
YN = YW + 2 * D
YU = 1024
NYU = YW // YU
Y_REGION = ((0, 1, 2, 0), (1, 2, 0, 1))
Y_BEFORE = ((2, 3, 1), (1, 2, 3))
FIVE = 5

SMALL_LOADS = 18

ALU = mybir.AluOpType
ACT = mybir.ActivationFunctionType
AX = mybir.AxisListType
F32 = mybir.dt.float32
BF16 = mybir.dt.bfloat16
I32 = mybir.dt.int32
U32 = mybir.dt.uint32


def steps(eng, lead, step, peel=1, between=None):
    for i in range(peel * U):
        step(i, i % U, i // U)
    parts = PARTS if between else 1
    cuts = [peel] + [TURNS * (n + 1) // parts for n in range(parts)]
    for n in range(parts):
        with eng.Fori(cuts[n], cuts[n + 1]) as t:
            for u in range(U):
                step(t * U + u, u, t)
        if n < parts - 1:
            between(n)
    for i in range(GROUPS, GROUPS + lead):
        step(i, i % U, i // U)


def turns(eng, n, turn):
    turn(0)
    with eng.Fori(1, n) as j:
        turn(j)


def live(i, lag):
    return not isinstance(i, int) or 0 <= i - lag < GROUPS


def wait(eng, sem, value):
    if not isinstance(value, int) or value > 0:
        eng.wait_ge(sem, value)


def held_wait(eng, sem, value, tick):
    if not isinstance(value, int) or value > 0:
        eng.wait_ge(sem, value)
        eng.sem_inc(tick, 1)


def uses(l, t, u, lag=0):
    return t + (l * TURNS + (1 if u >= lag else 0))


def build(nc, x, src, dst, basis, etype, pp_W1, pp_b1, pp_W2, pp_b2, pi_W1, pi_b1, pi_W2, pi_b2,
          pi_W3, ii_W1, ii_b1, ii_W2, ii_b2, r_W, r_root, r_bias, r_res_W, r_res_b, out):
    rec_d = nc.dram_tensor("rec_d", (ROWS, W), F32, kind="Internal").ap()
    p_d = nc.dram_tensor("p_d", (NT * P, D), F32, kind="Internal").ap()
    y_d = nc.dram_tensor("y_d", (BINS * P * RELS, D), F32, kind="Internal").ap()
    y_rows = y_d.rearrange("(n r) d -> n (r d)", r=RELS)

    with ExitStack() as ctx:
        def sb(name, shape, dt):
            return ctx.enter_context(nc.sbuf_tensor(name, shape, dt))

        def sem(name):
            return ctx.enter_context(nc.semaphore(name))

        region_a = sb("region_a", [P, COLS * W], F32)
        rec_a = region_a[:, 0:COLS * W].rearrange("p (n w) -> p n w", w=W)
        w_all = region_a[:, 0:YN]
        w_parts = region_a[:, YN:YN + 3 * YN // 2].bitcast(BF16).rearrange("p (s n) -> p s n", s=3)
        region_c = sb("region_c", [P, 9800], F32)
        basis_in = region_c[:, 0:COLS * BASIS].rearrange("p (n b) -> p n b", b=BASIS)
        dst_in = region_c[:, COLS * BASIS:COLS * (BASIS + 1)].bitcast(I32)
        src_in = region_c[:, COLS * (BASIS + 1):COLS * (BASIS + 2)].bitcast(I32)
        typ_in = region_c[:, COLS * (BASIS + 2):COLS * (BASIS + 3)].bitcast(I32)
        y_stage = region_c[:, 0:NYU * YU + D]
        region_r = sb("region_r", [P, 4 * COLS], F32)
        spot = [0]

        def part_of_c(width):
            spot[0] += width
            return region_c[:, spot[0] - width:spot[0]]
        vT = part_of_c(8 * K * P).rearrange("p (s c n) -> p s c n", s=2, c=4)
        uT = part_of_c(2 * K * P).rearrange("p (s n) -> p s n", s=2)
        u_sb = part_of_c(4 * K * D).rearrange("p (s k o d) -> p s k o d", s=2, k=K, o=2)
        ohT_b = part_of_c(K * P).bitcast(BF16).rearrange("p (s n) -> p s n", s=2)
        bT = part_of_c(K * P).bitcast(BF16).rearrange("p (s n) -> p s n", s=2)
        spot[0] = NYU * YU + D
        hT, tT1 = part_of_c(SUP * P)[0:D, :], part_of_c(SUP * P)[0:D + 1, :]
        p_st = part_of_c(SUP * D).rearrange("p (t d) -> p t d", t=SUP)
        q_st = part_of_c(2 * SUP * D).rearrange("p (s t d) -> p s t d", s=2, t=SUP)
        spot[0] = NYU * YU + D
        h_parts = part_of_c(BINS * 3 * D // 2).bitcast(BF16).rearrange("p (a n) -> p a n", a=BINS)
        hh_st = part_of_c(3 * D).bitcast(BF16).rearrange("p (q n) -> p q n", q=2)
        hhT = part_of_c(2 * P).bitcast(BF16).rearrange("p (q s n) -> p q s n", q=2, s=2)
        s_st = part_of_c(FIVE * (D + 1)).rearrange("p (t d) -> p t d", t=FIVE)
        sT = part_of_c(FIVE * P)[0:D + 1, :]
        bin_of = region_r[:, 0:COLS]
        bin_int = region_r[:, COLS:2 * COLS].bitcast(I32)
        junk = region_r[:, 2 * COLS:3 * COLS]
        place = region_r[:, 3 * COLS:4 * COLS]
        place_i = bin_int
        rr = region_r[:, 0:BINS * 2 * D].rearrange("p (a n) -> p a n", a=BINS)
        next_int = sb("next_int", [P, 1], I32)
        next_bin = sb("next_bin", [P, 1], F32)
        count_pa = sb("count_pa", [P, BINS + 1], F32)
        pad_rec = sb("pad_rec", [P, (ROWS - P * COLS) // P * W], F32)

        ident = sb("ident", [P, P], F32)
        ident_b = sb("ident_b", [P, P], BF16)
        ones = sb("ones", [P, P], F32)
        before = sb("before", [P, P], F32)
        upto = sb("upto", [P, P], F32)
        iota_p = sb("iota_p", [P, P], F32)
        iota_g = sb("iota_g", [P, GROUPS], F32)
        zero_c = sb("zero_c", [P, D], F32)
        small = sb("small", [P, 16], F32)
        small_i = sb("small_i", [P, 4], I32)
        mask_ag = sb("mask_ag", [BINS, GROUPS], F32)
        gap_b = sb("gap_b", [BINS, P], F32)
        bin_g = sb("bin_g", [P, GROUPS], F32)
        base_neg = sb("base_neg", [P, GROUPS], F32)
        bin_gi = sb("bin_gi", [P, GROUPS], I32)
        start_g = sb("start_g", [P, GROUPS], F32)
        start_gi = sb("start_gi", [P, GROUPS], I32)
        offset_pa = sb("offset_pa", [P, BINS + 1], F32)
        total_pa = sb("total_pa", [P, BINS + 1], F32)
        flag_i = sb("flag_i", [P, 1], I32)
        place_s = sb("place_s", [P, SC], U32)
        rec_s = sb("rec_s", [P, SC * W], F32)

        x_sb = sb("x_sb", [P, NT, D], F32)
        h_sb = sb("h_sb", [P, NT, D], F32)
        ln_s = sb("ln_s", [P, 3, NT], F32)
        sq = sb("sq", [P, NT, D], F32)
        q_parts = sb("q_parts", [P, NT, 3, D], BF16)
        acc = sb("acc", [P, BINS + 1, ND], F32)
        loc = sb("loc", [P, GROUPS * K], F32)
        typ = sb("typ", [P, GROUPS * K], F32)
        w_edge = sb("w_edge", [P, GROUPS * K], F32)

        w1 = sb("w1", [D, D], F32)
        w2 = sb("w2", [D, D], F32)
        wa = sb("wa", [D, 2, D], F32)
        wi2 = sb("wi2", [D, D], F32)
        w3 = sb("w3", [D, D, BASIS], F32)
        w3t = sb("w3t", [D, BASIS * D], F32)
        wii1 = sb("wii1", [D, D], F32)
        wz = sb("wz", [P, BASIS // 2, D], F32)
        wii2 = sb("wii2", [D + 1, D], F32)
        b1c = sb("b1c", [D, 1], F32)
        w2T = sb("w2T", [D, D + 1], F32)
        wpi = sb("wpi", [D, 2, D + 1], F32)
        wpq = sb("wpq", [D + 1, 2, D], F32)
        pib1c = sb("pib1c", [D, 1], F32)
        pib2r = sb("pib2r", [P, D], F32)
        iib1c = sb("iib1c", [P, 1], F32)
        ident2 = sb("ident2", [P, D], F32)
        zT = sb("zT", [P, K * P], F32)
        brr = sb("brr", [P, 2, 2 * D], F32)
        sel_f = sb("sel_f", [P, 4 * P], F32)
        sel_t = h_sb[:, 0:NT - 4, :].rearrange("k t d -> k (t d)").rearrange("k (t m) -> k t m", t=3)
        sel = sb("sel", [P, 4, P], BF16)

        h_st = sb("h_st", [P, SUP * D], F32)

        rec_u = sb("rec_u", [P, U, K * W], F32)
        gat = sb("gat", [P, U, K, D], F32)
        oh = sb("oh", [P, U, K, P], F32)
        oh_b = sb("oh_b", [P, U, K, P], BF16)
        rel_b = sb("rel_b", [P, 2, K, RELS], BF16)
        ohT_f = sb("ohT_f", [P, 2, K * P], F32)
        tr = sb("tr", [P, 2, K, D], F32)
        pick = sb("pick", [P, 2, RELS], F32)

        ps = ctx.enter_context(nc.psum_tensor("ps", [P, 8, 512], F32))
        ps_flat = ps[:, :, :].rearrange("p b n -> p (b n)")
        bb = ps_flat[:, 0:4 * 512].rearrange("p (s c n) -> p s c n", s=2, c=4)
        ps_t, ps_b = ps[:, 4, 0:K * D].bitcast(BF16), ps[:, 4, K * P:K * P + K * D].bitcast(BF16)
        ps_u = ps[:, 5, 0:K * P]
        ps_zT, ps_z = ps[:, 6, 0:K * P], ps[:, 6, K * P:K * P + K * D]
        ps_s, ps_q = ps[:, 7, 0:ND], ps[:, 7, 256:256 + K * D]
        ps_t2 = [ps[:, 4 + q, 0:K * P] for q in range(2)]
        ps_s2 = [ps[:, 6 + q, 0:D] for q in range(2)]
        ps_hT = [ps[:, 7, q * P:(q + 1) * P].bitcast(BF16).rearrange("p (s n) -> p s n", s=2) for q in range(2)]
        ps_w = [ps[:, q, 0:K * RELS].rearrange("p (k r) -> p k r", k=K) for q in range(2)]

        edges_in = sem("edges_in")
        basis_in_s = sem("basis_in_s")
        x_in = sem("x_in")
        w_in = sem("w_in")
        const = sem("const")
        dve_c = sem("dve_c")
        pool_c = sem("pool_c")
        counted = sem("counted")
        totals = sem("totals")
        in_groups = sem("in_groups")
        cumulated = sem("cumulated")
        masks = sem("masks")
        spread = sem("spread")
        tables = sem("tables")
        flag = sem("flag")
        placed = sem("placed")
        rec_made = sem("rec_made")
        pad_out = sem("pad_out")
        rec_out = sem("rec_out")
        rec_ready = sem("rec_ready")
        scat = sem("scat")
        scat_in = sem("scat_in")
        w_split = [sem(f"w_split{l}") for l in range(2)]
        w3_t = sem("w3_t")
        w3_c = sem("w3_c")
        wz_p = sem("wz_p")
        wz_c = sem("wz_c")
        var_ready = sem("var_ready")
        std_ready = sem("std_ready")
        h_ready = sem("h_ready")
        n_hs = sem("n_hs")
        n_hp = sem("n_hp")
        n_hT = sem("n_hT")
        n_tp = sem("n_tp")
        n_tT = sem("n_tT")
        w2_t = sem("w2_t")
        w2_c = sem("w2_c")
        wpi_p = sem("wpi_p")
        wpi_c = sem("wpi_c")
        wpq_p = sem("wpq_p")
        wpq_c = sem("wpq_c")
        n_PQ = sem("n_PQ")
        n_Ps = sem("n_Ps")
        n_Q = sem("n_Q")
        n_Pout = sem("n_Pout")
        tick = sem("tick")
        placed_c = sem("placed_c")
        cleared = sem("cleared")

        ctx.enter_context(nc.allow_non_contiguous_dma(reason="a few columns of single words"))
        block = ctx.enter_context(nc.Block())

        def gsems(tag, slots):
            return [sem(f"{tag}{u}") for u in range(slots)]

        rec_slot = gsems("rec_slot", U)
        gathered = gsems("gathered", U)
        names = (("oh", "ohb", "ohT", "ohTc", "bTc", "q", "bb", "u", "uT", "uTc", "v", "zT", "zTc", "z", "t",
                  "rel", "s", "acc", "loc"),
                 ("oh", "ohT", "ohTc", "wt", "w", "scaled", "s", "acc"),
                 ("oh", "s", "acc"))
        L = [{n: sem(f"l{l}_{n}") for n in names[l]} for l in range(3)]
        nd = {n: sem(f"nd_{n}") for n in ("st", "tp", "tT", "o", "x")}
        Y = [{n: sem(f"y{l}_{n}") for n in ("w", "st", "tp", "hT", "mm0", "mm1", "mm2", "mm3", "mm4",
                                           "ev0", "ev1", "ev2", "ev3", "ev4", "o0", "o1", "o2", "o3", "h")}
             for l in range(2)]
        final = sem("final")
        out_s = sem("out_s")

        STT = nc.vector.scalar_tensor_tensor
        TT = nc.vector.tensor_tensor
        TS = nc.vector.tensor_scalar

        @block.sync
        def _(sp):
            def edge_array(ap_sb, ap_d, s):
                sp.dma_start(ap_sb[0:FULL, :], ap_d[0:FULL * COLS].rearrange("(p n) -> p n", n=COLS)).then_inc(s, 16)
                sp.dma_start(ap_sb[FULL:FULL + 1, 0:REST],
                             ap_d[FULL * COLS:EDGES_ALL].rearrange("(p n) -> p n", p=1)).then_inc(s, 16)

            sp.wait_ge(const, 1)
            edge_array(dst_in, dst, edges_in)
            sp.dma_start(next_int[0:FULL, :],
                         dst[COLS:EDGES_ALL].rearrange("(n o) -> n o", o=1)[0:(FULL - 1) * COLS + 1:COLS, :]
                         ).then_inc(edges_in, 16)
            edge_array(src_in, src, edges_in)
            edge_array(typ_in, etype, edges_in)
            sp.dma_start(basis_in[0:FULL, :, :],
                         basis[0:FULL * COLS, :].rearrange("(p n) b -> p n b", n=COLS)).then_inc(basis_in_s, 16)
            sp.dma_start(basis_in[FULL:FULL + 1, 0:REST, :],
                         basis[FULL * COLS:EDGES_ALL, :].rearrange("(p n) b -> p n b", p=1)).then_inc(basis_in_s, 16)
            sp.dma_start(x_sb[:, 0:BINS - 1, :],
                         x[0:(BINS - 1) * P, :].rearrange("(a p) d -> p a d", p=P)).then_inc(x_in, 16)
            sp.dma_start(x_sb[0:LAST, BINS - 1, :], x[(BINS - 1) * P:NODES, :]).then_inc(x_in, 16)
            loads = [
                (w1[:, :], pp_W1), (w2[:, :], pp_W2), (wi2[:, :], pi_W2), (wii1[:, :], ii_W1),
                (wa[:, 0, :], pi_W1[0:D, :]), (wa[:, 1, :], pi_W1[D:2 * D, :]),
                (w3[:, :, :], pi_W3.rearrange("d (c b) -> d c b", b=BASIS)),
                (wii2[0:D, :], ii_W2), (wii2[D:D + 1, :], ii_b2.rearrange("(o d) -> o d", o=1)),
                (b1c[:, :], pp_b1.rearrange("(d o) -> d o", o=1)),
                (w2T[:, D:D + 1], pp_b2.rearrange("(d o) -> d o", o=1)),
                (pib1c[:, :], pi_b1.rearrange("(d o) -> d o", o=1)),
                (pib2r[:, :], pi_b2.rearrange("(o d) -> o d", o=1).broadcast_to([P, D])),
                (iib1c[0:D, :], ii_b1.rearrange("(d o) -> d o", o=1)),
            ]
            for l in range(2):
                loads.append((brr[:, l, 0:D], r_bias[l:l + 1, :].broadcast_to([P, D])))
                loads.append((brr[:, l, D:2 * D], r_res_b[l:l + 1, :].broadcast_to([P, D])))
            assert len(loads) == SMALL_LOADS
            for a, b in loads:
                sp.dma_start(a, b).then_inc(w_in, 16)

            def turn(j):
                held_wait(sp, n_Ps, j + 1, tick)
                sp.dma_start(p_d[bass.ds(j * (SUP * P), SUP * P), :].rearrange("(t p) d -> p t d", p=P),
                             p_st[:, :, :]).then_inc(n_Pout, 16)
            turns(sp, SUPS, turn)
            sp.wait_ge(tables, 1)
            sp.wait_ge(rec_ready, 1)

            def load_w(l):
                for half in range(2):
                    w = w_all[half * D:(half + 1) * D, :]
                    sp.dma_start(w[:, 0:YW].rearrange("d (r k) -> d r k", k=D),
                                 r_W[l].rearrange("r d k -> d r k")).then_inc(Y[l]["w"], 16)
                    sp.dma_start(w[:, YW:YW + D], r_root[l]).then_inc(Y[l]["w"], 16)
                    sp.dma_start(w[:, YW + D:YN], r_res_W[l]).then_inc(Y[l]["w"], 16)

            def slots(l, between=None):
                def step(j, u, t):
                    first = sp.value_load(start_gi[0:1, bass.ds(j, 1)], min_val=0, max_val=EDGES_ALL)
                    held_wait(sp, gathered[u], (uses(l, t, u) - 1) * (16 * K), tick)
                    if l == 0:
                        held_wait(sp, L[0]["ohT"], j - U + 1, tick)
                        held_wait(sp, L[0]["loc"], 2 * (j - U + 1), tick)
                    sp.dma_start(rec_u[:, u, :],
                                 rec_d[bass.ds(first, GE), :].rearrange("(p k) w -> p (k w)", k=K)
                                 ).then_inc(rec_slot[u], 16)
                steps(sp, 0, step, between=between)

            load_w(0)
            slots(0)
            for l in range(2):
                y = Y[l]
                if l == 1:
                    sp.wait_ge(L[1]["acc"], GROUPS)

                def store(a):
                    for c in range(NYU):
                        n = YU + (D if c == NYU - 1 else 0)
                        held_wait(sp, y[f"ev{c}"], a + 1, tick)
                        if c == NYU - 1:
                            held_wait(sp, y["ev4"], a + 1, tick)
                        sp.dma_start(y_rows[bass.ds(a * P, P), c * YU:c * YU + n],
                                     y_stage[:, c * YU:c * YU + n]).then_inc(y[f"o{c}"], 16)
                turns(sp, BINS, store)
                slots(l + 1, (lambda n: load_w(1) if n == 0 else None) if l == 0 else None)
            sp.wait_ge(final, 1)
            sp.dma_start(out[0:(BINS - 1) * P, :].rearrange("(a p) d -> p a d", p=P),
                         h_sb[:, 0:BINS - 1, :]).then_inc(out_s, 16)
            sp.dma_start(out[(BINS - 1) * P:NODES, :], h_sb[0:LAST, BINS - 1, :]).then_inc(out_s, 16)
            sp.wait_ge(out_s, 32)
            sp.wait_ge(n_Pout, 16 * SUPS)

        @block.gpsimd
        def _(pool):
            nc.gpsimd.memset(ones[:, :], 1.0).then_inc(pool_c, 1)
            nc.gpsimd.iota(iota_p[:, :], [[1, P]], base=0, channel_multiplier=0,
                           allow_small_or_imprecise_dtypes=True).then_inc(pool_c, 1)
            nc.gpsimd.iota(iota_g[:, :], [[1, GROUPS]], base=0, channel_multiplier=0,
                           allow_small_or_imprecise_dtypes=True).then_inc(pool_c, 1)
            nc.gpsimd.iota(sel_f[:, :], [[-1, BASIS], [0, D]], base=0, channel_multiplier=1,
                           allow_small_or_imprecise_dtypes=True).then_inc(pool_c, 1)
            pool.wait_ge(pool_c, 1)
            nc.gpsimd.affine_select(out=ident[:, :], in_=ones[:, :], compare_op=ALU.is_equal, fill=0.0, base=0,
                                    pattern=[[-1, P]], channel_multiplier=1).then_inc(pool_c, 1)
            nc.gpsimd.affine_select(out=before[:, :], in_=ones[:, :], compare_op=ALU.is_gt, fill=0.0, base=0,
                                    pattern=[[1, P]], channel_multiplier=-1).then_inc(pool_c, 1)
            nc.gpsimd.affine_select(out=upto[:, :], in_=ones[:, :], compare_op=ALU.is_ge, fill=0.0, base=0,
                                    pattern=[[1, P]], channel_multiplier=-1).then_inc(pool_c, 1)

            pool.wait_ge(rec_made, 1)
            pool.dma_start(rec_d[P * COLS:ROWS, :].rearrange("(p n) w -> p (n w)", p=P),
                           pad_rec[:, :]).then_inc(pad_out, 16)
            pool.wait_ge(flag, 1)
            unsorted = pool.value_load(flag_i[0:1, 0:1], min_val=0, max_val=EDGES_ALL)
            with pool.If(unsorted < 1):
                pool.dma_start(rec_d[0:P * COLS, :].rearrange("(p n) w -> p (n w)", p=P),
                               region_a[:, 0:COLS * W]).then_inc(rec_out, 16)
                pool.wait_ge(rec_out, 16)
            with pool.Else():
                pool.wait_ge(placed, 1)

                def turn(n):
                    pool.dma_start(rec_s[:, :], region_a[:, bass.ds(n * (SC * W), SC * W)]).then_inc(scat_in, 16)
                    pool.dma_start(place_s[:, :], place_i[:, bass.ds(n * SC, SC)].bitcast(U32)).then_inc(scat_in, 16)
                    pool.wait_ge(scat_in, 32 * (n + 1))
                    pool.sem_inc(tick, 1)
                    for c in range(SC):
                        nc.gpsimd.indirect_dma_start(
                            rec_d[0:P * COLS, :], bass.IndirectOffsetOnAxis(ap=place_s[:, c:c + 1], axis=0),
                            rec_s[:, c * W:(c + 1) * W], None).then_inc(scat, 16)
                    pool.wait_ge(scat, 16 * SC * (n + 1))
                    pool.sem_inc(tick, 1)
                turns(pool, SCT, turn)
            pool.end_ifs()
            pool.wait_ge(pad_out, 16)
            pool.sem_inc(rec_ready, 1)

            def gathers(l):
                s = L[l]
                used = s[("u", "scaled", "s")[l]]

                def step(j, u, t):
                    wait(pool, rec_slot[u], uses(l, t, u) * 16)
                    wait(pool, used, j - U + 1)
                    pool.sem_inc(tick, 1)
                    for k in range(K):
                        word = k * W + (0 if l == 0 else 1)
                        nc.gpsimd.indirect_dma_start(
                            gat[:, u, k, :], None, p_d[0:NODES, :] if l == 0 else y_d[:, :],
                            bass.IndirectOffsetOnAxis(ap=rec_u[:, u, word:word + 1].bitcast(U32), axis=0)
                        ).then_inc(gathered[u], 16)
                steps(pool, 0, step)

            pool.wait_ge(n_Pout, 16 * SUPS)
            gathers(0)
            for l in range(2):
                for c in range(NYU):
                    pool.wait_ge(Y[l][f"o{c}"], 16 * BINS)
                gathers(l + 1)

        @block.scalar
        def _(act):
            A = nc.scalar.activation
            act.wait_ge(w3_t, 1)
            A(w3t[:, :], ps[0:D, 3, :], ACT.Copy).then_inc(w3_c, 1)
            act.wait_ge(wz_p, 1)
            A(wz[:, :, :], ps[:, 2, 0:4 * D].rearrange("p (c d) -> p c d", c=4), ACT.Copy).then_inc(wz_c, 1)
            act.wait_ge(w2_t, 1)
            A(w2T[:, 0:D], ps[0:D, 0, 0:D], ACT.Copy).then_inc(w2_c, 1)
            act.wait_ge(wpi_p, 1)
            A(wpi[:, :, :], ps[0:D, 1, 0:2 * (D + 1)].rearrange("p (h n) -> p h n", h=2), ACT.Copy).then_inc(wpi_c, 1)
            act.wait_ge(wpi_c, 1)
            A(wpi[:, 1, D:D + 1], wpi[:, 1, D:D + 1], ACT.Identity, bias=pib1c[:, 0:1]).then_inc(wpi_c, 1)
            act.wait_ge(wpq_p, 1)
            A(wpq[:, :, :], ps[0:D + 1, 0, 0:2 * D].rearrange("p (h n) -> p h n", h=2), ACT.Copy).then_inc(wpq_c, 1)
            act.wait_ge(var_ready, 1)
            A(ln_s[:, 2, :], ln_s[:, 1, :], ACT.Sqrt).then_inc(std_ready, 1)

            def turn(j):
                act.wait_ge(n_tp, j + 1)
                A(tT1[0:D, :], ps[0:D, 1, :], ACT.Tanh, bias=b1c[:, 0:1]).then_inc(n_tT, 1)
            turns(act, SUPS, turn)

            def w_part(l, m):
                if m == 0:
                    act.wait_ge(Y[l]["w"], 96)
                else:
                    act.wait_ge(w_split[l], 2 * m)
                if m < 2:
                    A(w_parts[:, m, :], w_all, ACT.Copy).then_inc(w_split[l], 1)
                else:
                    A(w_parts[0:D, 2, :], w_all[0:D, :], ACT.Copy).then_inc(w_split[l], 1)
                    A(w_parts[D:P, 2, :], w_parts[D:P, 0, :], ACT.Copy).then_inc(w_split[l], 1)

            s = L[0]

            def step(i, u, t):
                if live(i, 3):
                    a = (u + 1) % 2
                    wait(act, s["v"], i - 4)
                    wait(act, s["uT"], i - 2)
                    A(uT[:, a, :], ps_u, ACT.Copy).then_inc(s["uTc"], 1)
                if live(i, 0):
                    wait(act, rec_slot[u], uses(0, t, u) * 16)
                    words = rec_u[:, u, :].rearrange("p (k w) -> p k w", w=W)
                    A(loc[:, bass.ds(i * K, K)], words[:, :, 2], ACT.Identity,
                      bias=base_neg[:, bass.ds(i, 1)]).then_inc(s["loc"], 1)
                    A(typ[:, bass.ds(i * K, K)], words[:, :, 3], ACT.Copy).then_inc(s["loc"], 1)
                if live(i, 1):
                    v = (u - 1) % U
                    wait(act, s["s"], i - U)
                    wait(act, s["oh"], i)
                    A(oh_b[:, v, :, :], oh[:, v, :, :], ACT.Copy).then_inc(s["ohb"], 1)
                if live(i, 4):
                    wait(act, s["z"], i - 4)
                    wait(act, s["zT"], i - 3)
                    A(zT[:, :], ps_zT, ACT.Identity, bias=iib1c[:, 0:1]).then_inc(s["zTc"], 1)
                if live(i, 1):
                    a = (u + 1) % 2
                    wait(act, s["q"], i - 2)
                    wait(act, s["ohT"], i)
                    A(ohT_b[:, a, :], ps_t, ACT.Copy).then_inc(s["ohTc"], 1)
                if live(i, 4):
                    wait(act, s["s"], i - 5)
                    wait(act, s["z"], i - 3)
                    A(tr[:, u % 2, :, :], ps_z.rearrange("p (k d) -> p k d", k=K),
                      ACT.Tanh).then_inc(s["t"], 1)
                if live(i, 1):
                    a = (u + 1) % 2
                    wait(act, s["bb"], i - 2)
                    A(bT[0:SPLIT, a, :], ps_b[0:SPLIT, :], ACT.Copy).then_inc(s["bTc"], 1)
            steps(act, 4, step, peel=2)
            for m in range(3):
                w_part(0, m)

            act.wait_ge(var_ready, 2)
            A(ln_s[:, 2, :], ln_s[:, 1, :], ACT.Sqrt).then_inc(std_ready, 1)
            for l in range(2):
                y = Y[l]

                def turn_y(a, q, ahead):
                    for c in (0, 2):
                        if ahead and c == 2:
                            act.wait_ge(y["tp"], a + 2)
                            A(hhT[:, 1 - q, :, :], ps_hT[1 - q], ACT.Copy).then_inc(y["hT"], 1)
                        act.wait_ge(y[f"mm{c}"], a + 1)
                        wait(act, y[f"o{c}"], 16 * a)
                        r = Y_REGION[q][c]
                        A(y_stage[:, c * YU:(c + 1) * YU], ps_flat[:, r * YU:(r + 1) * YU],
                          ACT.Copy).then_inc(y[f"ev{c}"], 1)
                act.wait_ge(y["tp"], 1)
                A(hhT[:, 0, :, :], ps_hT[0], ACT.Copy).then_inc(y["hT"], 1)

                def turn(pair):
                    turn_y(pair * 2, 0, True)
                    turn_y(pair * 2 + 1, 1, True)
                turns(act, BINS // 2, turn)
                turn_y(BINS - 1, 0, False)

                if l == 0:
                    s = L[1]

                    def step1(i, u, t):
                        if live(i, 0):
                            wait(act, s["wt"], i - 1)
                            wait(act, s["ohT"], i + 1)
                            A(ohT_f[:, u % 2, :], ps_t2[u % 2], ACT.Copy).then_inc(s["ohTc"], 1)
                    steps(act, 0, step1, between=lambda n: w_part(1, n - 1) if n > 0 else None)

        @block.vector
        def _(dve):
            n = [0]

            def link(ins):
                n[0] += 1
                ins.then_inc(dve_c, 1)
                dve.wait_ge(dve_c, n[0])

            lo = FULL // 32 * 32
            nc.vector.memset(basis_in[lo:P, REST:COLS, :], 0.0)
            nc.vector.memset(dst_in[lo:P, REST:COLS], PAD_DST)
            nc.vector.memset(src_in[lo:P, REST:COLS], 0)
            nc.vector.memset(typ_in[lo:P, REST:COLS], 0)
            nc.vector.memset(next_int[:, :], PAD_DST)
            link(nc.vector.memset(x_sb[:, :, :], 0.0))
            link(nc.vector.memset(pad_rec[:, :], 0.0))
            dve.sem_inc(const, 1)
            link(nc.vector.memset(pad_rec[:, :].rearrange("p (n w) -> p n w", w=W)[:, :, 2], float(PAD_DST)))
            nc.vector.memset(acc[:, :, :], 0.0)
            nc.vector.memset(zero_c[:, :], 0.0)
            nc.vector.memset(iib1c[D:P, :], 0.0)
            dve.wait_ge(pool_c, 7)
            for t in range(3):
                nc.vector.tensor_scalar(sel_t[:, t, :], sel_f[:, :], float(BASIS * t), None, ALU.is_equal
                                        ).then_inc(dve_c, 1)
                n[0] += 1
            nc.vector.tensor_copy(ident_b[:, :], ident[:, :]).then_inc(dve_c, 1)
            n[0] += 1
            dve.wait_ge(dve_c, n[0])
            link(TT(sel_t[:, 0, :], sel_t[:, 0, :], sel_t[:, 1, :], ALU.add))
            link(TT(ident2[:, :], ident[:, 0:D], ident[:, D:P], ALU.add))
            link(TT(sel[:, :, :].rearrange("k c m -> k (c m)"), sel_t[:, 0, :], sel_t[:, 2, :], ALU.add))

            dve.wait_ge(edges_in, 16 * 7)
            nc.vector.tensor_single_scalar(next_int[:, :], next_int[:, :], 7, ALU.arith_shift_right).then_inc(dve_c, 1)
            n[0] += 1
            link(nc.vector.tensor_single_scalar(bin_int[:, :], dst_in, 7, ALU.arith_shift_right))
            nc.vector.tensor_copy(next_bin[:, :], next_int[:, :]).then_inc(dve_c, 1)
            n[0] += 1
            link(nc.vector.tensor_copy(bin_of[:, :], bin_int[:, :]))
            halves = junk.bitcast(BF16)
            link(nc.vector.tensor_copy(halves[:, COLS:2 * COLS], bin_of))
            for a in range(BINS + 1):
                link(TS(halves[:, 0:COLS], halves[:, COLS:2 * COLS], float(a), 0.0, ALU.is_equal, ALU.add,
                        accum_out=count_pa[:, a:a + 1]))
            link(TT(junk[:, 0:COLS - 1], bin_of[:, 0:COLS - 1], bin_of[:, 1:COLS], ALU.is_gt))
            link(TT(junk[:, COLS - 1:COLS], bin_of[:, COLS - 1:COLS], next_bin[:, :], ALU.is_gt))
            link(nc.vector.tensor_reduce(small[:, 0:1], junk[:, :], AX.X, ALU.add))
            dve.sem_inc(counted, 1)
            dve.wait_ge(totals, 1)
            link(nc.vector.tensor_copy(small[:, 1:2], ps[:, 6, 0:1]))
            link(nc.vector.tensor_copy(small[0:BINS + 1, 2:3], ps[0:BINS + 1, 6, 1:2]))
            link(TS(small[0:BINS, 3:4], small[0:BINS, 2:3], float(GE - 1), None, ALU.add))
            link(nc.vector.tensor_copy(small_i[0:BINS, 0:1], small[0:BINS, 3:4]))
            link(nc.vector.tensor_single_scalar(small_i[0:BINS, 1:2], small_i[0:BINS, 0:1], GE.bit_length() - 1,
                                                ALU.arith_shift_right))
            nc.vector.tensor_copy(flag_i[:, :], small[:, 1:2]).then_inc(dve_c, 1)
            n[0] += 1
            link(nc.vector.tensor_copy(small[0:BINS, 4:5], small_i[0:BINS, 1:2]))
            dve.sem_inc(flag, 1)
            dve.sem_inc(in_groups, 1)
            link(STT(out=small[0:BINS, 5:6], in0=small[0:BINS, 4:5], scalar=-float(GE),
                     in1=small[0:BINS, 2:3], op0=ALU.mult, op1=ALU.add))
            link(nc.vector.tensor_copy(gap_b[:, :], small[0:BINS, 5:6].broadcast_to([BINS, P])))
            dve.wait_ge(cumulated, 1)
            link(nc.vector.tensor_copy(small[0:BINS, 6:7], ps[0:BINS, 6, 2:3]))
            link(TS(mask_ag[:, :], iota_g[0:BINS, :], small[0:BINS, 6:7], None, ALU.is_ge))
            dve.sem_inc(masks, 1)
            dve.wait_ge(spread, 1)
            link(nc.vector.tensor_copy(bin_g[:, :], ps[:, 4, 0:GROUPS]))
            link(STT(out=start_g[:, :], in0=iota_g[:, :], scalar=float(GE), in1=ps[:, 5, 0:GROUPS],
                     op0=ALU.mult, op1=ALU.add))
            link(TS(start_g[:, :], start_g[:, :], float(EDGES_ALL), None, ALU.min))
            link(nc.vector.tensor_copy(start_gi[:, :], start_g[:, :]))
            link(nc.vector.tensor_copy(bin_gi[:, :], bin_g[:, :]))
            link(TS(base_neg[:, :], bin_g[:, :], -float(P), None, ALU.mult))
            dve.sem_inc(tables, 1)

            link(nc.vector.tensor_copy(rec_a[:, :, 0].bitcast(I32), src_in))
            link(STT(out=rec_a[:, :, 1].bitcast(I32), in0=src_in, scalar=float(RELS), in1=typ_in,
                     op0=ALU.mult, op1=ALU.add))
            link(nc.vector.tensor_copy(rec_a[:, :, 2], dst_in))
            link(nc.vector.tensor_copy(rec_a[:, :, 3], typ_in))
            dve.wait_ge(basis_in_s, 32)
            part = [region_a[:, 0:COLS * W].bitcast(BF16).rearrange("p (n w) -> p n w", w=2 * W)
                    [:, :, 8 + BASIS * t:8 + BASIS * (t + 1)] for t in range(3)]
            link(nc.vector.tensor_copy(part[0], basis_in))
            link(TT(basis_in, basis_in, part[0], ALU.subtract))
            link(nc.vector.tensor_copy(part[1], basis_in))
            link(TT(part[2], basis_in, part[1], ALU.subtract))
            dve.sem_inc(rec_made, 1)

            out_of_order = dve.value_load(flag_i[0:1, 0:1], min_val=0, max_val=EDGES_ALL)
            with dve.If(out_of_order > 0):
                m = [0]

                def slow(ins):
                    m[0] += 1
                    ins.then_inc(placed_c, 1)
                    dve.wait_ge(placed_c, m[0])
                slow(nc.vector.tensor_copy(total_pa[:, :], ps[:, 6, 64:64 + BINS + 1]))
                slow(nc.vector.tensor_tensor_scan(offset_pa[:, :], total_pa[:, :], zero_c[:, 0:BINS + 1], 0.0, ALU.add, ALU.add))
                slow(TT(offset_pa[:, :], offset_pa[:, :], total_pa[:, :], ALU.subtract))
                slow(TT(offset_pa[:, :], offset_pa[:, :], ps[:, 6, 128:128 + BINS + 1], ALU.add))
                slow(nc.vector.memset(place[:, :], -1.0))
                same, ranks = basis_in.rearrange("p n b -> p (n b)")[:, 0:COLS], \
                    basis_in.rearrange("p n b -> p (n b)")[:, COLS:2 * COLS]
                slow(nc.vector.memset(junk[:, :], 0.0))
                for a in range(BINS + 1):
                    slow(TS(same, bin_of[:, :], float(a), None, ALU.is_equal))
                    slow(nc.vector.tensor_tensor_scan(ranks, same, junk[:, :], 0.0, ALU.add, ALU.add))
                    slow(STT(out=ranks, in0=ranks, scalar=offset_pa[:, a:a + 1], in1=same, op0=ALU.add, op1=ALU.mult))
                    slow(TT(place[:, :], place[:, :], ranks, ALU.add))
                slow(nc.vector.tensor_copy(place_i[:, :], place[:, :]))
                dve.sem_inc(placed, 1)
            dve.end_ifs()
            link(nc.vector.memset(bT[:, :, :], 0.0))

            def layernorm(tiles, k):
                xs, hs, qs = x_sb[:, 0:tiles, :], h_sb[:, 0:tiles, :], sq[:, 0:tiles, :]

                def bc(i):
                    return ln_s[:, i, 0:tiles].rearrange("p (t o) -> p t o", o=1).broadcast_to([P, tiles, D])
                link(nc.vector.tensor_reduce(ln_s[:, 0, 0:tiles], xs, AX.X, ALU.add))
                link(TS(ln_s[:, 0, 0:tiles], ln_s[:, 0, 0:tiles], 1.0 / D, None, ALU.mult))
                link(TT(hs, xs, bc(0), ALU.subtract))
                link(TT(qs, hs, hs, ALU.mult))
                link(nc.vector.tensor_reduce(ln_s[:, 1, 0:tiles], qs, AX.X, ALU.add))
                link(TS(ln_s[:, 1, 0:tiles], ln_s[:, 1, 0:tiles], 1.0 / D, 1e-5, ALU.mult, ALU.add))
                dve.sem_inc(var_ready, 1)
                dve.wait_ge(std_ready, k)
                link(nc.vector.reciprocal(ln_s[:, 0, 0:tiles], ln_s[:, 2, 0:tiles]))
                link(STT(out=hs, in0=hs, scalar=0.0, in1=bc(0), op0=ALU.max, op1=ALU.mult))

            dve.wait_ge(x_in, 32)
            layernorm(NT, 1)
            hf = h_sb[:, :, :].rearrange("p t d -> p (t d)")
            link(nc.vector.memset(tT1[D:D + 1, :], 1.0))

            def stage_h(j):
                nc.vector.tensor_copy(h_st[:, :], hf[:, bass.ds(j * (SUP * D), SUP * D)]).then_inc(n_hs, 1)

            def turn(j, last=False):
                dve.wait_ge(n_hp, j + 1)
                nc.vector.tensor_copy(hT[:, :], ps[0:D, 0, :]).then_inc(n_hT, 1)
                if not last:
                    stage_h(j + 1)
                dve.wait_ge(n_PQ, j + 1)
                wait(dve, n_Pout, 16 * j)
                pq = ps[:, 5, :].rearrange("p (t n) -> p t n", t=SUP)
                nc.vector.tensor_copy(p_st[:, :, :], pq[:, :, 0:D]).then_inc(n_Ps, 1)
                q0, q1 = q_st[:, 0, :, :], q_st[:, 1, :, :]
                qd = q_parts[:, :, :, :].rearrange("p t s d -> p t (s d)")
                qp = [qd[:, bass.ds(j * SUP, SUP), t * D:(t + 1) * D] for t in range(3)]
                TT(q0, pq[:, :, D:2 * D],
                   pib2r[:, :].rearrange("p (o d) -> p o d", o=1).broadcast_to([P, SUP, D]), ALU.add).then_inc(n_Q, 1)
                dve.wait_ge(n_Q, j * 5 + 1)
                nc.vector.tensor_copy(qp[0], q0).then_inc(n_Q, 1)
                dve.wait_ge(n_Q, j * 5 + 2)
                TT(q1, q0, qp[0], ALU.subtract).then_inc(n_Q, 1)
                dve.wait_ge(n_Q, j * 5 + 3)
                nc.vector.tensor_copy(qp[1], q1).then_inc(n_Q, 1)
                dve.wait_ge(n_Q, j * 5 + 4)
                TT(qp[2], q1, qp[1], ALU.subtract).then_inc(n_Q, 1)
            stage_h(0)
            turns(dve, SUPS - 1, turn)
            turn(SUPS - 1, last=True)
            iota3 = iota_p[:, :].rearrange("p (o m) -> p o m", o=1).broadcast_to([P, K, P])
            iota_r = iota_p[:, 0:RELS].rearrange("p (o m) -> p o m", o=1).broadcast_to([P, K, RELS])

            def rest_of_w(l, m):
                dve.wait_ge(w_split[l], 2 * m + 1)
                TT(w_all, w_all, w_parts[:, m, :], ALU.subtract).then_inc(w_split[l], 1)

            def per_edge(ap, j, width):
                return ap[:, bass.ds(j * K, K)].rearrange("p (k o) -> p k o", o=1).broadcast_to([P, K, width])

            def bin_sums(j, width):
                b = dve.value_load(bin_gi[0:1, bass.ds(j, 1)], min_val=0, max_val=BINS)
                return acc[:, :, :].rearrange("p a n -> p (a n)")[:, bass.ds(dve.snap(b * ND), width)]

            def add_to_bin(dst_acc, j, s, sums_ps):
                wait(dve, s["acc"], j)
                wait(dve, s["s"], j + 1)
                TT(dst_acc, dst_acc, sums_ps, ALU.add).then_inc(s["acc"], 1)

            s = L[0]

            def step(i, u, t):
                if live(i, 5):
                    dst_acc = bin_sums(i - 5, ND)
                if live(i, 3):
                    a = (u + 1) % 2
                    wait(dve, s["zT"], i - 4)
                    wait(dve, s["bb"], i - 2)
                    wait(dve, s["uTc"], i - 2)
                    TT(vT[:, a, :, :], bb[:, a, :, :],
                       uT[:, a, :].rearrange("p (o n) -> p o n", o=1).broadcast_to([P, 4, K * P]),
                       ALU.mult).then_inc(s["v"], 1)
                if live(i, 2):
                    a, v = u % 2, (u - 2) % U
                    wait(dve, gathered[v], uses(0, t, u, 2) * (16 * K))
                    wait(dve, s["uT"], i - 3)
                    wait(dve, s["q"], i - 1)
                    TT(u_sb[:, a, :, :, :],
                       gat[:, v, :, :].rearrange("p k (o d) -> p k o d", o=1).broadcast_to([P, K, 2, D]),
                       ps_q.rearrange("p (k o d) -> p k o d", k=K, o=1).broadcast_to([P, K, 2, D]),
                       ALU.add).then_inc(s["u"], 1)
                if live(i, 5):
                    add_to_bin(dst_acc, i - 5, s, ps_s)
                if live(i, 3):
                    a = (u + 1) % 2
                    wait(dve, s["s"], i - 4)
                    TT(rel_b[:, a, :, :], iota_r, per_edge(typ, i - 3, RELS), ALU.is_equal).then_inc(s["rel"], 1)
                if live(i, 0):
                    wait(dve, s["ohb"], i - U + 1)
                    wait(dve, s["s"], i - U + 1)
                    wait(dve, s["loc"], 2 * (i + 1))
                    TT(oh[:, u, :, :], iota3, per_edge(loc, i, P), ALU.is_equal).then_inc(s["oh"], 1)
            steps(dve, 5, step)


            sums, counts = acc[:, 0:BINS, 0:D], acc[:, 0:BINS, D:ND]
            dve.wait_ge(s["acc"], GROUPS)
            link(nc.vector.tensor_reduce(ln_s[:, 0, 0:BINS], counts, AX.X, ALU.add))
            for j in range(BINS // FIVE):
                five = slice(j * FIVE, (j + 1) * FIVE)
                wait(dve, nd["tp"], j)
                nc.vector.tensor_copy(s_st[:, :, 0:D], acc[:, five, 0:D]).then_inc(nd["st"], 1)
                nc.vector.tensor_copy(s_st[:, :, D:D + 1].rearrange("p t o -> p (t o)"),
                                      ln_s[:, 0, five]).then_inc(nd["st"], 1)
                link(TS(counts[:, five, :], counts[:, five, :], 1.0, None, ALU.max))
                link(nc.vector.reciprocal(counts[:, five, :], counts[:, five, :]))
                dve.wait_ge(nd["tp"], j + 1)
                nc.vector.tensor_copy(sT[:, :], ps_flat[0:D + 1, 0:FIVE * P]).then_inc(nd["tT"], 1)
                if j < 2:
                    rest_of_w(0, j)
                dve.wait_ge(nd["o"], j + 1)
                xj = x_sb[:, five, :]
                TT(xj, xj, ps[:, 2, 0:FIVE * D].rearrange("p (t d) -> p t d", t=FIVE), ALU.add).then_inc(nd["x"], 1)
            dve.wait_ge(nd["x"], BINS // FIVE)
            layernorm(BINS, 2)
            dve.sem_inc(h_ready, 1)

            for l in range(2):
                y = Y[l]

                hi, mid, lo = h_parts[:, :, D:2 * D], h_parts[:, :, 0:D], h_parts[:, :, 2 * D:3 * D]
                hs, rest = h_sb[:, 0:BINS, :], sq[:, 0:BINS, :]
                link(nc.vector.tensor_copy(hi, hs))
                link(TT(rest, hs, hi, ALU.subtract))
                link(nc.vector.tensor_copy(mid, rest))
                link(TT(lo, rest, mid, ALU.subtract))

                def stage(a, q):
                    nc.vector.tensor_copy(hh_st[:, q, :],
                                          h_parts[:, :, :].rearrange("p a n -> p (a n)")[:, bass.ds(a * (3 * D), 3 * D)]
                                          ).then_inc(y["st"], 1)

                def turn_y(a, q, ahead):
                    if ahead:
                        wait(dve, y["tp"], a)
                        stage(a + 1, 1 - q)
                    for c in (1, 3):
                        dve.wait_ge(y[f"mm{c}"], a + 1)
                        wait(dve, y[f"o{c}"], 16 * a)
                        r = Y_REGION[q][c]
                        nc.vector.tensor_copy(y_stage[:, c * YU:(c + 1) * YU],
                                              ps_flat[:, r * YU:(r + 1) * YU]).then_inc(y[f"ev{c}"], 1)
                        if l == 0 and c == 1:
                            flat = acc[:, :, :].rearrange("p a n -> p (a n)")
                            nc.vector.tensor_copy(flat[:, bass.ds(a * ND, D)], zero_c[:, 0:D]).then_inc(cleared, 1)
                    dve.wait_ge(y["mm4"], a + 1)
                    nc.vector.tensor_copy(y_stage[:, NYU * YU:NYU * YU + D], ps[:, 6, 0:D]).then_inc(y["ev4"], 1)
                    TT(rr[:, :, :].rearrange("p a n -> p (a n)")[:, bass.ds(a * (2 * D), 2 * D)],
                       ps[:, 6, D:3 * D], brr[:, l, :], ALU.add).then_inc(y["h"], 1)
                stage(0, 0)

                def turn(pair):
                    turn_y(pair * 2, 0, True)
                    turn_y(pair * 2 + 1, 1, True)
                turns(dve, BINS // 2, turn)
                turn_y(BINS - 1, 0, False)

                s = L[l + 1]
                if l == 0:
                    dve.wait_ge(cleared, BINS)

                    def step1(i, u, t):
                        if live(i, 5):
                            dst_acc = bin_sums(i - 5, D)
                        if live(i, 0):
                            wait(dve, s["s"], i - U + 1)
                            TT(oh[:, u, :, :], iota3, per_edge(loc, i, P), ALU.is_equal).then_inc(s["oh"], 1)
                        if live(i, 3):
                            a, v = (u + 1) % 2, (u - 3) % U
                            wait(dve, s["wt"], i - 2)
                            for k in range(K):
                                e = (i - 3) * K + k
                                STT(out=pick[:, k, :], in0=iota_p[:, 0:RELS], scalar=typ[:, bass.ds(e, 1)],
                                    in1=ps_w[a][:, k, :], op0=ALU.is_equal, op1=ALU.mult,
                                    accum_out=w_edge[:, bass.ds(e, 1)]).then_inc(s["w"], 1)
                            wait(dve, s["w"], K * (i - 2))
                            wait(dve, gathered[v], uses(1, t, u, 3) * (16 * K))
                            wait(dve, s["s"], i - 4)
                            TT(tr[:, a, :, :], gat[:, v, :, :], per_edge(w_edge, i - 3, D), ALU.mult
                               ).then_inc(s["scaled"], 1)
                        if live(i, 5):
                            add_to_bin(dst_acc, i - 5, s, ps_s2[(u + 1) % 2])
                    steps(dve, 5, step1, between=lambda n: rest_of_w(1, n - 1) if n in (1, 2) else None)
                else:
                    def step2(i, u, t):
                        if live(i, 3):
                            dst_acc = bin_sums(i - 3, D)
                        if live(i, 0):
                            wait(dve, s["s"], i - U + 1)
                            for k in range(K):
                                e = i * K + k
                                TS(oh[:, u, k, :], iota_p[:, :], loc[:, bass.ds(e, 1)], w_edge[:, bass.ds(e, 1)],
                                   ALU.is_equal, ALU.mult).then_inc(s["oh"], 1)
                        if live(i, 3):
                            add_to_bin(dst_acc, i - 3, s, ps_s2[(u + 1) % 2])
                    steps(dve, 3, step2)
                dve.wait_ge(s["acc"], GROUPS)
                link(TT(sq[:, 0:BINS, :], sums, rr[:, :, 0:D], ALU.add))
                link(TS(rr[:, :, D:2 * D], rr[:, :, D:2 * D], 0.0, None, ALU.max))
                link(STT(out=h_sb[:, 0:BINS, :], in0=sq[:, 0:BINS, :], scalar=0.0, in1=rr[:, :, D:2 * D],
                         op0=ALU.max, op1=ALU.add))
                if l == 0:
                    link(nc.vector.memset(sums, 0.0))
            TT(h_sb[:, 0:BINS, :], h_sb[:, 0:BINS, :], x_sb[:, 0:BINS, :], ALU.add).then_inc(final, 1)

        @block.tensor
        def _(pe):
            MM = nc.tensor.matmul
            pe.wait_ge(w_in, 16 * SMALL_LOADS)
            pe.wait_ge(pool_c, 7)
            for b in range(BASIS):
                mm = MM(ps[0:D, 3, b * D:(b + 1) * D], w3[:, :, b], ident[0:D, 0:D], start=True, stop=True)
            mm.then_inc(w3_t, 1)
            pe.wait_ge(w3_c, 1)
            for c in range(4):
                mm = MM(ps[:, 2, c * D:(c + 1) * D], w3t[:, c * P:(c + 1) * P], wii1[:, :], start=True, stop=True)
            mm.then_inc(wz_p, 1)
            MM(ps[0:D, 0, 0:D], w2[:, :], ident[0:D, 0:D], start=True, stop=True).then_inc(w2_t, 1)
            pe.wait_ge(w2_c, 1)
            for h in range(2):
                mm = MM(ps[0:D, 1, h * (D + 1):(h + 1) * (D + 1)], wa[:, h, :], w2T[:, :], start=True, stop=True)
            mm.then_inc(wpi_p, 1)
            pe.wait_ge(wpi_c, 2)
            for h in range(2):
                mm = MM(ps[0:D + 1, 0, h * D:(h + 1) * D], wpi[:, h, :], wi2[:, :], start=True, stop=True)
            mm.then_inc(wpq_p, 1)
            pe.wait_ge(counted, 1)
            MM(ps[:, 6, 0:1], ones[:, :], small[:, 0:1], start=True, stop=True)
            MM(ps[0:BINS + 1, 6, 1:2], count_pa[:, :], ones[:, 0:1], start=True, stop=True)
            MM(ps[:, 6, 64:64 + BINS + 1], ones[:, :], count_pa[:, :], start=True, stop=True)
            MM(ps[:, 6, 128:128 + BINS + 1], before[:, :], count_pa[:, :], start=True, stop=True).then_inc(totals, 1)
            pe.wait_ge(in_groups, 1)
            MM(ps[0:BINS, 6, 2:3], upto[0:BINS, 0:BINS], small[0:BINS, 4:5], start=True, stop=True
               ).then_inc(cumulated, 1)
            pe.wait_ge(masks, 1)
            MM(ps[:, 4, 0:GROUPS], ones[0:BINS, :], mask_ag[:, :], start=True, stop=True)
            MM(ps[:, 5, 0:GROUPS], gap_b[:, :], mask_ag[:, :], start=True, stop=True).then_inc(spread, 1)

            pe.wait_ge(wz_c, 1)
            pe.wait_ge(wpq_c, 1)

            def transpose_nodes(j):
                held_wait(pe, n_hs, j + 1, tick)
                for t in range(SUP):
                    mm = MM(ps[0:D, 0, t * P:(t + 1) * P], h_st[:, t * D:(t + 1) * D], ident[:, :],
                            start=True, stop=True)
                mm.then_inc(n_hp, 1)

            def turn(j, last=False):
                held_wait(pe, n_hT, j + 1, tick)
                MM(ps[0:D, 1, :], w1[:, :], hT[:, :], start=True, stop=True).then_inc(n_tp, 1)
                if not last:
                    transpose_nodes(j + 1)
                held_wait(pe, n_tT, j + 1, tick)
                wait(pe, n_Q, j * 5)
                for t in range(SUP):
                    mm = MM(ps[:, 5, t * 2 * D:(t + 1) * 2 * D], tT1[:, t * P:(t + 1) * P],
                            wpq[:, :, :].rearrange("p h n -> p (h n)"), start=True, stop=True)
                mm.then_inc(n_PQ, 1)
            transpose_nodes(0)
            turns(pe, SUPS - 1, turn)
            turn(SUPS - 1, last=True)

            pe.wait_ge(n_Q, SUPS * 5)
            pe.wait_ge(n_Ps, SUPS)
            s = L[0]
            qf = q_parts[:, :, :, :].rearrange("p t s d -> p (t s d)")
            Z3 = (3 * D)

            def step(i, u, t):
                if live(i, 2):
                    b = pe.value_load(bin_gi[0:1, bass.ds(i - 2, 1)], min_val=0, max_val=BINS)
                    q_at = [pe.snap(b * Z3 + part * D) for part in range(3)]
                if live(i, 3):
                    a = (u + 1) % 2
                    wait(pe, s["u"], i - 2)
                    wait(pe, s["uTc"], i - 3)
                    for k in range(K):
                        mm = pe.transpose(ps_u[:, k * P:(k + 1) * P],
                                          u_sb[:, a, k, :, :].rearrange("p o d -> p (o d)"), ident[:, :])
                    mm.then_inc(s["uT"], 1)
                if live(i, 4):
                    a = u % 2
                    wait(pe, s["v"], i - 3)
                    wait(pe, s["t"], i - 4)
                    for c in range(2):
                        for q in range(2):
                            mm = MM(ps_zT[q * D:(q + 1) * D, :], wz[:, 2 * q + c, :], vT[:, a, 2 * q + c, :],
                                    start=(c == 0), stop=(c == 1))
                    mm.then_inc(s["zT"], 1)
                if live(i, 5):
                    a, v = (u + 1) % 2, (u - 5) % U
                    wait(pe, s["acc"], i - 5)
                    wait(pe, s["t"], i - 4)
                    if live(i, 3):
                        wait(pe, s["u"], i - 2)
                    for k in range(K):
                        MM(ps_s[:, 0:D], oh[:, v, k, :], tr[:, a, k, :], start=(k == 0), stop=(k == K - 1))
                    wait(pe, s["rel"], i - 4)
                    for k in range(K):
                        mm = MM(ps_s[:, D:ND], oh_b[:, v, k, :], rel_b[:, a, k, :],
                                start=(k == 0), stop=(k == K - 1))
                    mm.then_inc(s["s"], 1)
                if live(i, 2):
                    a = u % 2
                    wait(pe, s["ohTc"], i - 1)
                    wait(pe, s["u"], i - 2)
                    for k in range(K):
                        for part in range(3):
                            mm = MM(ps_q[:, k * D:(k + 1) * D], ohT_b[:, a, k * P:(k + 1) * P],
                                    qf[:, bass.ds(q_at[part], D)], start=(part == 0), stop=(part == 2))
                    mm.then_inc(s["q"], 1)
                if live(i, 1):
                    v = (u - 1) % U
                    wait(pe, s["ohb"], i)
                    wait(pe, s["bTc"], i - 1)
                    for k in range(K):
                        pe.transpose(ps_t[:, k * P:(k + 1) * P], oh_b[:, v, k, :], ident_b[:, :])
                    wait(pe, rec_slot[v], uses(0, t, u, 1) * 16)
                    for k in range(K):
                        mm = pe.transpose(ps_b[0:SPLIT, k * P:(k + 1) * P],
                                          rec_u[:, v, k * W + 4:(k + 1) * W].bitcast(BF16), ident_b[:, :])
                    mm.then_inc(s["ohT"], 1)
                if live(i, 4):
                    wait(pe, s["zTc"], i - 3)
                    for k in range(K):
                        mm = MM(ps_z[:, k * D:(k + 1) * D], zT[:, k * P:(k + 1) * P], ident2[:, :],
                                start=True, stop=True)
                    mm.then_inc(s["z"], 1)
                if live(i, 2):
                    a = u % 2
                    wait(pe, s["bTc"], i - 1)
                    for c in range(4):
                        mm = MM(bb[:, a, c, :], sel[:, c, :], bT[:, a, :], start=True, stop=True)
                    mm.then_inc(s["bb"], 1)
            steps(pe, 5, step)

            pe.wait_ge(s["acc"], GROUPS)

            def turn(j):
                pe.wait_ge(nd["st"], 2 * (j + 1))
                for t in range(FIVE):
                    mm = MM(ps_flat[0:D + 1, t * P:(t + 1) * P], s_st[:, t, :], ident[:, :], start=True, stop=True)
                mm.then_inc(nd["tp"], 1)
                pe.wait_ge(nd["tT"], j + 1)
                wait(pe, nd["x"], j)
                for t in range(FIVE):
                    mm = MM(ps[:, 2, t * D:(t + 1) * D], sT[:, t * P:(t + 1) * P], wii2[:, :], start=True, stop=True)
                mm.then_inc(nd["o"], 1)
            turns(pe, BINS // FIVE, turn)

            for l in range(2):
                y = Y[l]

                def transpose_h(a, q):
                    pe.wait_ge(y["st"], a + 1)
                    for m in range(2):
                        mm = pe.transpose(ps_hT[q][:, m, :], hh_st[:, q, m * D:m * D + P], ident_b[:, :])
                    mm.then_inc(y["tp"], 1)

                def product(o, q, first, n):
                    for m, (half, part) in enumerate(((0, 0), (0, 1), (1, 2))):
                        mm = MM(o, hhT[:, q, half, :], w_parts[:, part, first:first + n], start=(m == 0), stop=(m == 2))
                    return mm

                def turn_y(a, q, ahead):
                    pe.wait_ge(y["hT"], a + 1)
                    for c in range(NYU):
                        if ahead and c == 2:
                            transpose_h(a + 1, 1 - q)
                        r = Y_REGION[q][c]
                        if c == 3:
                            pe.wait_ge(y["ev0"], a + 1)
                        else:
                            wait(pe, y[f"ev{Y_BEFORE[q][c]}"], a)
                        for half in range(2):
                            o = c * YU + half * 512
                            mm = product(ps_flat[:, r * YU + half * 512:r * YU + (half + 1) * 512], q, o, 512)
                        mm.then_inc(y[f"mm{c}"], 1)
                    wait(pe, y["ev4"], a)
                    wait(pe, y["h"], a)
                    product(ps[:, 6, 0:3 * D], q, NYU * YU, 3 * D).then_inc(y["mm4"], 1)
                pe.wait_ge(w_split[l], 6)
                transpose_h(0, 0)

                def turn(pair):
                    turn_y(pair * 2, 0, True)
                    turn_y(pair * 2 + 1, 1, True)
                turns(pe, BINS // 2, turn)
                turn_y(BINS - 1, 0, False)
                for c in range(4):
                    pe.wait_ge(y[f"ev{c}"], BINS)
                pe.wait_ge(y["h"], BINS)
                pe.wait_ge(y["ev4"], BINS)

                s = L[l + 1]
                af = acc[:, :, :].rearrange("p a n -> p (a n)")
                if l == 0:
                    def step1(i, u, t):
                        if live(i, 0):
                            a = u % 2
                            wait(pe, s["oh"], i + 1)
                            wait(pe, s["ohTc"], i - 1)
                            for k in range(K):
                                mm = pe.transpose(ps_t2[a][:, k * P:(k + 1) * P], oh[:, u, k, :], ident[:, :])
                            mm.then_inc(s["ohT"], 1)
                        if live(i, 4):
                            a, v = u % 2, (u - 4) % U
                            wait(pe, s["acc"], i - 5)
                            wait(pe, s["scaled"], i - 3)
                            for k in range(K):
                                mm = MM(ps_s2[a], oh[:, v, k, :], tr[:, a, k, :],
                                        start=(k == 0), stop=(k == K - 1))
                            mm.then_inc(s["s"], 1)
                        if live(i, 1):
                            a = (u + 1) % 2
                            b = pe.value_load(bin_gi[0:1, bass.ds(i - 1, 1)], min_val=0, max_val=BINS)
                            wait(pe, s["ohTc"], i)
                            wait(pe, s["w"], K * (i - 2))
                            for k in range(K):
                                mm = MM(ps_w[a][:, k, :], ohT_f[:, a, k * P:(k + 1) * P],
                                        af[:, bass.ds(b * ND + D, RELS)], start=True, stop=True)
                            mm.then_inc(s["wt"], 1)
                    steps(pe, 4, step1)
                else:
                    def step2(i, u, t):
                        if live(i, 2):
                            a, v = u % 2, (u - 2) % U
                            wait(pe, s["oh"], K * (i - 1))
                            wait(pe, gathered[v], uses(2, t, u, 2) * (16 * K))
                            wait(pe, s["acc"], i - 3)
                            for k in range(K):
                                mm = MM(ps_s2[a], oh[:, v, k, :], gat[:, v, k, :],
                                        start=(k == 0), stop=(k == K - 1))
                            mm.then_inc(s["s"], 1)
                    steps(pe, 2, step2)


_INS = ["x", "src", "dst", "edge_attr_8", "edge_type_65",
        "L0_gnn_pp_W1", "L0_gnn_pp_b1", "L0_gnn_pp_W2", "L0_gnn_pp_b2", "L0_gnn_pi_W1", "L0_gnn_pi_b1",
        "L0_gnn_pi_W2", "L0_gnn_pi_b2", "L0_gnn_pi_W3", "L0_gnn_ii_W1", "L0_gnn_ii_b1", "L0_gnn_ii_W2",
        "L0_gnn_ii_b2", "L1_gnn_W", "L1_gnn_root", "L1_gnn_bias", "L1_gnn_res_W", "L1_gnn_res_b"]


def kernel(**inputs):
    import numpy as np
    import concourse.bacc as bacc
    from concourse.bass_utils import run_bass_kernel_spmd

    nc = bacc.Bacc("TRN2", target_bir_lowering=False, num_devices=1)
    arrays, args = {}, []
    for name in _INS:
        a = np.ascontiguousarray(inputs[name])
        arrays[f"in_{name}"] = a
        args.append(nc.dram_tensor(f"in_{name}", a.shape, mybir.dt.from_np(a.dtype), kind="ExternalInput").ap())
    args.append(nc.dram_tensor("out_0", (NODES, D), F32, kind="ExternalOutput").ap())
    build(nc, *args)
    r = run_bass_kernel_spmd(nc, [arrays], core_ids=[0])
    return r.results[0]["out_0"]
```
